# Optimizing a Trainium2 kernel written in Bass

```python
import numpy as np
import jax
import jax.numpy as jnp

def _softmax(x, axis=-1):
    return jax.nn.softmax(x, axis=axis)

def _gelu(x):
    return jax.nn.gelu(x, approximate=True)

def _silu(x):
    return jax.nn.silu(x)

def _sigmoid(x):
    return jax.nn.sigmoid(x)

def _layernorm(x, axis=-1, eps=1e-05):
    m = jnp.mean(x, axis=axis, keepdims=True)
    v = jnp.var(x, axis=axis, keepdims=True)
    return (x - m) / jnp.sqrt(v + eps)

def _scatter_add(tgt, idx, src, axis=0):
    return tgt.at[idx].add(src)

def _segment_sum(src, seg, n):
    return jax.ops.segment_sum(src, seg, n)
kernel_name = 'mk_adaln_attn_ffn_d1_seqx_r8_8cbaf1'

def setup_inputs(seed: int=0):
    np.random.seed(seed)
    _w = jnp.asarray

    def _rec_inputs():
        import jax
        import jax.numpy as jnp
        _rk = jax.random.key(seed)
        x = -7.109e-05 + 0.9999 * jax.random.normal(jax.random.fold_in(_rk, 1), (128, 32, 256), jnp.float32)
        _lenS = 32 - jax.random.randint(jax.random.fold_in(_rk, 7), (128,), 0, max(1, 32 // 4) + 1, jnp.int32)
        _lenS2 = 32 - jax.random.randint(jax.random.fold_in(_rk, 8), (128,), 0, max(1, 32 // 4) + 1, jnp.int32)
        itok_B_0_7 = jax.random.randint(jax.random.fold_in(_rk, 11), (128,), 0, 8, jnp.int32)
        itok_B_1_198 = jax.random.randint(jax.random.fold_in(_rk, 12), (128,), 1, 199, jnp.int32)
        return (x, itok_B_0_7, itok_B_1_198)
    x, itok_B_0_7, itok_B_1_198 = _rec_inputs()

    def _L0_cond_setup():
        import jax, jax.numpy as jnp
        import numpy as np
        B, C, D, T, N_SUBJECTS = (128, 32, 32, 256, 8)
        key = jax.random.key(seed)
        kx, ks, kw = jax.random.split(key, 3)
        x = jax.random.normal(kx, (B, C, T), dtype=jnp.float32)
        subjects = jax.random.randint(ks, (B,), 0, N_SUBJECTS, dtype=jnp.int64)
        weights = jax.random.normal(kw, (N_SUBJECTS, C, D), dtype=jnp.float32) * (1.0 / C ** 0.5)
        return {'x': x, 'subjects': subjects, 'weights': weights}
    _L0_cond_all = _L0_cond_setup()
    _L0_cond_in = {k: v for k, v in _L0_cond_all.items() if k in ('weights',)}
    del _L0_cond_all

    def _L0_attn_setup():
        import jax, jax.numpy as jnp
        import numpy as np
        EPS = 1e-05

        def _subln(x):
            mean = jnp.mean(x, axis=-1, keepdims=True)
            var = jnp.var(x, axis=-1, keepdims=True)
            return (x - mean) / jnp.sqrt(var + EPS)

        def _activation_quant(x):
            scale = 127.0 / jnp.clip(jnp.max(jnp.abs(x), axis=-1, keepdims=True), 1e-05, None)
            return jnp.clip(jnp.round(x * scale), -128.0, 127.0) / scale

        def _weight_quant(w):
            am = jnp.mean(jnp.abs(w))
            return jnp.clip(jnp.round(w / (am + EPS)), -1.0, 1.0) * am

        def _bitlinear(x, w):
            x_norm = _subln(x)
            x_q = x_norm + jax.lax.stop_gradient(_activation_quant(x_norm) - x_norm)
            w_q = w + jax.lax.stop_gradient(_weight_quant(w) - w)
            return jnp.einsum('bsd,od->bso', x_q, w_q)
        key = jax.random.key(seed)
        ks = jax.random.split(key, 5)
        B, S, D = (2, 256, 256)
        return {'x': jax.random.normal(ks[0], (B, S, D), dtype=jnp.float32), 'wq': jax.random.normal(ks[1], (D, D), dtype=jnp.float32) * 0.02, 'wk': jax.random.normal(ks[2], (D, D), dtype=jnp.float32) * 0.02, 'wv': jax.random.normal(ks[3], (D, D), dtype=jnp.float32) * 0.02, 'wp': jax.random.normal(ks[4], (D, D), dtype=jnp.float32) * 0.02}
    _L0_attn_all = _L0_attn_setup()
    _L0_attn_in = {k: v for k, v in _L0_attn_all.items() if k in ('wq', 'wk', 'wv', 'wp')}
    del _L0_attn_all

    def _L0_cond2_setup():
        import jax, jax.numpy as jnp
        import numpy as np
        B, C, T = (128, 32, 256)
        S, D = (200, 32)
        key = jax.random.key(seed)
        k1, k2, k3 = jax.random.split(key, 3)
        x = jax.random.normal(k1, (B, C, T), dtype=jnp.float32)
        conditions = jax.random.randint(k2, (B,), 0, S, dtype=jnp.int64)
        weights = jax.random.normal(k3, (S, C, D), dtype=jnp.float32) / jnp.sqrt(jnp.float32(C))
        return {'x': x, 'conditions': conditions, 'weights': weights}
    _L0_cond2_all = _L0_cond2_setup()
    _L0_cond2_in = {k: v for k, v in _L0_cond2_all.items() if k in ('weights',)}
    del _L0_cond2_all

    def _L0_ffn_setup():
        import jax, jax.numpy as jnp
        import numpy as np
        B, T, D, F, E, K = (2, 128, 256, 96, 16, 2)
        key = jax.random.key(seed)
        k0, k1, k2, k3, k4 = jax.random.split(key, 5)
        scale = 0.02
        return {'x': jax.random.normal(k0, (B, T, D), dtype=jnp.float32), 'router_w': jax.random.normal(k1, (D, E), dtype=jnp.float32) * scale, 'gate_w': jax.random.normal(k2, (E, D, F), dtype=jnp.float32) * scale, 'up_w': jax.random.normal(k3, (E, D, F), dtype=jnp.float32) * scale, 'down_w': jax.random.normal(k4, (E, F, D), dtype=jnp.float32) * scale}
    _L0_ffn_all = _L0_ffn_setup()
    _L0_ffn_in = {k: v for k, v in _L0_ffn_all.items() if k in ('router_w', 'gate_w', 'up_w', 'down_w')}
    del _L0_ffn_all
    return {'x': x, 'itok_B_0_7': itok_B_0_7, 'itok_B_1_198': itok_B_1_198, 'L0_cond_weights': _L0_cond_in['weights'], 'L0_attn_wq': _L0_attn_in['wq'], 'L0_attn_wk': _L0_attn_in['wk'], 'L0_attn_wv': _L0_attn_in['wv'], 'L0_attn_wp': _L0_attn_in['wp'], 'L0_cond2_weights': _L0_cond2_in['weights'], 'L0_ffn_router_w': _L0_ffn_in['router_w'], 'L0_ffn_gate_w': _L0_ffn_in['gate_w'], 'L0_ffn_up_w': _L0_ffn_in['up_w'], 'L0_ffn_down_w': _L0_ffn_in['down_w']}

def reference(x, itok_B_0_7, itok_B_1_198, L0_cond_weights, L0_attn_wq, L0_attn_wk, L0_attn_wv, L0_attn_wp, L0_cond2_weights, L0_ffn_router_w, L0_ffn_gate_w, L0_ffn_up_w, L0_ffn_down_w):
    import jax
    import jax.numpy as jnp

    def _L0_cond_ref(x, subjects, weights):
        import jax, jax.numpy as jnp
        import numpy as np
        B, C, D, T, N_SUBJECTS = (128, 32, 32, 256, 8)
        w = weights[subjects]
        out = jnp.einsum('bct,bcd->bdt', x, w)
        return out

    def _L0_attn_ref(x, wq, wk, wv, wp):
        import jax, jax.numpy as jnp
        import numpy as np
        EPS = 1e-05

        def _subln(x):
            mean = jnp.mean(x, axis=-1, keepdims=True)
            var = jnp.var(x, axis=-1, keepdims=True)
            return (x - mean) / jnp.sqrt(var + EPS)

        def _activation_quant(x):
            scale = 127.0 / jnp.clip(jnp.max(jnp.abs(x), axis=-1, keepdims=True), 1e-05, None)
            return jnp.clip(jnp.round(x * scale), -128.0, 127.0) / scale

        def _weight_quant(w):
            am = jnp.mean(jnp.abs(w))
            return jnp.clip(jnp.round(w / (am + EPS)), -1.0, 1.0) * am

        def _bitlinear(x, w):
            x_norm = _subln(x)
            x_q = x_norm + jax.lax.stop_gradient(_activation_quant(x_norm) - x_norm)
            w_q = w + jax.lax.stop_gradient(_weight_quant(w) - w)
            return jnp.einsum('bsd,od->bso', x_q, w_q)
        B, S, D = x.shape
        H = 16
        hd = D // H
        q = _bitlinear(x, wq).reshape(B, S, H, hd).transpose(0, 2, 1, 3)
        k = _bitlinear(x, wk).reshape(B, S, H, hd).transpose(0, 2, 1, 3)
        v = _bitlinear(x, wv).reshape(B, S, H, hd).transpose(0, 2, 1, 3)
        attn = jnp.einsum('bhqd,bhkd->bhqk', q, k) / np.sqrt(hd).astype(np.float32)
        causal = jnp.tril(jnp.ones((S, S), dtype=bool))
        attn = jnp.where(causal, attn, -jnp.inf)
        attn = jax.nn.softmax(attn, axis=-1)
        out = jnp.einsum('bhqk,bhkd->bhqd', attn, v)
        out = out.transpose(0, 2, 1, 3).reshape(B, S, D)
        return _bitlinear(out, wp)

    def _L0_cond2_ref(x, conditions, weights):
        import jax, jax.numpy as jnp
        import numpy as np
        B, C, T = (128, 32, 256)
        S, D = (200, 32)
        w = weights[conditions]
        return jnp.einsum('bct,bcd->bdt', x, w)

    def _L0_ffn_ref(x, router_w, gate_w, up_w, down_w):
        import jax, jax.numpy as jnp
        import numpy as np
        B, T, D, F, E, K = (2, 128, 256, 96, 16, 2)
        scores = jnp.einsum('btd,de->bte', x, router_w).astype(jnp.float32)
        probs = jax.nn.softmax(scores, axis=-1)
        routing_weights, routing_idx = jax.lax.top_k(probs, K)
        routing_weights = routing_weights / jnp.sum(routing_weights, axis=-1, keepdims=True)
        routing_weights = routing_weights.astype(x.dtype)
        one_hot = jax.nn.one_hot(routing_idx, E, dtype=x.dtype)
        combine = jnp.einsum('btk,btke->bte', routing_weights, one_hot)
        g = jnp.einsum('btd,edf->ebtf', x, gate_w)
        u = jnp.einsum('btd,edf->ebtf', x, up_w)
        h = jax.nn.silu(g) * u
        expert_out = jnp.einsum('ebtf,efd->ebtd', h, down_w)
        out = jnp.einsum('ebtd,bte->btd', expert_out, combine)
        return out
    x = x + _L0_attn_ref(_L0_cond_ref(x, itok_B_0_7, L0_cond_weights), L0_attn_wq, L0_attn_wk, L0_attn_wv, L0_attn_wp)
    x = x + _L0_ffn_ref(_L0_cond2_ref(x, itok_B_1_198, L0_cond2_weights), L0_ffn_router_w, L0_ffn_gate_w, L0_ffn_up_w, L0_ffn_down_w)
    return x

_drawn_inputs = setup_inputs


def setup_inputs(seed=0):
    import zlib

    import numpy as np

    out = dict(_drawn_inputs(seed))
    spreads = {}
    factors = {'L0_attn_wq': 4.668,
     'L0_attn_wk': 4.611,
     'L0_cond2_weights': 7.219,
     'L0_ffn_router_w': 7.74,
     'L0_ffn_gate_w': 7.301,
     'L0_ffn_up_w': 7.202,
     'L0_ffn_down_w': 7.186}
    for name, (base, spread) in spreads.items():
        noise = np.random.default_rng([zlib.crc32(name.encode()), seed]).standard_normal(out[name].shape)
        drawn = base * np.exp(spread * noise) if base else spread * noise
        out[name] = jnp.asarray(drawn.astype(out[name].dtype))
    for name, factor in factors.items():
        out[name] = (out[name] * factor).astype(out[name].dtype)
    return out
```

```python
import concourse.bass as bass
from concourse import mybir
from contextlib import ExitStack

P = 128
BATCH, SEQ, D = 128, 32, 256
TOKENS = BATCH * SEQ
TILES = TOKENS // P
TG = 4
GROUPS = TILES // TG
GT = TG * P
BT = P // SEQ
KC = D // P
H, HD = 16, 16
HC = P // HD
VW = HD + 1
SLOTS = 4
E, F, TOPK = 16, 96, 2
ROW = D + 2
PITCH = TOKENS + P
EXPERT_TILES = (TOKENS * TOPK + E * (P - 1)) // P + 1
PADS = 16
EPS = 1e-5
MAGIC = 1.5 * 2.0 ** 23
QMAX = 127.0
NEG = -1e30
Y_ROWS = TOKENS * TOPK

fp32 = mybir.dt.float32
bf16 = mybir.dt.bfloat16
i32 = mybir.dt.int32
u32 = mybir.dt.uint32
ALU = mybir.AluOpType
ACT = mybir.ActivationFunctionType
AX = mybir.AxisListType


def build(nc, x, sub, cond, w_mix1, wq, wk, wv, wp, w_mix2, w_router, w_gate, w_up, w_down, out):
    with ExitStack() as ctx:
        build_in(ctx, nc, x, sub, cond, w_mix1, wq, wk, wv, wp, w_mix2, w_router, w_gate, w_up, w_down, out)


def build_in(ctx, nc, x, sub, cond, w_mix1, wq, wk, wv, wp, w_mix2, w_router, w_gate, w_up, w_down, out):
    def sb(name, shape, dt=fp32):
        return ctx.enter_context(nc.sbuf_tensor(name, shape, dt))

    def sem(name):
        return ctx.enter_context(nc.semaphore(name))

    mix_d = [nc.dram_tensor(f"mix{i}_d", [BATCH, SEQ * SEQ], fp32, kind="Internal").ap() for i in range(2)]
    v_d = nc.dram_tensor("v_d", [GT, H * VW], fp32, kind="Internal").ap()
    routed = nc.dram_tensor("routed", [E * PITCH, ROW], fp32, kind="Internal").ap()
    y_d = nc.dram_tensor("y_d", [Y_ROWS, D], fp32, kind="Internal").ap()

    X = sb("X", [P, TILES, D])
    arena = sb("arena", [P, 2 * KC * HC * GT])
    KX_WORDS = KC * HC * GT
    kx = [arena[:, i * KX_WORDS:(i + 1) * KX_WORDS].rearrange("p (c h t) -> p c h t", c=KC, h=HC) for i in range(2)]
    vx = sb("vx", [P, TG * BT, SLOTS, SLOTS * VW])
    ids = sb("ids", [P, 2], i32)
    mix_rows = [arena[:, 0:1024], arena[:, 1024:2048]]
    mix = [sb(f"mix{i}", [P, TILES + TG, SEQ]) for i in range(2)]
    bd1 = [sb(f"bd1_{i}", [P, TG, BT, SEQ]) for i in range(2)]
    bd2 = [sb(f"bd2_{i}", [P, TG, BT, SEQ]) for i in range(2)]
    w_nat = arena[:, 2048:4096].rearrange("p (w o d) -> p w o d", w=4, o=KC)
    w_z = arena[:, 4096:6144].rearrange("p (w o d) -> p w o d", w=4, o=KC)
    w_q = arena[:, 6144:7168].bitcast(bf16).rearrange("p (w o d) -> p w o d", w=4, o=KC)
    wT = sb("wT", [P, 4, KC, D], bf16)
    wabs = sb("wabs", [P, 4])
    am = sb("am", [P, 4])
    am_eps = sb("am_eps", [P, 4])
    am_inv = sb("am_inv", [P, 4])
    c_qk = sb("c_qk", [P, 2])
    rw = sb("rw", [P, KC, E])

    ident = sb("ident", [P, P])
    ident_b = sb("ident_b", [P, P], bf16)
    ones = sb("ones", [P, P])
    ones_b = sb("ones_b", [P, P], bf16)
    before = sb("before", [P, P], bf16)
    causal = sb("causal", [P, SEQ])
    seen = sb("seen", [P, BT, SEQ])
    own = sb("own", [P, BT])
    half = sb("half", [P, TG])
    expert_no = sb("expert_no", [P, E])

    ys = sb("ys", [P, TG, D])
    stats = sb("stats", [P, 2, TG, 6])
    mv = sb("mv", [P, 2, TG, 2])
    veps = sb("veps", [P, 2, TG])
    rstd = sb("rstd", [P, 2, TG])
    amax = sb("amax", [P, 2, TG])
    inv = sb("inv", [P, 2, TG])
    mul = sb("mul", [P, 2, TG])
    s1 = sb("s1", [P, TG])
    s2 = sb("s2", [P, TG])
    s_qk = [sb(f"s_qk{i}", [P, TG]) for i in range(2)]
    s_v = sb("s_v", [P, TG])
    s_p = [sb(f"s_p{i}", [P, TG]) for i in range(2)]
    q1 = sb("q1", [P, TG, D], bf16)
    q2 = [sb(f"q2_{i}", [P, TG, D], bf16) for i in range(2)]
    diag = sb("diag", [P, TG, P])
    xq = sb("xq", [P, KC, GT], bf16)
    oq = sb("oq", [P, KC, GT], bf16)
    s_row = sb("s_row", [P, GT])
    qT = [sb(f"qT{i}", [P, KC, GT]) for i in range(2)]
    kT = sb("kT", [P, KC, GT])
    v_sb = sb("v_sb", [P, TG, H, VW])
    sc = [sb(f"sc{i}", [P, H, SEQ]) for i in range(2)]
    mx = [sb(f"mx{i}", [P, H]) for i in range(2)]
    pr = [sb(f"pr{i}", [P, SLOTS, SLOTS, SEQ]) for i in range(2)]
    pT = [sb(f"pT{i}", [P, SLOTS, P]) for i in range(2)]
    rs = sb("rs", [P, H])
    o_sb = sb("o_sb", [P, TG, D])
    hrow = sb("hrow", [P, TG, TOPK, ROW])
    hT = sb("hT", [P, KC, GT])
    scT = sb("scT", [E, GT])
    rmax = sb("rmax", [P, TG])
    rsub = sb("rsub", [P, TG, E])
    rexp = sb("rexp", [P, TG, E])
    top = sb("top", [P, TG, 8])
    topi = sb("topi", [P, TG, 8], u32)
    topf = sb("topf", [P, TG, TOPK])
    hot = sb("hot", [P, TG, TOPK, E])
    both = sb("both", [P, TG, E], bf16)
    den = sb("den", [P, TG])
    deni = sb("deni", [P, TG])
    dest = sb("dest", [P, TG, TOPK])
    filled = sb("filled", [P, E])
    pos = sb("pos", [P, TG, E])
    posh = sb("posh", [P, TG, TOPK, E])
    posf = sb("posf", [P, TG, TOPK])
    posi = sb("posi", [P, TG, TOPK], i32)

    GU_WORDS, DW_WORDS, PAD_WORDS = KC * E * 2 * F, E * D, PADS * ROW
    gu = arena[:, 0:GU_WORDS].rearrange("p (c e f) -> p c e f", c=KC, e=E)
    dw = arena[0:F, GU_WORDS:GU_WORDS + DW_WORDS].rearrange("p (e d) -> p e d", e=E)
    PAD_AT = GU_WORDS + DW_WORDS
    pad = arena[:, PAD_AT:PAD_AT + PAD_WORDS].rearrange("p (k r) -> p k r", r=ROW)
    FIN_WORDS = TG * TOPK * D
    fin = [arena[:, PAD_AT + i * FIN_WORDS:PAD_AT + (i + 1) * FIN_WORDS].rearrange("p (t k d) -> p t k d", t=TG, k=TOPK) for i in range(2)]
    xe = [hrow[:, i, 0, :] for i in range(4)]
    xeT = [qT[0][:, i, 0:D].rearrange("p (c t) -> p c t", c=KC) for i in range(2)]
    sg = [kT[:, 0, i * F:(i + 1) * F] for i in range(2)]
    hh = [kT[:, 1, i * F:(i + 1) * F] for i in range(2)]
    hhT = [sc[i][:, :, :].rearrange("p h j -> p (h j)")[0:F, 0:P] for i in range(2)]
    ye = [ys[:, i, :] for i in range(4)]
    di = sb("di", [P, 4], i32)
    eighth = sb("eighth", [P, E])
    pad_at = sb("pad_at", [P, 3])
    pad_no = sb("pad_no", [P, PADS])
    pad_i = sb("pad_i", [P, 1], i32)
    sel = sb("sel", [P, E])
    cnt = sb("cnt", [P, E])
    cum = [sb(f"cum{i}", [P, E // 2 + E]) for i in range(2)]
    tile_no = sb("tile_no", [P, EXPERT_TILES])
    live = sb("live", [P, EXPERT_TILES])
    kp = sb("kp", [P, EXPERT_TILES])
    past = arena[:, PAD_AT + PAD_WORDS:PAD_AT + PAD_WORDS + EXPERT_TILES * E].rearrange("p (k e) -> p k e", e=E)
    ek = sb("ek", [P, 2, EXPERT_TILES])
    table = sb("table", [P, 2, EXPERT_TILES], i32)

    bank = [ctx.enter_context(nc.psum_tensor(f"bank{i}", [P, 512], fp32)) for i in range(8)]
    ps_a, ps_q, ps_k, ps_pt, ps_o, ps_c = bank[0], bank[1], bank[2], bank[5], bank[6], bank[7]
    ps_s = [bank[3], bank[4]]

    ids_in, mixed_in, w_in, rw_in = sem("ids_in"), sem("mixed_in"), sem("w_in"), sem("rw_in")
    mix_got, mix_put, mix_in = [sem("mix_got0"), sem("mix_got1")], sem("mix_put"), sem("mix_in")
    x_in = [sem("x_in0"), sem("x_in1")]
    const_ok, zero0_ok, zero1_ok, vones_ok = sem("const_ok"), sem("zero0_ok"), sem("zero1_ok"), sem("vones_ok")
    wabs_ok, am_sum, am_ok, wT_ps, wT_ok = [sem(n) for n in ("wabs_ok", "am_sum", "am_ok", "wT_ps", "wT_ok")]
    bd1_ok, bd2_ok = sem("bd1_ok"), sem("bd2_ok")
    y_ready, y_copied, var1_ok, rstd1_ok, s1_ok, q1_ok = [sem(n) for n in ("y_ready", "y_copied", "var1_ok", "rstd1_ok", "s1_ok", "q1_ok")]
    diag_ok, xqT_ready, xqT_copied, srow_ready, srow_copied = [sem(n) for n in ("diag_ok", "xqT_ready", "xqT_copied", "srow_ready", "srow_copied")]
    q_ready, q_copied, k_ready, k_scaled, v_ready, v_copied = [sem(n) for n in ("q_ready", "q_copied", "k_ready", "k_scaled", "v_ready", "v_copied")]
    kx_in, v_put, vx_in = sem("kx_in"), sem("v_put"), sem("vx_in")
    sc_ready, sc_scaled, mx_ok, sub_ok, exp_ok = [sem(n) for n in ("sc_ready", "sc_scaled", "mx_ok", "sub_ok", "exp_ok")]
    pT_ready, pT_copied, o_ready, o_ok, var2_ok, rstd2_ok, q2_ok = [sem(n) for n in ("pT_ready", "pT_copied", "o_ready", "o_ok", "var2_ok", "rstd2_ok", "q2_ok")]
    oqT_ready, oqT_copied, proj_ready, x1_ok, h_ready, h_copied = [sem(n) for n in ("oqT_ready", "oqT_copied", "proj_ready", "x1_ok", "h_ready", "h_copied")]
    hT_ready, hT_copied, scT_ready, scT_copied, rt_ready, rsub_ok, rexp_ok, both_ok, rank_ready, rank_used, pos_ok, scattered = [
        sem(n) for n in ("hT_ready", "hT_copied", "scT_ready", "scT_copied", "rt_ready", "rsub_ok", "rexp_ok", "both_ok", "rank_ready", "rank_used", "pos_ok", "scattered")]

    gu_in, dw_in, pad_ok, padi_ok, padded, table_ok = [sem(n) for n in ("gu_in", "dw_in", "pad_ok", "padi_ok", "padded", "table_ok")]
    xe_in = [sem(f"xe_in{i}") for i in range(4)]
    y_put = [sem(f"y_put{i}") for i in range(4)]
    xeT_ready, xeT_copied, gu_ready, silu_ok, hh_ok, hhT_ready, hhT_copied, ye_ready, ye_copied = [
        sem(n) for n in ("xeT_ready", "xeT_copied", "gu_ready", "silu_ok", "hh_ok", "hhT_ready", "hhT_copied", "ye_ready", "ye_copied")]
    fin_in = [sem("fin_in0"), sem("fin_in1")]
    passed = sem("passed")
    pair_ok, fin_ok, out_put = sem("pair_ok"), sem("fin_ok"), sem("out_put")

    def wait(eng, s, g, per_group, nth, lag=0):
        if isinstance(g, int) and g < lag:
            return
        eng.wait_ge(s, (g - lag) * per_group + nth)

    def pipeline(eng, iteration):
        iteration(0, None, None, 0)
        iteration(1, 0, None, 1)
        iteration(2, 1, 0, 0)
        iteration(3, 2, 1, 1)
        with eng.Fori(2, GROUPS // 2) as i:
            iteration(2 * i, 2 * i - 1, 2 * i - 2, 0)
            iteration(2 * i + 1, 2 * i, 2 * i - 1, 1)
        iteration(None, GROUPS - 1, GROUPS - 2, 0)
        iteration(None, None, GROUPS - 1, 1)

    def stand(eng):
        eng.sem_inc(passed, 1)

    def since(eng, s, k, ago, first=1):
        if isinstance(k, int) and k < ago:
            return
        eng.wait_ge(s, k - ago + first)

    def tiles(eng, step):
        for k in range(8):
            step(k, k % 4, k // 4)
        with eng.Fori(2, EXPERT_TILES // 4) as i:
            for j in range(4):
                step(4 * i + j, j, i)
        for k in range(EXPERT_TILES, EXPERT_TILES + 3):
            step(k, k % 4, k // 4)

    def groups(eng, step):
        step(0, 0)
        step(1, 1)
        with eng.Fori(1, GROUPS // 2) as i:
            step(2 * i, 0)
            step(2 * i + 1, 1)

    def slot_in(eng, s, g, par):
        eng.wait_ge(s, (g - par) * 8 + 16)

    out_v = out.rearrange("(t b) s d -> (b s) t d", b=BT)
    y_v = y_d.rearrange("(t p k) d -> p t k d", p=P, k=TOPK)

    x_v = x.rearrange("(t b) s d -> (b s) t d", b=BT)
    v_rows = v_d.rearrange("(t p) r -> p t r", p=P)
    v_slots = v_d.rearrange("(n j) (s r) -> s j n r", j=SEQ, s=SLOTS)

    with nc.Block() as block:

        @block.sync
        def _(sp):
            sp.dma_start(ids[:, 0:1], sub.unsqueeze(1)).then_inc(ids_in, 16)
            sp.dma_start(ids[:, 1:2], cond.unsqueeze(1)).then_inc(ids_in, 16)
            for i, w in enumerate((wq, wk, wv, wp)):
                sp.dma_start(w_nat[:, i], w.rearrange("(o p) d -> p o d", p=P)).then_inc(w_in, 16)
            for g in range(2):
                sp.dma_start(X[:, g * TG:(g + 1) * TG, :], x_v[:, g * TG:(g + 1) * TG, :]).then_inc(x_in[g], 16)
            for i in range(2):
                sp.wait_ge(mix_got[i], 16)
                sp.dma_start(mix_d[i], mix_rows[i]).then_inc(mix_put, 16)
                sp.wait_ge(mix_put, 16 * (i + 1))
                if i == 0:
                    sp.wait_ge(const_ok, 1)
                sp.dma_start(mix[i][:, 0:TILES, :], mix_d[i].rearrange("b (c d) -> (b c) d", d=SEQ).rearrange("(t p) d -> p t d", p=P)).then_inc(mix_in, 16)
            sp.dma_start(rw[:, :, :], w_router.rearrange("(c p) e -> p c e", p=P)).then_inc(rw_in, 16)

            def spread_k(g, par):
                if g is None:
                    return
                wait(sp, k_scaled, g, 2, 2)
                wait(sp, sc_ready, g, TG, TG, lag=2)
                if isinstance(g, int) and g < 2:
                    sp.wait_ge((zero0_ok, zero1_ok)[g], 1)
                for h in range(HC):
                    rows = slice(h * HD, (h + 1) * HD)
                    sp.dma_start(kx[par][rows, :, h, :], kT[rows, :, :]).then_inc(kx_in, 16)

            def spread_v(g):
                if g is None:
                    return
                wait(sp, v_copied, g, 2, 2)
                wait(sp, vx_in, g, 16 * SLOTS, 16 * SLOTS, lag=1)
                sp.dma_start(v_rows, v_sb[:, :, :, :].rearrange("p t h r -> p t (h r)")).then_inc(v_put, 16)
                wait(sp, v_put, g, 16, 16)
                wait(sp, o_ready, g, TG, TG, lag=1)
                for s in range(SLOTS):
                    sp.dma_start(vx[s * SEQ:(s + 1) * SEQ, :, s, :], v_slots[s]).then_inc(vx_in, 16)

            def iteration(a, b, c, par):
                spread_k(a, par)
                spread_v(a)

            for g in range(2, GROUPS):
                sp.wait_ge(x_in[g % 2], (g // 2) * 16)
                sp.dma_start(X[:, g * TG:(g + 1) * TG, :], x_v[:, g * TG:(g + 1) * TG, :]).then_inc(x_in[g % 2], 16)
            pipeline(sp, iteration)
            sp.wait_ge(sc_ready, TILES - TG)
            for half_, w in enumerate((w_gate, w_up)):
                for c in range(KC):
                    sp.dma_start(gu[:, c, :, half_ * F:(half_ + 1) * F], w[:, c * P:(c + 1) * P, :].rearrange("e p f -> p e f")).then_inc(gu_in, 16)
            sp.wait_ge(sc_ready, TILES)
            sp.dma_start(dw, w_down.rearrange("e f d -> f e d")).then_inc(dw_in, 16)
            sp.wait_ge(scattered, 16 * TOPK * TILES)
            sp.wait_ge(padded, 16)
            sp.wait_ge(table_ok, 1)

            def load_rows(k, j, i):
                if isinstance(k, int) and k >= EXPERT_TILES:
                    return
                since(sp, hh_ok, k, 4)
                row = sp.value_load(table[0:1, 1, bass.ds(k, 1)], min_val=0, max_val=E * PITCH - P)
                sp.dma_start(xe[j], routed[bass.ds(row, P), :]).then_inc(xe_in[j], 16)

            tiles(sp, load_rows)
            for j in range(4):
                sp.wait_ge(y_put[j], 16 * (EXPERT_TILES // 4))

            def load_pair(g, par):
                wait(sp, fin_ok, g, 1, 1, lag=2)
                sp.dma_start(fin[par], y_v[:, bass.ds(g * TG, TG), :, :]).then_inc(fin_in[par], 16)

            load_pair(0, 0)
            load_pair(1, 1)
            with sp.Fori(1, GROUPS // 2) as i:
                load_pair(2 * i, 0)
                load_pair(2 * i + 1, 1)
            sp.wait_ge(out_put, 16 * GROUPS)

        @block.gpsimd
        def _(pool):
            g_ = nc.gpsimd
            g_.iota(pad_no[:, :], [[1, PADS]], base=Y_ROWS, channel_multiplier=0, allow_small_or_imprecise_dtypes=True)
            g_.iota(pad_at[:, 0:1], [[0, 1]], base=0, channel_multiplier=PADS, allow_small_or_imprecise_dtypes=True)
            g_.iota(tile_no[:, :], [[1, EXPERT_TILES]], base=0, channel_multiplier=0, allow_small_or_imprecise_dtypes=True)
            g_.memset(cum[0][:, :], 0.0)
            g_.memset(cum[1][:, :], 0.0)
            for t_, v_ in ((eighth, 1.0), (ident, 0.0), (ones, 1.0), (ones_b, 1.0), (before, 1.0), (seen, 1.0), (own, 1.0), (half, -0.5), (v_sb, 1.0), (mix[0], 0.0)):
                g_.memset(t_[tuple([slice(None)] * len(t_.shape))], v_)
            g_.iota(expert_no[:, :], [[1, E]], base=0, channel_multiplier=0, allow_small_or_imprecise_dtypes=True)
            g_.iota(filled[:, :], [[PITCH, E]], base=0, channel_multiplier=0, allow_small_or_imprecise_dtypes=True)
            g_.iota(dest[:, :, :], [[TOPK * P, TG], [1, TOPK]], base=-TOPK * GT, channel_multiplier=TOPK, allow_small_or_imprecise_dtypes=True)
            pool.wait_ge(ids_in, 32)
            for i, table in enumerate((w_mix1, w_mix2)):
                g_.indirect_dma_start(mix_rows[i], None, table.rearrange("s c d -> s (c d)"),
                                      bass.IndirectOffsetOnAxis(ap=ids[:, i:i + 1], axis=0)).then_inc(mix_got[i], 16)
            pool.drain()
            g_.affine_select(out=ident[:, :], in_=ident[:, :], compare_op=ALU.not_equal, fill=1.0, base=0, pattern=[[-1, P]], channel_multiplier=1)
            g_.affine_select(out=before[:, :], in_=before[:, :], compare_op=ALU.is_gt, fill=0.0, base=0, pattern=[[1, P]], channel_multiplier=-1)
            g_.affine_select(out=seen[:, :, :], in_=seen[:, :, :], compare_op=ALU.is_ge, fill=0.0, base=0, pattern=[[-SEQ, BT], [-1, SEQ]], channel_multiplier=1)
            g_.affine_select(out=own[:, :], in_=own[:, :], compare_op=ALU.is_ge, fill=0.0, base=0, pattern=[[-SEQ, BT]], channel_multiplier=1)
            g_.affine_select(out=eighth[:, :], in_=eighth[:, :], compare_op=ALU.is_ge, fill=0.0, base=0, pattern=[[-(P // E), E]], channel_multiplier=1)
            pool.drain()
            g_.affine_select(out=eighth[:, :], in_=eighth[:, :], compare_op=ALU.is_ge, fill=0.0, base=P // E - 1, pattern=[[P // E, E]], channel_multiplier=-1)
            g_.affine_select(out=own[:, :], in_=own[:, :], compare_op=ALU.is_ge, fill=0.0, base=SEQ - 1, pattern=[[SEQ, BT]], channel_multiplier=-1)
            pool.drain()
            g_.tensor_copy(ident_b[:, :], ident[:, :]).then_inc(const_ok, 1)
            pool.wait_ge(mix_in, 32)

            def spread(dst, i, g):
                src = mix[i][:, bass.ds(g * TG, TG), :].unsqueeze(2).to_broadcast([P, TG, BT, SEQ])
                return g_.tensor_tensor(dst[:, :, :, :], src, own[:, :].unsqueeze(1).unsqueeze(3).to_broadcast([P, TG, BT, SEQ]), ALU.mult)

            def spread1(g, par):
                if g is not None:
                    wait(pool, y_ready, g, 2, 2, lag=2)
                    spread(bd1[par], 0, g).then_inc(bd1_ok, 1)

            def spread2(g, par):
                if g is not None:
                    wait(pool, h_ready, g, 2, 2, lag=2)
                    spread(bd2[par], 1, g).then_inc(bd2_ok, 1)

            spread1(0, 0)
            pool.wait_ge(wT_ps, 1)
            pool.wait_ge(mix_put, 32)
            g_.memset(kx[0][:, :, :, :], 0.0)
            g_.memset(vx[:, :, :, :], 0.0).then_inc(zero0_ok, 1)

            def rstd_(g, n, ready, done):
                if g is not None:
                    wait(pool, ready, g, 1, 1)
                    g_.tensor_tensor(rstd[:, n, :], veps[:, n, :], half[:, :], ALU.pow).then_inc(done, 1)

            def diag_(g):
                if g is not None:
                    wait(pool, s1_ok, g, 1, 1)
                    wait(pool, srow_ready, g, 1, 1, lag=1)
                    g_.tensor_tensor(diag[:, :, :], ident[:, :].unsqueeze(1).to_broadcast([P, TG, P]),
                                     s1[:, :].unsqueeze(2).to_broadcast([P, TG, P]), ALU.mult).then_inc(diag_ok, 1)

            def sub_max(g, t):
                if g is not None:
                    wait(pool, mx_ok, g, TG, t + 1)
                    g_.tensor_tensor(sc[t % 2][:, :, :], sc[t % 2][:, :, :], mx[t % 2][:, :].unsqueeze(2).to_broadcast([P, H, SEQ]),
                                     ALU.subtract).then_inc(sub_ok, 1)

            def scatter(g):
                if g is not None:
                    wait(pool, pos_ok, g, 1, 1)
                    wait(pool, h_copied, g, 2, 2)
                    stand(pool)
                    for t in range(TG):
                        for k in range(TOPK):
                            g_.indirect_dma_start(routed, bass.IndirectOffsetOnAxis(ap=posi[:, t, k:k + 1], axis=0),
                                                  hrow[:, t, k, :], None).then_inc(scattered, 16)

            def iteration(a, b, c, par):
                sub_max(b, 0)
                sub_max(b, 1)
                rstd_(a, 0, var1_ok, rstd1_ok)
                diag_(a)
                sub_max(b, 2)
                spread2(c, par)
                sub_max(b, 3)
                rstd_(b, 1, var2_ok, rstd2_ok)
                if a is not None:
                    spread1(a + 1, 1 - par)
                if isinstance(a, int) and a == 0:
                    g_.memset(kx[1][:, :, :, :], 0.0).then_inc(zero1_ok, 1)
                scatter(c)

            pipeline(pool, iteration)

            pool.wait_ge(scattered, 16 * TOPK * TILES)
            g_.memset(pad[:, :, :], 0.0).then_inc(pad_ok, 1)
            pool.wait_ge(padi_ok, 1)
            g_.indirect_dma_start(routed, bass.IndirectOffsetOnAxis(ap=pad_i[:, 0:1], axis=0), pad.rearrange("p k r -> p (k r)"), None).then_inc(padded, 16)

            def put_rows(k, j, i):
                if isinstance(k, int) and k < 3:
                    return
                since(pool, ye_copied, k, 3)
                stand(pool)
                n = (j + 1) % 4
                g_.indirect_dma_start(y_d, bass.IndirectOffsetOnAxis(ap=di[:, n:n + 1], axis=0), ye[n], None,
                                      bounds_check=Y_ROWS - 1, oob_is_err=False).then_inc(y_put[n], 16)

            tiles(pool, put_rows)

            def add_pair(g, par):
                slot_in(pool, fin_in[par], g, par)
                g_.tensor_tensor(fin[par][:, :, 0, :], fin[par][:, :, 0, :], fin[par][:, :, 1, :], ALU.add).then_inc(pair_ok, 1)

            groups(pool, add_pair)

        @block.scalar
        def _(act):
            a_ = nc.scalar

            act.wait_ge(wT_ps, 1)
            for i in range(2):
                a_.activation(wT[:, 2 * i:2 * i + 2, :, :], bank[i][:, :].bitcast(bf16).rearrange("p (w c o) -> p w c o", w=2, c=KC), ACT.Copy).then_inc(wT_ok, 1)

            def copy_y(g, n):
                if g is None:
                    return
                wait(act, y_ready, g, 2, n + 1)
                wait(act, q1_ok, g, 1, 1, lag=1)
                a_.activation(ys[:, 2 * n:2 * n + 2, :], ps_a[:, :].rearrange("p (t d) -> p t d", t=2), ACT.Copy).then_inc(y_copied, 1)

            def copy_T(g, ready, dst, src, free, per, done):
                if g is None:
                    return
                wait(act, ready, g, 1, 1)
                wait(act, free, g, per, per, lag=1)
                a_.activation(dst[:, :, :], src[:, :].bitcast(bf16).rearrange("p (c t) -> p c t", c=KC), ACT.Copy).then_inc(done, 1)

            def copy_srow(g):
                if g is None:
                    return
                wait(act, srow_ready, g, 1, 1)
                wait(act, k_scaled, g, 2, 2, lag=1)
                a_.activation(s_row[:, :], ps_a[:, :], ACT.Copy).then_inc(srow_copied, 1)

            def copy_q(g, par, cc):
                if g is None:
                    return
                wait(act, q_ready, g, 2, cc + 1)
                wait(act, sc_ready, g, TG, TG, lag=2)
                a_.activation(qT[par][:, cc, :], ps_q[:, :], ACT.Copy).then_inc(q_copied, 1)

            def copy_v(g, n):
                if g is None:
                    return
                wait(act, v_ready, g, 2, n + 1)
                wait(act, s1_ok, g, 1, 1)
                wait(act, v_put, g, 16, 16, lag=1)
                src = (ps_q, ps_k)[n]
                for k in range(2):
                    t = 2 * n + k
                    last = a_.activation(v_sb[:, t, :, 0:HD], src[:, k * D:(k + 1) * D].rearrange("p (h r) -> p h r", h=H), ACT.Copy, scale=s_v[:, t:t + 1])
                last.then_inc(v_copied, 1)

            def exp_(g, t):
                if g is None:
                    return
                wait(act, sub_ok, g, TG, t + 1)
                if t >= 2:
                    wait(act, pT_ready, g, TG, t - 1)
                else:
                    wait(act, pT_ready, g, TG, TG + t - 1, lag=1)
                a_.activation(pr[t % 2][:, :, :, :].rearrange("p c s j -> p s c j"),
                              sc[t % 2][:, :, :].rearrange("p (s c) j -> p s c j", c=SLOTS), ACT.Exp).then_inc(exp_ok, 1)

            def copy_pT(g, t):
                if g is None:
                    return
                wait(act, pT_ready, g, TG, t + 1)
                if t >= 2:
                    wait(act, o_ready, g, TG, t - 1)
                else:
                    wait(act, o_ready, g, TG, TG + t - 1, lag=1)
                a_.activation(pT[t % 2][:, :, :], ps_pt[:, :].rearrange("p (c i) -> p c i", c=SLOTS), ACT.Copy).then_inc(pT_copied, 1)

            def copy_h(g, n):
                if g is None:
                    return
                wait(act, h_ready, g, 2, n + 1)
                wait(act, scattered, g, 16 * TG * TOPK, 16 * TG * TOPK, lag=1)
                for k in range(TOPK):
                    last = a_.activation(hrow[:, 2 * n:2 * n + 2, k, 0:D], ps_c[:, :].rearrange("p (t d) -> p t d", t=2), ACT.Copy)
                last.then_inc(h_copied, 1)

            def copy_hT(g, n):
                if g is None:
                    return
                wait(act, hT_ready, g, 2, n + 1)
                wait(act, scT_ready, g, 1, 1, lag=1)
                a_.activation(hT[:, :, 2 * n * P:(2 * n + 2) * P], ps_c[:, :].rearrange("p (c t) -> p c t", c=KC), ACT.Copy).then_inc(hT_copied, 1)

            def copy_scT(g):
                if g is None:
                    return
                wait(act, scT_ready, g, 1, 1)
                wait(act, rt_ready, g, 1, 1, lag=1)
                a_.activation(scT[:, :], ps_c[0:E, :], ACT.Copy).then_inc(scT_copied, 1)

            def exp_router(g):
                if g is None:
                    return
                wait(act, rsub_ok, g, 1, 1)
                a_.activation(rexp[:, :, :], rsub[:, :, :], ACT.Exp).then_inc(rexp_ok, 1)

            def iteration(a, b, c, par):
                copy_y(a, 0)
                exp_(b, 0)
                copy_y(a, 1)
                exp_(b, 1)
                copy_T(c, oqT_ready, oq, ps_c, proj_ready, 2, oqT_copied)
                copy_pT(b, 0)
                copy_T(a, xqT_ready, xq, ps_a, v_ready, 2, xqT_copied)
                copy_pT(b, 1)
                copy_srow(a)
                exp_(b, 2)
                copy_q(a, par, 0)
                copy_h(c, 0)
                copy_pT(b, 2)
                copy_q(a, par, 1)
                copy_h(c, 1)
                exp_(b, 3)
                copy_v(a, 0)
                copy_v(a, 1)
                copy_hT(c, 0)
                copy_pT(b, 3)
                copy_hT(c, 1)
                copy_scT(c)
                exp_router(c)

            pipeline(act, iteration)

            def step(k, j, i):
                if not (isinstance(k, int) and k >= EXPERT_TILES):
                    since(act, xeT_ready, k, 0)
                    since(act, gu_ready, k, 2)
                    a_.activation(xeT[j % 2], bank[j % 2][:, 0:D].rearrange("p (c t) -> p c t", c=KC), ACT.Copy).then_inc(xeT_copied, 1)
                if not (isinstance(k, int) and not 1 <= k <= EXPERT_TILES):
                    n = (j + 1) % 2
                    since(act, gu_ready, k, 1)
                    since(act, hh_ok, k, 3)
                    a_.activation(sg[n], bank[2 + n][:, 0:F], ACT.Silu).then_inc(silu_ok, 1)
                if not (isinstance(k, int) and k < 3):
                    n = (j + 1) % 4
                    since(act, ye_ready, k, 3)
                    if not (isinstance(k, int) and k < 7):
                        act.wait_ge(y_put[n], 16 * (i - 1 if n != 0 else i) if not isinstance(k, int) else 16 * ((k - 3) // 4))
                    a_.activation(ye[n], bank[6 + n % 2][:, 0:D], ACT.Copy).then_inc(ye_copied, 1)

            tiles(act, step)

            def put_out(g, par):
                wait(act, fin_ok, g, 1, 1)
                act.dma_start(out_v[:, bass.ds(g * TG, TG), :], X[:, bass.ds(g * TG, TG), :]).then_inc(out_put, 16)

            groups(act, put_out)

        @block.vector
        def _(dve):
            v = nc.vector

            dve.wait_ge(w_in, 64)
            v.tensor_reduce(wabs[:, :], w_nat[:, :, :, :], AX.XY, ALU.add, apply_absolute_value=True).then_inc(wabs_ok, 1)
            dve.wait_ge(am_sum, 1)
            v.tensor_scalar(am[:, :], bank[0][:, 0:4], 1.0 / (D * D), None, ALU.mult)
            v.tensor_scalar(am_eps[:, :], bank[0][:, 0:4], 1.0 / (D * D), EPS, ALU.mult, ALU.add)
            dve.drain()
            v.reciprocal(am_inv[:, :], am_eps[:, :])
            v.tensor_scalar(c_qk[:, 0:1], am[:, 0:1], am[:, 1:2], HD ** -0.5, ALU.mult, ALU.mult)
            dve.drain()
            for i in range(4):
                v.tensor_scalar(w_z[:, i], w_nat[:, i], am_inv[:, i:i + 1], MAGIC, ALU.mult, ALU.add)
            dve.drain()
            v.tensor_scalar(w_z[:, :, :, :], w_z[:, :, :, :], MAGIC, 1.0, ALU.subtract, ALU.min)
            dve.drain()
            v.tensor_scalar(w_q[:, :, :, :], w_z[:, :, :, :], -1.0, None, ALU.max).then_inc(am_ok, 1)
            dve.wait_ge(const_ok, 1)
            v.tensor_tensor(seen[:, :, :], seen[:, :, :], own[:, :].unsqueeze(2).to_broadcast([P, BT, SEQ]), ALU.mult)
            dve.drain()
            v.tensor_reduce(causal[:, :], seen[:, :, :].rearrange("p b j -> p j b"), AX.X, ALU.add)
            dve.drain()
            v.tensor_scalar(causal[:, :], causal[:, :], 1.0, -NEG, ALU.subtract, ALU.mult)

            def norm_tail(n, src, cen, s_out, g, var_ok, rstd_ok, s_ok, extra, q_out, q_ok):
                dve.drain()
                for t in range(TG):
                    v.bn_aggr(mv[:, n, t, :], stats[:, n, t, :])
                dve.drain()
                v.tensor_scalar(veps[:, n, :], mv[:, n, :, 1], EPS, None, ALU.add).then_inc(var_ok, 1)
                for t in range(TG):
                    v.tensor_scalar(cen[:, t, :], src[:, t, :], mv[:, n, t, 0:1], None, ALU.subtract)
                dve.drain()
                v.tensor_reduce(amax[:, n, :], cen[:, :, :], AX.X, ALU.max, apply_absolute_value=True)
                dve.drain()
                wait(dve, rstd_ok, g, 1, 1)
                v.tensor_tensor(amax[:, n, :], amax[:, n, :], rstd[:, n, :], ALU.mult)
                dve.drain()
                last = v.tensor_scalar(s_out[:, :], amax[:, n, :], 1e-5, 1.0 / QMAX, ALU.max, ALU.mult)
                dve.drain()
                v.reciprocal(inv[:, n, :], s_out[:, :])
                extra()
                dve.drain()
                v.tensor_tensor(mul[:, n, :], inv[:, n, :], rstd[:, n, :], ALU.mult)
                dve.drain()
                for t in range(TG):
                    v.tensor_scalar(cen[:, t, :], cen[:, t, :], mul[:, n, t:t + 1], MAGIC, ALU.mult, ALU.add)
                dve.drain()
                v.tensor_scalar(q_out[:, :, :], cen[:, :, :], MAGIC, None, ALU.subtract).then_inc(q_ok, 1)

            def stats1(g, n):
                if g is None:
                    return
                if n == 0:
                    wait(dve, diag_ok, g, 1, 1, lag=1)
                    wait(dve, v_copied, g, 2, 2, lag=1)
                    wait(dve, xqT_ready, g, 1, 1, lag=1)
                wait(dve, y_copied, g, 2, n + 1)
                for t in (2 * n, 2 * n + 1):
                    v.bn_stats(stats[:, 0, t, :], ys[:, t, :])

            def norm1(g, par):
                if g is None:
                    return

                def scales():
                    v.tensor_scalar(s_qk[par][:, :], s1[:, :], c_qk[:, 0:1], None, ALU.mult)
                    v.tensor_scalar(s_v[:, :], s1[:, :], am[:, 2:3], None, ALU.mult).then_inc(s1_ok, 1)

                norm_tail(0, ys, ys, s1, g, var1_ok, rstd1_ok, s1_ok, scales, q1, q1_ok)

            def norm2(g, par):
                if g is None:
                    return
                wait(dve, oqT_ready, g, 1, 1, lag=2)
                for t in range(TG):
                    v.bn_stats(stats[:, 1, t, :], o_sb[:, t, :])

                def scales():
                    v.tensor_scalar(s_p[par][:, :], s2[:, :], am[:, 3:4], None, ALU.mult)

                norm_tail(1, o_sb, o_sb, s2, g, var2_ok, rstd2_ok, None, scales, q2[par], q2_ok)

            def scale_k(g, cc):
                if g is None:
                    return
                wait(dve, k_ready, g, 2, cc + 1)
                wait(dve, srow_copied, g, 1, 1)
                wait(dve, kx_in, g, 16 * HC, 16 * HC, lag=1)
                v.tensor_tensor(kT[:, cc, :], ps_k[:, :], s_row[:, :], ALU.mult).then_inc(k_scaled, 1)

            def scale_scores(g, par, t):
                if g is None:
                    return
                wait(dve, sc_ready, g, TG, t + 1)
                if t >= 2:
                    wait(dve, exp_ok, g, TG, t - 1)
                else:
                    wait(dve, exp_ok, g, TG, TG + t - 1, lag=1)
                v.scalar_tensor_tensor(out=sc[t % 2][:, :, :], in0=ps_s[t % 2][:, :].rearrange("p (h j) -> p h j", j=SEQ), scalar=s_qk[par][:, t:t + 1],
                                       in1=causal[:, :].unsqueeze(1).to_broadcast([P, H, SEQ]), op0=ALU.mult, op1=ALU.add).then_inc(sc_scaled, 1)
                dve.drain()
                v.tensor_reduce(mx[t % 2][:, :], sc[t % 2][:, :, :], AX.X, ALU.max).then_inc(mx_ok, 1)

            def norm_o(g, t):
                if g is None:
                    return
                wait(dve, o_ready, g, TG, t + 1)
                o = ps_o[:, 0:H * VW].rearrange("p (h r) -> p h r", r=VW)
                v.reciprocal(rs[:, :], o[:, :, HD])
                dve.drain()
                v.tensor_tensor(o_sb[:, t, :].rearrange("p (h r) -> p h r", r=HD), o[:, :, 0:HD], rs[:, :].unsqueeze(2).to_broadcast([P, H, HD]),
                                ALU.mult).then_inc(o_ok, 1)
                dve.drain()

            def residual(g, par, n):
                if g is None:
                    return
                wait(dve, proj_ready, g, 2, n + 1)
                for k in range(2):
                    t = 2 * n + k
                    xt = X[:, bass.ds(g * TG + t, 1), :].rearrange("p o d -> p (o d)")
                    last = v.scalar_tensor_tensor(out=xt, in0=ps_c[:, k * D:(k + 1) * D], scalar=s_p[par][:, t:t + 1], in1=xt, op0=ALU.mult, op1=ALU.add)
                last.then_inc(x1_ok, 1)

            def route(g):
                if g is None:
                    return
                wait(dve, rt_ready, g, 1, 1)
                logits = ps_c[:, 0:TG * E].rearrange("p (t e) -> p t e", e=E)
                v.tensor_reduce(rmax[:, :], logits, AX.X, ALU.max)
                dve.drain()
                v.tensor_tensor(rsub[:, :, :], logits, rmax[:, :].unsqueeze(2).to_broadcast([P, TG, E]), ALU.subtract).then_inc(rsub_ok, 1)
                wait(dve, rexp_ok, g, 1, 1)
                v.tensor_scalar(dest[:, :, :], dest[:, :, :], float(TOPK * GT), None, ALU.add)
                for t in range(TG):
                    v.max(top[:, t, :], rexp[:, t, :])
                dve.drain()
                for t in range(TG):
                    v.max_index(topi[:, t, :], top[:, t, :], rexp[:, t, :])
                v.tensor_tensor(den[:, :], top[:, :, 0], top[:, :, 1], ALU.add)
                dve.drain()
                v.tensor_copy(topf[:, :, :], topi[:, :, 0:TOPK])
                v.reciprocal(deni[:, :], den[:, :])
                dve.drain()
                v.tensor_tensor(hot[:, :, :, :], expert_no[:, :].unsqueeze(1).unsqueeze(1).to_broadcast([P, TG, TOPK, E]),
                                topf[:, :, :].unsqueeze(3).to_broadcast([P, TG, TOPK, E]), ALU.is_equal)
                wait(dve, scattered, g, 16 * TG * TOPK, 16 * TG * TOPK, lag=1)
                v.tensor_tensor(hrow[:, :, :, D + 1], top[:, :, 0:TOPK], deni[:, :].unsqueeze(2).to_broadcast([P, TG, TOPK]), ALU.mult)
                v.tensor_copy(hrow[:, :, :, D], dest[:, :, :])
                dve.drain()
                v.tensor_tensor(both[:, :, :], hot[:, :, 0, :], hot[:, :, 1, :], ALU.add).then_inc(both_ok, 1)

            def place(g):
                if g is None:
                    return
                wait(dve, rank_ready, g, 1, 1)
                v.tensor_tensor(pos[:, :, :], ps_c[:, 0:TG * E].rearrange("p (t e) -> p t e", e=E),
                                filled[:, :].unsqueeze(1).to_broadcast([P, TG, E]), ALU.add)
                dve.drain()
                v.tensor_tensor(filled[:, :], filled[:, :], ps_c[:, TG * E:(TG + 1) * E], ALU.add).then_inc(rank_used, 1)
                v.tensor_tensor(posh[:, :, :, :], hot[:, :, :, :], pos[:, :, :].unsqueeze(2).to_broadcast([P, TG, TOPK, E]), ALU.mult)
                dve.drain()
                v.tensor_reduce(posf[:, :, :], posh[:, :, :, :], AX.X, ALU.add)
                dve.drain()
                v.tensor_copy(posi[:, :, :], posf[:, :, :]).then_inc(pos_ok, 1)

            def iteration(a, b, c, par):
                scale_scores(b, 1 - par, 0)
                stats1(a, 0)
                scale_scores(b, 1 - par, 1)
                stats1(a, 1)
                norm1(a, par)
                residual(c, par, 0)
                norm_o(b, 0)
                scale_scores(b, 1 - par, 2)
                residual(c, par, 1)
                norm_o(b, 1)
                scale_scores(b, 1 - par, 3)
                scale_k(a, 0)
                scale_k(a, 1)
                norm_o(b, 2)
                norm_o(b, 3)
                norm2(b, 1 - par)
                route(c)
                place(c)

            pipeline(dve, iteration)

            dve.drain()
            v.tensor_tensor(sel[:, :], eighth[:, :], filled[:, :], ALU.mult)
            v.tensor_scalar(cnt[:, :], expert_no[:, :], -float(PITCH), None, ALU.mult)
            dve.drain()
            v.tensor_reduce(pad_at[:, 1:2], sel[:, :], AX.X, ALU.add)
            v.tensor_tensor(cnt[:, :], cnt[:, :], filled[:, :], ALU.add)
            dve.drain()
            v.tensor_tensor(sel[:, :], eighth[:, :], expert_no[:, :], ALU.mult)
            v.tensor_scalar(cnt[:, :], cnt[:, :], float(P - 1), 1.0 / P, ALU.add, ALU.mult)
            dve.drain()
            v.tensor_reduce(pad_at[:, 2:3], sel[:, :], AX.X, ALU.add)
            v.tensor_scalar(cnt[:, :], cnt[:, :], 0.5 - 0.25 / P, MAGIC, ALU.subtract, ALU.add)
            dve.drain()
            v.tensor_scalar(pad_at[:, 2:3], pad_at[:, 2:3], -float(P), None, ALU.mult)
            v.tensor_scalar(cnt[:, :], cnt[:, :], MAGIC, None, ALU.subtract)
            dve.drain()
            v.tensor_tensor(pad_at[:, 0:1], pad_at[:, 0:1], pad_at[:, 2:3], ALU.add)
            v.tensor_copy(cum[0][:, E // 2:], cnt[:, :])
            dve.drain()
            v.tensor_tensor(pad_at[:, 1:2], pad_at[:, 1:2], pad_at[:, 0:1], ALU.add)
            dve.wait_ge(pad_ok, 1)
            v.tensor_scalar(pad[:, :, D], pad_no[:, :], pad_at[:, 0:1], None, ALU.add)
            for n, step_ in enumerate((1, 2, 4, 8)):
                v.tensor_tensor(cum[(n + 1) % 2][:, E // 2:], cum[n % 2][:, E // 2:], cum[n % 2][:, E // 2 - step_:E // 2 + E - step_], ALU.add)
                dve.drain()
                if n == 0:
                    v.tensor_copy(pad_i[:, :], pad_at[:, 1:2]).then_inc(padi_ok, 1)
            ends = cum[0][:, E // 2:]
            v.tensor_scalar(live[:, :], tile_no[:, :], ends[:, E - 1:E], None, ALU.is_lt)
            dve.drain()
            v.tensor_tensor(kp[:, :], tile_no[:, :], live[:, :], ALU.mult)
            v.tensor_scalar(live[:, :], live[:, :], -float(Y_ROWS), float(Y_ROWS), ALU.mult, ALU.add)
            dve.drain()
            v.tensor_tensor(past[:, :, :], kp[:, :].unsqueeze(2).to_broadcast([P, EXPERT_TILES, E]), ends.unsqueeze(1).to_broadcast([P, EXPERT_TILES, E]), ALU.is_ge)
            dve.drain()
            v.tensor_reduce(ek[:, 0, :], past[:, :, :], AX.X, ALU.add)
            dve.drain()
            v.tensor_tensor(past[:, :, :], past[:, :, :], cnt[:, :].unsqueeze(1).to_broadcast([P, EXPERT_TILES, E]), ALU.mult)
            dve.drain()
            v.tensor_reduce(ek[:, 1, :], past[:, :, :], AX.X, ALU.add)
            dve.drain()
            v.tensor_tensor(ek[:, 1, :], kp[:, :], ek[:, 1, :], ALU.subtract)
            v.tensor_copy(table[:, 0, :], ek[:, 0, :])
            dve.drain()
            v.tensor_scalar(ek[:, 1, :], ek[:, 1, :], float(P), None, ALU.mult)
            v.tensor_scalar(kp[:, :], ek[:, 0, :], float(PITCH), None, ALU.mult)
            dve.drain()
            v.tensor_tensor(table[:, 1, :], ek[:, 1, :], kp[:, :], ALU.add).then_inc(table_ok, 1)

            def step(k, j, i):
                if not (isinstance(k, int) and not 1 <= k <= EXPERT_TILES):
                    n = (j + 3) % 4
                    since(dve, silu_ok, k, 1)
                    since(dve, hhT_ready, k, 3)
                    v.scalar_tensor_tensor(out=hh[n % 2], in0=sg[n % 2], scalar=xe[n][:, D + 1:D + 2], in1=bank[2 + n % 2][:, F:2 * F], op0=ALU.mult, op1=ALU.mult)
                    if isinstance(k, int):
                        if k >= 5:
                            dve.wait_ge(y_put[n], 16 * ((k - 1) // 4))
                    else:
                        dve.wait_ge(y_put[n], 16 * i if j else 16 * (i - 1))
                    v.tensor_scalar(di[:, n:n + 1], xe[n][:, D:D + 1], live[:, bass.ds(k - 1, 1)], None, ALU.add).then_inc(hh_ok, 1)
                if not (isinstance(k, int) and not 2 <= k <= EXPERT_TILES + 1):
                    n = j % 2
                    since(dve, hhT_ready, k, 2)
                    since(dve, ye_ready, k, 4)
                    v.tensor_copy(hhT[n], bank[4 + n][0:F, 0:P]).then_inc(hhT_copied, 1)

            tiles(dve, step)

            def add_x(g, par):
                wait(dve, pair_ok, g, 1, 1)
                xg = X[:, bass.ds(g * TG, TG), :]
                v.tensor_tensor(xg, xg, fin[par][:, :, 0, :], ALU.add).then_inc(fin_ok, 1)

            groups(dve, add_x)

        @block.tensor
        def _(pe):
            t_ = nc.tensor

            pe.wait_ge(wabs_ok, 1)
            pe.wait_ge(const_ok, 1)
            t_.matmul(bank[0][:, 0:4], ones[:, :], wabs[:, :], start=True, stop=True).then_inc(am_sum, 1)
            pe.wait_ge(am_ok, 1)
            for i in range(4):
                ps = bank[i // 2][:, :].bitcast(bf16).rearrange("p (w c o) -> p w c o", w=2, c=KC)
                for c in range(KC):
                    for o in range(KC):
                        last = t_.transpose(ps[:, i % 2, c, o * P:(o + 1) * P], w_q[:, i, o, c * P:(c + 1) * P], ident_b[:, :])
            last.then_inc(wT_ps, 1)
            pe.wait_ge(wT_ok, 2)

            def mix1(g, par, n):
                if g is None:
                    return
                if n == 0:
                    wait(pe, bd1_ok, g, 1, 1)
                    if isinstance(g, int):
                        pe.wait_ge(x_in[par], 16 * (g // 2 + 1))
                    else:
                        pe.wait_ge(x_in[par], (g - par) * 8 + 16)
                    wait(pe, srow_copied, g, 1, 1, lag=1)
                else:
                    wait(pe, y_copied, g, 2, 1)
                for k in range(2):
                    t = 2 * n + k
                    last = t_.matmul(ps_a[:, k * D:(k + 1) * D], bd1[par][:, t, :, :].rearrange("p b d -> p (b d)"),
                                     X[:, bass.ds(g * TG + t, 1), :].rearrange("p o d -> p (o d)"), start=True, stop=True)
                last.then_inc(y_ready, 1)

            def transpose_q(g, src, q_ok, dst, free, free_per, free_lag, done):
                if g is None:
                    return
                wait(pe, q_ok, g, 1, 1)
                wait(pe, free, g, free_per, free_per, lag=free_lag)
                ps = dst[:, :].bitcast(bf16).rearrange("p (c t) -> p c t", c=KC)
                for t in range(TG):
                    for c in range(KC):
                        last = t_.transpose(ps[:, c, t * P:(t + 1) * P], src[:, t, c * P:(c + 1) * P], ident_b[:, :])
                last.then_inc(done, 1)

            def spread_s(g):
                if g is None:
                    return
                wait(pe, diag_ok, g, 1, 1)
                wait(pe, xqT_copied, g, 1, 1)
                t_.matmul(ps_a[:, :], ones[:, :], diag[:, :, :].rearrange("p t q -> p (t q)"), start=True, stop=True).then_inc(srow_ready, 1)

            def project_T(g, w, cc, ps, done):
                for c in range(KC):
                    last = t_.matmul(ps[:, :], wT[:, w, c, cc * P:(cc + 1) * P], xq[:, c, :], start=(c == 0), stop=(c == KC - 1))
                last.then_inc(done, 1)

            def project_qk(g, cc):
                if g is None:
                    return
                wait(pe, xqT_copied, g, 1, 1)
                if cc == 0:
                    wait(pe, v_copied, g, 2, 2, lag=1)
                else:
                    wait(pe, q_copied, g, 2, 1)
                project_T(g, 0, cc, ps_q, q_ready)
                if cc == 1:
                    wait(pe, k_scaled, g, 2, 1)
                project_T(g, 1, cc, ps_k, k_ready)

            def project_v(g, n):
                if g is None:
                    return
                if n == 0:
                    wait(pe, q_copied, g, 2, 2)
                else:
                    wait(pe, k_scaled, g, 2, 2)
                for k in range(2):
                    t = 2 * n + k
                    for c in range(KC):
                        last = t_.matmul((ps_q, ps_k)[n][:, k * D:(k + 1) * D], xq[:, c, t * P:(t + 1) * P], wT[:, 2, c, :], start=(c == 0), stop=(c == KC - 1))
                last.then_inc(v_ready, 1)

            def scores(g, par, t):
                if g is None:
                    return
                if t == 0:
                    wait(pe, kx_in, g, 16 * HC, 16 * HC)
                    wait(pe, q_copied, g, 2, 2)
                if t >= 2:
                    wait(pe, sc_scaled, g, TG, t - 1)
                else:
                    wait(pe, sc_scaled, g, TG, TG + t - 1, lag=1)
                for c in range(KC):
                    for b in range(BT):
                        cols = slice(t * P + b * SEQ, t * P + (b + 1) * SEQ)
                        last = t_.matmul(ps_s[t % 2][b * SEQ:(b + 1) * SEQ, c * HC * SEQ:(c + 1) * HC * SEQ], qT[par][:, c, cols], kx[par][:, c, :, cols],
                                         start=True, stop=True)
                last.then_inc(sc_ready, 1)

            def transpose_p(g, t):
                if g is None:
                    return
                wait(pe, exp_ok, g, TG, t + 1)
                if t > 0:
                    wait(pe, pT_copied, g, TG, t)
                else:
                    wait(pe, pT_copied, g, TG, TG, lag=1)
                for c in range(SLOTS):
                    last = t_.transpose(ps_pt[:, c * P:(c + 1) * P], pr[t % 2][:, c, :, :].rearrange("p s j -> p (s j)"), ident[:, :])
                last.then_inc(pT_ready, 1)

            def attend(g, par, t):
                if g is None:
                    return
                wait(pe, pT_copied, g, TG, t + 1)
                if t == 0:
                    wait(pe, vx_in, g, 16 * SLOTS, 16 * SLOTS)
                    wait(pe, o_ok, g, TG, TG, lag=1)
                else:
                    wait(pe, o_ok, g, TG, t)
                o = ps_o[:, 0:H * VW].rearrange("p (s c r) -> p s c r", s=SLOTS, c=SLOTS)
                for c in range(SLOTS):
                    for b in range(BT):
                        last = t_.matmul(o[b * SEQ:(b + 1) * SEQ, :, c, :], pT[t % 2][:, c, b * SEQ:(b + 1) * SEQ],
                                         vx[:, t * BT + b, :, c * VW:(c + 1) * VW], start=True, stop=True)
                last.then_inc(o_ready, 1)

            def project_o(g, n):
                if g is None:
                    return
                if n == 0:
                    wait(pe, oqT_copied, g, 1, 1)
                else:
                    wait(pe, x1_ok, g, 2, 1)
                for k in range(2):
                    t = 2 * n + k
                    for c in range(KC):
                        last = t_.matmul(ps_c[:, k * D:(k + 1) * D], oq[:, c, t * P:(t + 1) * P], wT[:, 3, c, :], start=(c == 0), stop=(c == KC - 1))
                last.then_inc(proj_ready, 1)

            def mix2(g, par, n):
                if g is None:
                    return
                if n == 0:
                    wait(pe, bd2_ok, g, 1, 1)
                    wait(pe, x1_ok, g, 2, 2)
                else:
                    wait(pe, h_copied, g, 2, 1)
                for k in range(2):
                    t = 2 * n + k
                    last = t_.matmul(ps_c[:, k * D:(k + 1) * D], bd2[par][:, t, :, :].rearrange("p b d -> p (b d)"),
                                     X[:, bass.ds(g * TG + t, 1), :].rearrange("p o d -> p (o d)"), start=True, stop=True)
                last.then_inc(h_ready, 1)

            def transpose_h(g, n):
                if g is None:
                    return
                if n == 0:
                    wait(pe, h_copied, g, 2, 2)
                else:
                    wait(pe, hT_copied, g, 2, 1)
                for k in range(2):
                    for c in range(KC):
                        last = t_.transpose(ps_c[:, (c * 2 + k) * P:(c * 2 + k + 1) * P], hrow[:, 2 * n + k, 0, c * P:(c + 1) * P], ident[:, :])
                last.then_inc(hT_ready, 1)

            def router(g):
                if g is None:
                    return
                if isinstance(g, int) and g == 0:
                    pe.wait_ge(rw_in, 16)
                wait(pe, hT_copied, g, 2, 2)
                for c in range(KC):
                    last = t_.matmul(ps_c[0:E, :], rw[:, c, :], hT[:, c, :], start=(c == 0), stop=(c == KC - 1))
                last.then_inc(scT_ready, 1)
                wait(pe, scT_copied, g, 1, 1)
                stand(pe)
                for t in range(TG):
                    last = t_.transpose(ps_c[:, t * E:(t + 1) * E], scT[:, t * P:(t + 1) * P], ident[0:E, 0:E])
                last.then_inc(rt_ready, 1)

            def rank(g):
                if g is None:
                    return
                wait(pe, both_ok, g, 1, 1)
                m = both[:, :, :].rearrange("p t e -> p (t e)")
                for k in range(1, TG):
                    t_.matmul(ps_c[:, k * E:TG * E], ones_b[:, :], m[:, 0:(TG - k) * E], start=(k == 1), stop=False, skip_group_check=True)
                t_.matmul(ps_c[:, 0:TG * E], before[:, :], m, start=False, stop=True, skip_group_check=True)
                for k in range(TG):
                    last = t_.matmul(ps_c[:, TG * E:(TG + 1) * E], ones_b[:, :], m[:, k * E:(k + 1) * E], start=(k == 0), stop=(k == TG - 1), skip_group_check=True)
                last.then_inc(rank_ready, 1)

            def iteration(a, b, c, par):
                scores(b, 1 - par, 0)
                mix1(a, par, 0)
                scores(b, 1 - par, 1)
                mix1(a, par, 1)
                transpose_q(c, q2[par], q2_ok, ps_c, rank_used, 1, 1, oqT_ready)
                transpose_p(b, 0)
                project_o(c, 0)
                transpose_q(a, q1, q1_ok, ps_a, y_copied, 2, 0, xqT_ready)
                attend(b, 1 - par, 0)
                scores(b, 1 - par, 2)
                transpose_p(b, 1)
                project_o(c, 1)
                spread_s(a)
                attend(b, 1 - par, 1)
                scores(b, 1 - par, 3)
                project_qk(a, 0)
                mix2(c, par, 0)
                transpose_p(b, 2)
                project_qk(a, 1)
                mix2(c, par, 1)
                attend(b, 1 - par, 2)
                project_v(a, 0)
                project_v(a, 1)
                transpose_h(c, 0)
                transpose_p(b, 3)
                transpose_h(c, 1)
                attend(b, 1 - par, 3)
                router(c)
                rank(c)

            pipeline(pe, iteration)

            pe.wait_ge(gu_in, 64)
            pe.wait_ge(dw_in, 16)
            pe.wait_ge(table_ok, 1)

            def step(k, j, i):
                if not (isinstance(k, int) and k >= EXPERT_TILES):
                    pe.wait_ge(xe_in[j], 16 * i + 16)
                    since(pe, xeT_copied, k, 2)
                    for c in range(KC):
                        last = t_.transpose(bank[j % 2][:, c * P:(c + 1) * P], xe[j][:, c * P:(c + 1) * P], ident[:, :])
                    last.then_inc(xeT_ready, 1)
                if not (isinstance(k, int) and not 1 <= k <= EXPERT_TILES):
                    n = (j + 1) % 2
                    e = pe.value_load(table[0:1, 0, bass.ds(k - 1, 1)], min_val=0, max_val=E - 1)
                    since(pe, xeT_copied, k, 1)
                    since(pe, hh_ok, k, 3)
                    for c in range(KC):
                        last = t_.matmul(bank[2 + n][:, 0:2 * F], xeT[n][:, c, :], gu[:, c, bass.ds(e, 1), :].rearrange("p o f -> p (o f)"), start=(c == 0), stop=(c == KC - 1))
                    last.then_inc(gu_ready, 1)
                if not (isinstance(k, int) and not 2 <= k <= EXPERT_TILES + 1):
                    n = j % 2
                    since(pe, hh_ok, k, 2)
                    since(pe, hhT_copied, k, 4)
                    t_.transpose(bank[4 + n][0:F, 0:P], hh[n], ident[:, :]).then_inc(hhT_ready, 1)
                if not (isinstance(k, int) and k < 3):
                    n = (j + 1) % 2
                    e = pe.value_load(table[0:1, 0, bass.ds(k - 3, 1)], min_val=0, max_val=E - 1)
                    since(pe, hhT_copied, k, 3)
                    since(pe, ye_copied, k, 5)
                    t_.matmul(bank[6 + n][:, 0:D], hhT[n], dw[:, bass.ds(e, 1), :].rearrange("p o d -> p (o d)"), start=True, stop=True).then_inc(ye_ready, 1)

            tiles(pe, step)


_INS = ["x", "itok_B_0_7", "itok_B_1_198", "L0_cond_weights", "L0_attn_wq", "L0_attn_wk", "L0_attn_wv", "L0_attn_wp",
        "L0_cond2_weights", "L0_ffn_router_w", "L0_ffn_gate_w", "L0_ffn_up_w", "L0_ffn_down_w"]


def kernel(**inputs):
    import numpy as _np
    import concourse.bacc as _bacc
    from concourse.bass_utils import run_bass_kernel_spmd as _run

    nc = _bacc.Bacc("TRN2", target_bir_lowering=False, num_devices=1)
    arrays, args = {}, []
    for name in _INS:
        a = _np.ascontiguousarray(inputs[name])
        arrays[f"in_{name}"] = a
        args.append(nc.dram_tensor(f"in_{name}", a.shape, mybir.dt.from_np(a.dtype), kind="ExternalInput").ap())
    args.append(nc.dram_tensor("out_x", (BATCH, SEQ, D), fp32, kind="ExternalOutput").ap())
    build(nc, *args)
    r = _run(nc, [arrays], core_ids=[0])
    return r.results[0]["out_x"]
```

```python
import concourse.bass as bass
from concourse import mybir
from contextlib import ExitStack

P = 128
BATCH, SEQ, D = 128, 32, 256
TOKENS = BATCH * SEQ
TILES = TOKENS // P
TG = 4
GROUPS = TILES // TG
GT = TG * P
BT = P // SEQ
KC = D // P
H, HD = 16, 16
HC = P // HD
VW = HD + 1
SLOTS = 4
E, F, TOPK = 16, 96, 2
ROW = D + 2
PITCH = TOKENS + P
EXPERT_TILES = (TOKENS * TOPK + E * (P - 1)) // P + 1
TURNS = EXPERT_TILES // 4 + 1
PADS = 16
EPS = 1e-5
MAGIC = 1.5 * 2.0 ** 23
QMAX = 127.0
NEG = -1e30
Y_ROWS = TOKENS * TOPK

fp32 = mybir.dt.float32
bf16 = mybir.dt.bfloat16
i32 = mybir.dt.int32
u32 = mybir.dt.uint32
ALU = mybir.AluOpType
ACT = mybir.ActivationFunctionType
AX = mybir.AxisListType


def build(nc, x, sub, cond, w_mix1, wq, wk, wv, wp, w_mix2, w_router, w_gate, w_up, w_down, out):
    with ExitStack() as ctx:
        build_in(ctx, nc, x, sub, cond, w_mix1, wq, wk, wv, wp, w_mix2, w_router, w_gate, w_up, w_down, out)


def build_in(ctx, nc, x, sub, cond, w_mix1, wq, wk, wv, wp, w_mix2, w_router, w_gate, w_up, w_down, out):
    def sb(name, shape, dt=fp32):
        return ctx.enter_context(nc.sbuf_tensor(name, shape, dt))

    def sem(name):
        return ctx.enter_context(nc.semaphore(name))

    mix_d = [nc.dram_tensor(f"mix{i}_d", [BATCH, SEQ * SEQ], fp32, kind="Internal").ap() for i in range(2)]
    v_d = nc.dram_tensor("v_d", [GT, H * VW], fp32, kind="Internal").ap()
    routed = nc.dram_tensor("routed", [E * PITCH, ROW], fp32, kind="Internal").ap()
    y_d = nc.dram_tensor("y_d", [Y_ROWS, D], fp32, kind="Internal").ap()

    X = sb("X", [P, TILES, D])
    arena = sb("arena", [P, 2 * KC * HC * GT])
    KX_WORDS = KC * HC * GT
    kx = [arena[:, i * KX_WORDS:(i + 1) * KX_WORDS].rearrange("p (c h t) -> p c h t", c=KC, h=HC) for i in range(2)]
    vx = sb("vx", [P, TG * BT, SLOTS, SLOTS * VW])
    ids = sb("ids", [P, 2], i32)
    mix_rows = [arena[:, 0:1024], arena[:, 1024:2048]]
    mix = [sb(f"mix{i}", [P, TILES + TG, SEQ]) for i in range(2)]
    bd1 = [sb(f"bd1_{i}", [P, TG, BT, SEQ]) for i in range(2)]
    bd2 = [sb(f"bd2_{i}", [P, TG, BT, SEQ]) for i in range(2)]
    w_nat = arena[:, 2048:4096].rearrange("p (w o d) -> p w o d", w=4, o=KC)
    w_z = arena[:, 4096:6144].rearrange("p (w o d) -> p w o d", w=4, o=KC)
    w_q = arena[:, 6144:7168].bitcast(bf16).rearrange("p (w o d) -> p w o d", w=4, o=KC)
    wT = sb("wT", [P, 4, KC, D], bf16)
    wabs = sb("wabs", [P, 4])
    am = sb("am", [P, 4])
    am_eps = sb("am_eps", [P, 4])
    am_inv = sb("am_inv", [P, 4])
    c_qk = sb("c_qk", [P, 2])
    rw = sb("rw", [P, KC, E])

    ident = sb("ident", [P, P])
    ident_b = sb("ident_b", [P, P], bf16)
    ones = sb("ones", [P, P])
    ones_b = sb("ones_b", [P, P], bf16)
    before = sb("before", [P, P], bf16)
    causal = sb("causal", [P, SEQ])
    seen = sb("seen", [P, BT, SEQ])
    own = sb("own", [P, BT])
    half = sb("half", [P, 2, TG])
    expert_no = sb("expert_no", [P, E])

    cen = sb("cen", [P, 2, TG, D])
    o_sb = cen[:, 1]
    stats = sb("stats", [P, 2, TG, 6])
    mv = sb("mv", [P, 2, TG, 2])
    veps = sb("veps", [P, 2, TG])
    rstd = sb("rstd", [P, 2, TG])
    amax = sb("amax", [P, 2, TG])
    inv = sb("inv", [P, 2, TG])
    mul = sb("mul", [P, 2, TG])
    nmean = sb("nmean", [P, 2, TG])
    step_of = sb("step_of", [P, 2, TG])
    s1 = step_of[:, 0, :]
    s_qk = [sb(f"s_qk{i}", [P, TG]) for i in range(2)]
    s_v = sb("s_v", [P, TG])
    s_p = sb("s_p", [P, TG])
    qn = sb("qn", [P, 2, TG, D], bf16)
    diag = sb("diag", [P, TG, P])
    xq = sb("xq", [P, KC, GT], bf16)
    oq = sb("oq", [P, KC, GT], bf16)
    s_row = sb("s_row", [P, GT])
    qT = [sb(f"qT{i}", [P, KC, GT]) for i in range(2)]
    kT = sb("kT", [P, KC, GT])
    v_sb = sb("v_sb", [P, TG, H, VW])
    sc = [sb(f"sc{i}", [P, H, SEQ]) for i in range(2)]
    mx = [sb(f"mx{i}", [P, H]) for i in range(2)]
    pr = [sb(f"pr{i}", [P, SLOTS, SLOTS, SEQ]) for i in range(2)]
    pT = [sb(f"pT{i}", [P, SLOTS, P]) for i in range(2)]
    rs = sb("rs", [P, H])
    hrow = sb("hrow", [P, TG, TOPK, ROW])
    hT = sb("hT", [P, KC, GT])
    scT = sb("scT", [E, GT])
    rmax = sb("rmax", [P, TG])
    rsub = sb("rsub", [P, TG, E])
    rexp = sb("rexp", [P, TG, E])
    top = sb("top", [P, TG, 8])
    topi = sb("topi", [P, TG, 8], u32)
    topf = sb("topf", [P, TG, TOPK])
    hot = sb("hot", [P, TG, TOPK, E])
    both = sb("both", [P, TG, E], bf16)
    den = sb("den", [P, TG])
    deni = sb("deni", [P, TG])
    dest = sb("dest", [P, TG, TOPK])
    filled = sb("filled", [P, E])
    pos = sb("pos", [P, TG, E])
    posh = sb("posh", [P, TG, TOPK, E])
    posf = sb("posf", [P, TG, TOPK])
    posi = sb("posi", [P, TG, TOPK], i32)

    GU_WORDS, DW_WORDS, PAD_WORDS = KC * E * 2 * F, E * D, PADS * ROW
    gu = arena[:, 0:GU_WORDS].rearrange("p (c e f) -> p c e f", c=KC, e=E)
    dw = arena[0:F, GU_WORDS:GU_WORDS + DW_WORDS].rearrange("p (e d) -> p e d", e=E)
    PAD_AT = GU_WORDS + DW_WORDS
    pad = arena[:, PAD_AT:PAD_AT + PAD_WORDS].rearrange("p (k r) -> p k r", r=ROW)
    FIN_WORDS = TG * TOPK * D
    fin = [arena[:, PAD_AT + i * FIN_WORDS:PAD_AT + (i + 1) * FIN_WORDS].rearrange("p (t k d) -> p t k d", t=TG, k=TOPK) for i in range(2)]
    xe = [hrow[:, i, 0, :] for i in range(4)]
    xeT = [qT[0][:, i, 0:D].rearrange("p (c t) -> p c t", c=KC) for i in range(2)]
    sg = [kT[:, 0, i * F:(i + 1) * F] for i in range(2)]
    hh = [kT[:, 1, i * F:(i + 1) * F] for i in range(2)]
    hhT = [sc[i][:, :, :].rearrange("p h j -> p (h j)")[0:F, 0:P] for i in range(2)]
    ye = [cen[:, 0, i, :] for i in range(4)]
    di = sb("di", [P, 4], i32)
    eighth = sb("eighth", [P, E])
    pad_at = sb("pad_at", [P, 3])
    pad_no = sb("pad_no", [P, PADS])
    pad_i = sb("pad_i", [P, 1], i32)
    sel = sb("sel", [P, E])
    cnt = sb("cnt", [P, E])
    cum = [sb(f"cum{i}", [P, E // 2 + E]) for i in range(2)]
    tile_no = sb("tile_no", [P, EXPERT_TILES])
    live = sb("live", [P, EXPERT_TILES])
    kp = sb("kp", [P, EXPERT_TILES])
    past = arena[:, PAD_AT + PAD_WORDS:PAD_AT + PAD_WORDS + EXPERT_TILES * E].rearrange("p (k e) -> p k e", e=E)
    ek = sb("ek", [P, 2, TURNS * 4 + 4])
    first_row = sb("first_row", [P, EXPERT_TILES], i32)
    expert_of = sb("expert_of", [P, TURNS, 2, 4], i32)

    bank = [ctx.enter_context(nc.psum_tensor(f"bank{i}", [P, 512], fp32)) for i in range(8)]
    ps_a, ps_q, ps_k, ps_pt, ps_o, ps_c = bank[0], bank[1], bank[2], bank[5], bank[6], bank[7]
    ps_s = [bank[3], bank[4]]

    ids_in, mixed_in, w_in, rw_in = sem("ids_in"), sem("mixed_in"), sem("w_in"), sem("rw_in")
    mix_got, mix_put, mix_in = [sem("mix_got0"), sem("mix_got1")], sem("mix_put"), sem("mix_in")
    x_in = [sem("x_in0"), sem("x_in1")]
    const_ok, zero0_ok, zero1_ok, vones_ok = sem("const_ok"), sem("zero0_ok"), sem("zero1_ok"), sem("vones_ok")
    wabs_ok, am_sum, am_ok, wT_ps, wT_ok = [sem(n) for n in ("wabs_ok", "am_sum", "am_ok", "wT_ps", "wT_ok")]
    bd1_ok, bd2_ok = sem("bd1_ok"), sem("bd2_ok")
    y_ready, var_ok, rstd_ok, centred, s1_ok, z1_ok, z2_ok, q1_ok, q2_ok = [sem(n) for n in ("y_ready", "var_ok", "rstd_ok", "centred", "s1_ok", "z1_ok", "z2_ok", "q1_ok", "q2_ok")]
    diag_ok, xqT_ready, xqT_copied, srow_ready, srow_copied = [sem(n) for n in ("diag_ok", "xqT_ready", "xqT_copied", "srow_ready", "srow_copied")]
    q_ready, q_copied, k_ready, k_scaled, v_ready, v_copied = [sem(n) for n in ("q_ready", "q_copied", "k_ready", "k_scaled", "v_ready", "v_copied")]
    kx_in, v_put, vx_in = sem("kx_in"), sem("v_put"), sem("vx_in")
    sc_ready, sc_scaled, mx_ok, sub_ok, exp_ok = [sem(n) for n in ("sc_ready", "sc_scaled", "mx_ok", "sub_ok", "exp_ok")]
    pT_ready, pT_copied, o_ready, o_ok = [sem(n) for n in ("pT_ready", "pT_copied", "o_ready", "o_ok")]
    oqT_ready, oqT_copied, proj_ready, x1_ok, h_ready, h_copied = [sem(n) for n in ("oqT_ready", "oqT_copied", "proj_ready", "x1_ok", "h_ready", "h_copied")]
    hT_ready, hT_copied, scT_ready, scT_copied, rt_ready, rsub_ok, rexp_ok, both_ok, rank_ready, rank_used, pos_ok, scattered = [
        sem(n) for n in ("hT_ready", "hT_copied", "scT_ready", "scT_copied", "rt_ready", "rsub_ok", "rexp_ok", "both_ok", "rank_ready", "rank_used", "pos_ok", "scattered")]

    gu_in, dw_in, pad_ok, padi_ok, padded, table_ok = [sem(n) for n in ("gu_in", "dw_in", "pad_ok", "padi_ok", "padded", "table_ok")]
    xe_in = [sem(f"xe_in{i}") for i in range(4)]
    y_put = [sem(f"y_put{i}") for i in range(4)]
    xeT_ready, xeT_copied, gu_ready, silu_ok, hh_ok, hhT_ready, hhT_copied, ye_ready, ye_copied = [
        sem(n) for n in ("xeT_ready", "xeT_copied", "gu_ready", "silu_ok", "hh_ok", "hhT_ready", "hhT_copied", "ye_ready", "ye_copied")]
    fin_in = [sem("fin_in0"), sem("fin_in1")]
    passed = sem("passed")
    pair_ok, fin_ok, out_put = sem("pair_ok"), sem("fin_ok"), sem("out_put")

    def wait(eng, s, g, per_group, nth, lag=0):
        if isinstance(g, int) and g < lag:
            return
        eng.wait_ge(s, (g - lag) * per_group + nth)

    def pipeline(eng, iteration):
        iteration(0, 0, None, None, None, 0)
        iteration(1, 1, 0, None, None, 1)
        iteration(2, 2, 1, 0, None, 0)
        iteration(3, 3, 2, 1, 0, 1)
        with eng.Fori(2, GROUPS // 2) as i:
            iteration(2 * i, 2 * i, 2 * i - 1, 2 * i - 2, 2 * i - 3, 0)
            iteration(2 * i + 1, 2 * i + 1, 2 * i, 2 * i - 1, 2 * i - 2, 1)
        iteration(GROUPS, None, GROUPS - 1, GROUPS - 2, GROUPS - 3, 0)
        iteration(GROUPS + 1, None, None, GROUPS - 1, GROUPS - 2, 1)
        iteration(GROUPS + 2, None, None, None, GROUPS - 1, 0)

    def both_of(a, c):
        if a is None and c is None:
            return None
        return slice(0 if a is not None else 1, 2 if c is not None else 1)

    def stand(eng):
        eng.sem_inc(passed, 1)

    def since(eng, s, k, ago, first=1):
        if isinstance(k, int) and k < ago:
            return
        eng.wait_ge(s, k - ago + first)

    def tiles(eng, step, begin=None):
        for i in range(2):
            got = begin(i) if begin else None
            for j in range(4):
                step(4 * i + j, j, i, got)
        with eng.Fori(2, EXPERT_TILES // 4) as i:
            got = begin(i) if begin else None
            for j in range(4):
                step(4 * i + j, j, i, got)
        got = begin(EXPERT_TILES // 4) if begin else None
        for k in range(EXPERT_TILES, EXPERT_TILES + 3):
            step(k, k % 4, k // 4, got)

    def registers(eng, name, n, i):
        turn = i if isinstance(i, int) else "n"
        return [eng.alloc_register(f"{name}{m}_{turn}") for m in range(n)]

    def groups(eng, step):
        step(0, 0)
        step(1, 1)
        with eng.Fori(1, GROUPS // 2) as i:
            step(2 * i, 0)
            step(2 * i + 1, 1)

    def slot_in(eng, s, g, par):
        eng.wait_ge(s, (g - par) * 8 + 16)

    out_v = out.rearrange("(t b) s d -> (b s) t d", b=BT)
    y_v = y_d.rearrange("(t p k) d -> p t k d", p=P, k=TOPK)

    x_v = x.rearrange("(t b) s d -> (b s) t d", b=BT)
    v_rows = v_d.rearrange("(t p) r -> p t r", p=P)
    v_slots = v_d.rearrange("(n j) (s r) -> s j n r", j=SEQ, s=SLOTS)

    with nc.Block() as block:

        @block.sync
        def _(sp):
            sp.dma_start(ids[:, 0:1], sub.unsqueeze(1)).then_inc(ids_in, 16)
            sp.dma_start(ids[:, 1:2], cond.unsqueeze(1)).then_inc(ids_in, 16)
            for i, w in enumerate((wq, wk, wv, wp)):
                sp.dma_start(w_nat[:, i], w.rearrange("(o p) d -> p o d", p=P)).then_inc(w_in, 16)
            for g in range(2):
                sp.dma_start(X[:, g * TG:(g + 1) * TG, :], x_v[:, g * TG:(g + 1) * TG, :]).then_inc(x_in[g], 16)
            for i in range(2):
                sp.wait_ge(mix_got[i], 16)
                sp.dma_start(mix_d[i], mix_rows[i]).then_inc(mix_put, 16)
                sp.wait_ge(mix_put, 16 * (i + 1))
                if i == 0:
                    sp.wait_ge(const_ok, 1)
                sp.dma_start(mix[i][:, 0:TILES, :], mix_d[i].rearrange("b (c d) -> (b c) d", d=SEQ).rearrange("(t p) d -> p t d", p=P)).then_inc(mix_in, 16)
            sp.dma_start(rw[:, :, :], w_router.rearrange("(c p) e -> p c e", p=P)).then_inc(rw_in, 16)

            def spread_k(g, par):
                if g is None:
                    return
                wait(sp, k_scaled, g, 2, 2)
                wait(sp, sc_ready, g, TG, TG, lag=2)
                if isinstance(g, int) and g < 2:
                    sp.wait_ge((zero0_ok, zero1_ok)[g], 1)
                for h in range(HC):
                    rows = slice(h * HD, (h + 1) * HD)
                    sp.dma_start(kx[par][rows, :, h, :], kT[rows, :, :]).then_inc(kx_in, 16)

            def spread_v(g):
                if g is None:
                    return
                wait(sp, v_copied, g, 2, 2)
                wait(sp, vx_in, g, 16 * SLOTS, 16 * SLOTS, lag=1)
                sp.dma_start(v_rows, v_sb[:, :, :, :].rearrange("p t h r -> p t (h r)")).then_inc(v_put, 16)
                wait(sp, v_put, g, 16, 16)
                wait(sp, o_ready, g, TG, TG, lag=1)
                for s in range(SLOTS):
                    sp.dma_start(vx[s * SEQ:(s + 1) * SEQ, :, s, :], v_slots[s]).then_inc(vx_in, 16)

            def iteration(it, a, b, c, d, par):
                spread_k(a, par)
                spread_v(a)

            for g in range(2, GROUPS):
                sp.wait_ge(x_in[g % 2], (g // 2) * 16)
                sp.dma_start(X[:, g * TG:(g + 1) * TG, :], x_v[:, g * TG:(g + 1) * TG, :]).then_inc(x_in[g % 2], 16)
            pipeline(sp, iteration)
            sp.wait_ge(sc_ready, TILES - TG)
            for half_, w in enumerate((w_gate, w_up)):
                for c in range(KC):
                    sp.dma_start(gu[:, c, :, half_ * F:(half_ + 1) * F], w[:, c * P:(c + 1) * P, :].rearrange("e p f -> p e f")).then_inc(gu_in, 16)
            sp.wait_ge(sc_ready, TILES)
            sp.dma_start(dw, w_down.rearrange("e f d -> f e d")).then_inc(dw_in, 16)
            sp.wait_ge(scattered, 16 * TOPK * TILES)
            sp.wait_ge(padded, 16)
            sp.wait_ge(table_ok, 1)

            def first_rows(i):
                if isinstance(i, int) and i >= EXPERT_TILES // 4:
                    return None
                rows = registers(sp, "row", 4, i)
                sp.load(rows, first_row[0:1, bass.ds(4 * i, 4)])
                return [sp.snap(r, donate=True, min_val=0, max_val=E * PITCH - P) for r in rows]

            def load_rows(k, j, i, row):
                if isinstance(k, int) and k >= EXPERT_TILES:
                    return
                since(sp, hh_ok, k, 4)
                sp.dma_start(xe[j], routed[bass.ds(row[j], P), :]).then_inc(xe_in[j], 16)

            tiles(sp, load_rows, first_rows)
            for j in range(4):
                sp.wait_ge(y_put[j], 16 * (EXPERT_TILES // 4))

            def load_pair(g, par):
                wait(sp, fin_ok, g, 1, 1, lag=2)
                sp.dma_start(fin[par], y_v[:, bass.ds(g * TG, TG), :, :]).then_inc(fin_in[par], 16)

            load_pair(0, 0)
            load_pair(1, 1)
            with sp.Fori(1, GROUPS // 2) as i:
                load_pair(2 * i, 0)
                load_pair(2 * i + 1, 1)
            sp.wait_ge(out_put, 16 * GROUPS)

        @block.gpsimd
        def _(pool):
            g_ = nc.gpsimd
            g_.iota(pad_no[:, :], [[1, PADS]], base=Y_ROWS, channel_multiplier=0, allow_small_or_imprecise_dtypes=True)
            g_.iota(pad_at[:, 0:1], [[0, 1]], base=0, channel_multiplier=PADS, allow_small_or_imprecise_dtypes=True)
            g_.iota(tile_no[:, :], [[1, EXPERT_TILES]], base=0, channel_multiplier=0, allow_small_or_imprecise_dtypes=True)
            g_.memset(cum[0][:, :], 0.0)
            g_.memset(cum[1][:, :], 0.0)
            for t_, v_ in ((eighth, 1.0), (ek, 0.0), (ident, 0.0), (ones, 1.0), (ones_b, 1.0), (before, 1.0), (seen, 1.0), (own, 1.0), (half, -0.5), (v_sb, 1.0), (mix[0], 0.0)):
                g_.memset(t_[tuple([slice(None)] * len(t_.shape))], v_)
            g_.iota(expert_no[:, :], [[1, E]], base=0, channel_multiplier=0, allow_small_or_imprecise_dtypes=True)
            g_.iota(filled[:, :], [[PITCH, E]], base=0, channel_multiplier=0, allow_small_or_imprecise_dtypes=True)
            g_.iota(dest[:, :, :], [[TOPK * P, TG], [1, TOPK]], base=-TOPK * GT, channel_multiplier=TOPK, allow_small_or_imprecise_dtypes=True)
            pool.wait_ge(ids_in, 32)
            for i, table in enumerate((w_mix1, w_mix2)):
                g_.indirect_dma_start(mix_rows[i], None, table.rearrange("s c d -> s (c d)"),
                                      bass.IndirectOffsetOnAxis(ap=ids[:, i:i + 1], axis=0)).then_inc(mix_got[i], 16)
            pool.drain()
            g_.affine_select(out=ident[:, :], in_=ident[:, :], compare_op=ALU.not_equal, fill=1.0, base=0, pattern=[[-1, P]], channel_multiplier=1)
            g_.affine_select(out=before[:, :], in_=before[:, :], compare_op=ALU.is_gt, fill=0.0, base=0, pattern=[[1, P]], channel_multiplier=-1)
            g_.affine_select(out=seen[:, :, :], in_=seen[:, :, :], compare_op=ALU.is_ge, fill=0.0, base=0, pattern=[[-SEQ, BT], [-1, SEQ]], channel_multiplier=1)
            g_.affine_select(out=own[:, :], in_=own[:, :], compare_op=ALU.is_ge, fill=0.0, base=0, pattern=[[-SEQ, BT]], channel_multiplier=1)
            g_.affine_select(out=eighth[:, :], in_=eighth[:, :], compare_op=ALU.is_ge, fill=0.0, base=0, pattern=[[-(P // E), E]], channel_multiplier=1)
            pool.drain()
            g_.affine_select(out=eighth[:, :], in_=eighth[:, :], compare_op=ALU.is_ge, fill=0.0, base=P // E - 1, pattern=[[P // E, E]], channel_multiplier=-1)
            g_.affine_select(out=own[:, :], in_=own[:, :], compare_op=ALU.is_ge, fill=0.0, base=SEQ - 1, pattern=[[SEQ, BT]], channel_multiplier=-1)
            pool.drain()
            g_.tensor_copy(ident_b[:, :], ident[:, :]).then_inc(const_ok, 1)
            pool.wait_ge(mix_in, 32)

            def spread(dst, i, g):
                src = mix[i][:, bass.ds(g * TG, TG), :].unsqueeze(2).to_broadcast([P, TG, BT, SEQ])
                return g_.tensor_tensor(dst[:, :, :, :], src, own[:, :].unsqueeze(1).unsqueeze(3).to_broadcast([P, TG, BT, SEQ]), ALU.mult)

            def spread1(g, par):
                if g is not None:
                    wait(pool, y_ready, g, 2, 2, lag=2)
                    spread(bd1[par], 0, g).then_inc(bd1_ok, 1)

            def spread2(g, par):
                if g is not None:
                    wait(pool, h_ready, g, 2, 2, lag=2)
                    spread(bd2[par], 1, g).then_inc(bd2_ok, 1)

            spread1(0, 0)
            pool.wait_ge(wT_ps, 1)
            pool.wait_ge(mix_put, 32)
            g_.memset(kx[0][:, :, :, :], 0.0)
            g_.memset(vx[:, :, :, :], 0.0).then_inc(zero0_ok, 1)

            def rstd_(it, which):
                if which is not None:
                    wait(pool, var_ok, it, 1, 1)
                    g_.tensor_tensor(rstd[:, which, :], veps[:, which, :], half[:, which, :], ALU.pow).then_inc(rstd_ok, 1)

            def diag_(g):
                if g is not None:
                    wait(pool, s1_ok, g, 1, 1)
                    wait(pool, srow_ready, g, 1, 1, lag=1)
                    g_.tensor_tensor(diag[:, :, :], ident[:, :].unsqueeze(1).to_broadcast([P, TG, P]),
                                     s1[:, :].unsqueeze(2).to_broadcast([P, TG, P]), ALU.mult).then_inc(diag_ok, 1)

            def sub_max(g, t):
                if g is not None:
                    wait(pool, mx_ok, g, TG, t + 1)
                    g_.tensor_tensor(sc[t % 2][:, :, :], sc[t % 2][:, :, :], mx[t % 2][:, :].unsqueeze(2).to_broadcast([P, H, SEQ]),
                                     ALU.subtract).then_inc(sub_ok, 1)

            def scatter(g, t):
                if g is not None:
                    if t == 0:
                        wait(pool, pos_ok, g, 1, 1)
                        wait(pool, h_copied, g, 2, 2)
                        stand(pool)
                    for k in range(TOPK):
                        g_.indirect_dma_start(routed, bass.IndirectOffsetOnAxis(ap=posi[:, t, k:k + 1], axis=0),
                                              hrow[:, t, k, :], None).then_inc(scattered, 16)

            def last_zeros(it):
                if isinstance(it, int) and it == 0:
                    g_.memset(kx[1][:, :, :, :], 0.0).then_inc(zero1_ok, 1)

            def next_spread1(a, par):
                if a is not None:
                    spread1(a + 1, 1 - par)

            def iteration(it, a, b, c, d, par):
                scatter(d, 0)
                rstd_(it, both_of(a, c))
                sub_max(b, 0)
                scatter(d, 1)
                diag_(a)
                spread2(c, par)
                scatter(d, 2)
                sub_max(b, 1)
                scatter(d, 3)
                next_spread1(a, par)
                sub_max(b, 2)
                sub_max(b, 3)
                last_zeros(it)

            pipeline(pool, iteration)

            pool.wait_ge(scattered, 16 * TOPK * TILES)
            g_.memset(pad[:, :, :], 0.0).then_inc(pad_ok, 1)
            pool.wait_ge(padi_ok, 1)
            g_.indirect_dma_start(routed, bass.IndirectOffsetOnAxis(ap=pad_i[:, 0:1], axis=0), pad.rearrange("p k r -> p (k r)"), None).then_inc(padded, 16)

            def put_rows(k, j, i, _):
                if isinstance(k, int) and k < 3:
                    return
                since(pool, ye_copied, k, 3)
                stand(pool)
                n = (j + 1) % 4
                g_.indirect_dma_start(y_d, bass.IndirectOffsetOnAxis(ap=di[:, n:n + 1], axis=0), ye[n], None,
                                      bounds_check=Y_ROWS - 1, oob_is_err=False).then_inc(y_put[n], 16)

            tiles(pool, put_rows)

            def add_pair(g, par):
                slot_in(pool, fin_in[par], g, par)
                g_.tensor_tensor(fin[par][:, :, 0, :], fin[par][:, :, 0, :], fin[par][:, :, 1, :], ALU.add).then_inc(pair_ok, 1)

            groups(pool, add_pair)

        @block.scalar
        def _(act):
            a_ = nc.scalar

            act.wait_ge(wT_ps, 1)
            for i in range(2):
                a_.activation(wT[:, 2 * i:2 * i + 2, :, :], bank[i][:, :].bitcast(bf16).rearrange("p (w c o) -> p w c o", w=2, c=KC), ACT.Copy).then_inc(wT_ok, 1)

            def centre(it, a):
                if a is None:
                    return
                wait(act, var_ok, it, 1, 1)
                wait(act, z1_ok, a, 1, 1, lag=1)
                for t in range(TG):
                    last = a_.activation(cen[:, 0, t, :], (ps_q, ps_k)[t // 2][:, (t % 2) * D:(t % 2 + 1) * D], ACT.Identity, bias=nmean[:, 0, t:t + 1])
                last.then_inc(centred, 1)

            def whole(g, n, z_ok, read, done):
                if g is None:
                    return
                wait(act, z_ok, g, 1, 1)
                wait(act, read, g, 1, 1, lag=1)
                a_.activation(qn[:, n, :, :], cen[:, n, :, :], ACT.Copy, bias=-MAGIC).then_inc(done, 1)

            def copy_T(g, ready, dst, src, free, per, done):
                if g is None:
                    return
                wait(act, ready, g, 1, 1)
                wait(act, free, g, per, per, lag=1)
                a_.activation(dst[:, :, :], src[:, :].bitcast(bf16).rearrange("p (c t) -> p c t", c=KC), ACT.Copy).then_inc(done, 1)

            def copy_srow(g):
                if g is None:
                    return
                wait(act, srow_ready, g, 1, 1)
                wait(act, k_scaled, g, 2, 2, lag=1)
                a_.activation(s_row[:, :], ps_a[:, :], ACT.Copy).then_inc(srow_copied, 1)

            def copy_q(g, par, cc):
                if g is None:
                    return
                wait(act, q_ready, g, 2, cc + 1)
                wait(act, sc_ready, g, TG, TG, lag=2)
                a_.activation(qT[par][:, cc, :], ps_q[:, :], ACT.Copy).then_inc(q_copied, 1)

            def copy_v(g, n):
                if g is None:
                    return
                wait(act, v_ready, g, 2, n + 1)
                wait(act, s1_ok, g, 1, 1)
                wait(act, v_put, g, 16, 16, lag=1)
                src = (ps_q, ps_k)[n]
                for k in range(2):
                    t = 2 * n + k
                    last = a_.activation(v_sb[:, t, :, 0:HD], src[:, k * D:(k + 1) * D].rearrange("p (h r) -> p h r", h=H), ACT.Copy, scale=s_v[:, t:t + 1])
                last.then_inc(v_copied, 1)

            def exp_(g, t):
                if g is None:
                    return
                wait(act, sub_ok, g, TG, t + 1)
                if t >= 2:
                    wait(act, pT_ready, g, TG, t - 1)
                else:
                    wait(act, pT_ready, g, TG, TG + t - 1, lag=1)
                a_.activation(pr[t % 2][:, :, :, :].rearrange("p c s j -> p s c j"),
                              sc[t % 2][:, :, :].rearrange("p (s c) j -> p s c j", c=SLOTS), ACT.Exp).then_inc(exp_ok, 1)

            def copy_pT(g, t):
                if g is None:
                    return
                wait(act, pT_ready, g, TG, t + 1)
                if t >= 2:
                    wait(act, o_ready, g, TG, t - 1)
                else:
                    wait(act, o_ready, g, TG, TG + t - 1, lag=1)
                a_.activation(pT[t % 2][:, :, :], ps_pt[:, :].rearrange("p (c i) -> p c i", c=SLOTS), ACT.Copy).then_inc(pT_copied, 1)

            def copy_h(g, n):
                if g is None:
                    return
                wait(act, h_ready, g, 2, n + 1)
                wait(act, scattered, g, 16 * TG * TOPK, 16 * TG * TOPK, lag=1)
                for k in range(TOPK):
                    last = a_.activation(hrow[:, 2 * n:2 * n + 2, k, 0:D], ps_c[:, :].rearrange("p (t d) -> p t d", t=2), ACT.Copy)
                last.then_inc(h_copied, 1)

            def copy_hT(g, n):
                if g is None:
                    return
                wait(act, hT_ready, g, 2, n + 1)
                wait(act, scT_ready, g, 1, 1, lag=1)
                a_.activation(hT[:, :, 2 * n * P:(2 * n + 2) * P], ps_c[:, :].rearrange("p (c t) -> p c t", c=KC), ACT.Copy).then_inc(hT_copied, 1)

            def copy_scT(g):
                if g is None:
                    return
                wait(act, scT_ready, g, 1, 1)
                wait(act, rt_ready, g, 1, 1, lag=1)
                a_.activation(scT[:, :], ps_c[0:E, :], ACT.Copy).then_inc(scT_copied, 1)

            def exp_router(g):
                if g is None:
                    return
                wait(act, rsub_ok, g, 1, 1)
                a_.activation(rexp[:, :, :], rsub[:, :, :], ACT.Exp).then_inc(rexp_ok, 1)

            def iteration(it, a, b, c, d, par):
                centre(it, a)
                exp_(b, 0)
                copy_pT(b, 0)
                whole(a, 0, z1_ok, xqT_ready, q1_ok)
                whole(c, 1, z2_ok, oqT_ready, q2_ok)
                copy_T(a, xqT_ready, xq, ps_a, v_ready, 2, xqT_copied)
                copy_T(c, oqT_ready, oq, ps_c, proj_ready, 2, oqT_copied)
                exp_(b, 1)
                copy_srow(a)
                copy_q(a, par, 0)
                copy_h(c, 0)
                exp_(b, 2)
                copy_pT(b, 1)
                copy_h(c, 1)
                copy_pT(b, 2)
                copy_hT(c, 0)
                exp_(b, 3)
                copy_q(a, par, 1)
                copy_hT(c, 1)
                copy_pT(b, 3)
                copy_scT(c)
                exp_router(c)
                copy_v(a, 0)
                copy_v(a, 1)

            pipeline(act, iteration)

            def step(k, j, i, _):
                if not (isinstance(k, int) and k >= EXPERT_TILES):
                    since(act, xeT_ready, k, 0)
                    since(act, gu_ready, k, 2)
                    a_.activation(xeT[j % 2], bank[j % 2][:, 0:D].rearrange("p (c t) -> p c t", c=KC), ACT.Copy).then_inc(xeT_copied, 1)
                if not (isinstance(k, int) and not 1 <= k <= EXPERT_TILES):
                    n = (j + 1) % 2
                    since(act, gu_ready, k, 1)
                    since(act, hh_ok, k, 3)
                    a_.activation(sg[n], bank[2 + n][:, 0:F], ACT.Silu).then_inc(silu_ok, 1)
                if not (isinstance(k, int) and k < 3):
                    n = (j + 1) % 4
                    since(act, ye_ready, k, 3)
                    if not (isinstance(k, int) and k < 7):
                        act.wait_ge(y_put[n], 16 * (i - 1 if n != 0 else i) if not isinstance(k, int) else 16 * ((k - 3) // 4))
                    a_.activation(ye[n], bank[6 + n % 2][:, 0:D], ACT.Copy).then_inc(ye_copied, 1)

            tiles(act, step)

            def put_out(g, par):
                wait(act, fin_ok, g, 1, 1)
                act.dma_start(out_v[:, bass.ds(g * TG, TG), :], X[:, bass.ds(g * TG, TG), :]).then_inc(out_put, 16)

            groups(act, put_out)

        @block.vector
        def _(dve):
            v = nc.vector

            dve.wait_ge(w_in, 64)
            v.tensor_reduce(wabs[:, :], w_nat[:, :, :, :], AX.XY, ALU.add, apply_absolute_value=True).then_inc(wabs_ok, 1)
            dve.wait_ge(am_sum, 1)
            v.tensor_scalar(am[:, :], bank[0][:, 0:4], 1.0 / (D * D), None, ALU.mult)
            v.tensor_scalar(am_eps[:, :], bank[0][:, 0:4], 1.0 / (D * D), EPS, ALU.mult, ALU.add)
            dve.drain()
            v.reciprocal(am_inv[:, :], am_eps[:, :])
            v.tensor_scalar(c_qk[:, 0:1], am[:, 0:1], am[:, 1:2], HD ** -0.5, ALU.mult, ALU.mult)
            dve.drain()
            for i in range(4):
                v.tensor_scalar(w_z[:, i], w_nat[:, i], am_inv[:, i:i + 1], MAGIC, ALU.mult, ALU.add)
            dve.drain()
            v.tensor_scalar(w_z[:, :, :, :], w_z[:, :, :, :], MAGIC, 1.0, ALU.subtract, ALU.min)
            dve.drain()
            v.tensor_scalar(w_q[:, :, :, :], w_z[:, :, :, :], -1.0, None, ALU.max).then_inc(am_ok, 1)
            dve.wait_ge(const_ok, 1)
            v.tensor_tensor(seen[:, :, :], seen[:, :, :], own[:, :].unsqueeze(2).to_broadcast([P, BT, SEQ]), ALU.mult)
            dve.drain()
            v.tensor_reduce(causal[:, :], seen[:, :, :].rearrange("p b j -> p j b"), AX.X, ALU.add)
            dve.drain()
            v.tensor_scalar(causal[:, :], causal[:, :], 1.0, -NEG, ALU.subtract, ALU.mult)

            def stats1(g, n):
                if g is None:
                    return
                wait(dve, y_ready, g, 2, n + 1)
                for t in (2 * n, 2 * n + 1):
                    v.bn_stats(stats[:, 0, t, :], (ps_q, ps_k)[n][:, (t % 2) * D:(t % 2 + 1) * D])

            def moments(it, a, c):
                which = both_of(a, c)
                if which is None:
                    return
                dve.drain()
                for n in range(which.start, which.stop):
                    for t in range(TG):
                        v.bn_aggr(mv[:, n, t, :], stats[:, n, t, :])
                dve.drain()
                v.tensor_scalar(nmean[:, which, :], mv[:, which, :, 0], -1.0, None, ALU.mult)
                v.tensor_scalar(veps[:, which, :], mv[:, which, :, 1], EPS, None, ALU.add).then_inc(var_ok, 1)
                if c is not None:
                    for t in range(TG):
                        v.tensor_scalar(cen[:, 1, t, :], cen[:, 1, t, :], mv[:, 1, t, 0:1], None, ALU.subtract)

            def quantise(it, a, c, par):
                which = both_of(a, c)
                if which is None:
                    return
                if a is not None:
                    wait(dve, centred, a, 1, 1)
                    wait(dve, diag_ok, a, 1, 1, lag=1)
                    wait(dve, v_copied, a, 2, 2, lag=1)
                    stand(dve)
                dve.drain()
                v.tensor_reduce(amax[:, which, :], cen[:, which, :, :], AX.X, ALU.max, apply_absolute_value=True)
                wait(dve, rstd_ok, it, 1, 1)
                stand(dve)
                dve.drain()
                v.tensor_tensor(amax[:, which, :], amax[:, which, :], rstd[:, which, :], ALU.mult)
                dve.drain()
                v.tensor_scalar(step_of[:, which, :], amax[:, which, :], 1e-5, 1.0 / QMAX, ALU.max, ALU.mult)
                dve.drain()
                v.reciprocal(inv[:, which, :], step_of[:, which, :])
                if c is not None:
                    v.tensor_scalar(s_p[:, :], step_of[:, 1, :], am[:, 3:4], None, ALU.mult)
                if a is not None:
                    v.tensor_scalar(s_qk[par][:, :], s1, c_qk[:, 0:1], None, ALU.mult)
                    v.tensor_scalar(s_v[:, :], s1, am[:, 2:3], None, ALU.mult).then_inc(s1_ok, 1)
                dve.drain()
                v.tensor_tensor(mul[:, which, :], inv[:, which, :], rstd[:, which, :], ALU.mult)
                dve.drain()
                for n in range(which.start, which.stop):
                    for t in range(TG):
                        last = v.tensor_scalar(cen[:, n, t, :], cen[:, n, t, :], mul[:, n, t:t + 1], MAGIC, ALU.mult, ALU.add)
                    last.then_inc((z1_ok, z2_ok)[n], 1)

            def scale_k(g, cc):
                if g is None:
                    return
                wait(dve, k_ready, g, 2, cc + 1)
                wait(dve, srow_copied, g, 1, 1)
                wait(dve, kx_in, g, 16 * HC, 16 * HC, lag=1)
                v.tensor_tensor(kT[:, cc, :], ps_k[:, :], s_row[:, :], ALU.mult).then_inc(k_scaled, 1)

            def scale_scores(g, par, t):
                if g is None:
                    return
                wait(dve, sc_ready, g, TG, t + 1)
                if t >= 2:
                    wait(dve, exp_ok, g, TG, t - 1)
                else:
                    wait(dve, exp_ok, g, TG, TG + t - 1, lag=1)
                v.scalar_tensor_tensor(out=sc[t % 2][:, :, :], in0=ps_s[t % 2][:, :].rearrange("p (h j) -> p h j", j=SEQ), scalar=s_qk[par][:, t:t + 1],
                                       in1=causal[:, :].unsqueeze(1).to_broadcast([P, H, SEQ]), op0=ALU.mult, op1=ALU.add).then_inc(sc_scaled, 1)
                dve.drain()
                v.tensor_reduce(mx[t % 2][:, :], sc[t % 2][:, :, :], AX.X, ALU.max).then_inc(mx_ok, 1)

            def norm_o(g, t):
                if g is None:
                    return
                wait(dve, o_ready, g, TG, t + 1)
                if t == 0:
                    wait(dve, q2_ok, g, 1, 1, lag=1)
                    if not (isinstance(g, int) and g < 1):
                        stand(dve)
                o = ps_o[:, 0:H * VW].rearrange("p (h r) -> p h r", r=VW)
                v.reciprocal(rs[:, :], o[:, :, HD])
                dve.drain()
                v.tensor_tensor(o_sb[:, t, :].rearrange("p (h r) -> p h r", r=HD), o[:, :, 0:HD], rs[:, :].unsqueeze(2).to_broadcast([P, H, HD]),
                                ALU.mult).then_inc(o_ok, 1)
                dve.drain()
                v.bn_stats(stats[:, 1, t, :], o_sb[:, t, :])

            def residual(g, n):
                if g is None:
                    return
                wait(dve, proj_ready, g, 2, n + 1)
                for k in range(2):
                    t = 2 * n + k
                    xt = X[:, bass.ds(g * TG + t, 1), :].rearrange("p o d -> p (o d)")
                    last = v.scalar_tensor_tensor(out=xt, in0=ps_c[:, k * D:(k + 1) * D], scalar=s_p[:, t:t + 1], in1=xt, op0=ALU.mult, op1=ALU.add)
                last.then_inc(x1_ok, 1)

            def route(g):
                if g is None:
                    return
                wait(dve, rt_ready, g, 1, 1)
                logits = ps_c[:, 0:TG * E].rearrange("p (t e) -> p t e", e=E)
                v.tensor_reduce(rmax[:, :], logits, AX.X, ALU.max)
                dve.drain()
                v.tensor_tensor(rsub[:, :, :], logits, rmax[:, :].unsqueeze(2).to_broadcast([P, TG, E]), ALU.subtract).then_inc(rsub_ok, 1)

            def choose(g):
                if g is None:
                    return
                wait(dve, rexp_ok, g, 1, 1)
                v.tensor_scalar(dest[:, :, :], dest[:, :, :], float(TOPK * GT), None, ALU.add)
                for t in range(TG):
                    v.max(top[:, t, :], rexp[:, t, :])
                dve.drain()
                for t in range(TG):
                    v.max_index(topi[:, t, :], top[:, t, :], rexp[:, t, :])
                v.tensor_tensor(den[:, :], top[:, :, 0], top[:, :, 1], ALU.add)
                dve.drain()
                v.tensor_copy(topf[:, :, :], topi[:, :, 0:TOPK])
                v.reciprocal(deni[:, :], den[:, :])
                dve.drain()
                v.tensor_tensor(hot[:, :, :, :], expert_no[:, :].unsqueeze(1).unsqueeze(1).to_broadcast([P, TG, TOPK, E]),
                                topf[:, :, :].unsqueeze(3).to_broadcast([P, TG, TOPK, E]), ALU.is_equal)
                wait(dve, scattered, g, 16 * TG * TOPK, 16 * TG * TOPK, lag=1)
                v.tensor_tensor(hrow[:, :, :, D + 1], top[:, :, 0:TOPK], deni[:, :].unsqueeze(2).to_broadcast([P, TG, TOPK]), ALU.mult)
                v.tensor_copy(hrow[:, :, :, D], dest[:, :, :])
                dve.drain()
                v.tensor_tensor(both[:, :, :], hot[:, :, 0, :], hot[:, :, 1, :], ALU.add).then_inc(both_ok, 1)

            def place(g):
                if g is None:
                    return
                wait(dve, rank_ready, g, 1, 1)
                v.tensor_tensor(pos[:, :, :], ps_a[:, 0:TG * E].rearrange("p (t e) -> p t e", e=E),
                                filled[:, :].unsqueeze(1).to_broadcast([P, TG, E]), ALU.add)
                dve.drain()
                v.tensor_tensor(filled[:, :], filled[:, :], ps_a[:, TG * E:(TG + 1) * E], ALU.add).then_inc(rank_used, 1)
                v.tensor_tensor(posh[:, :, :, :], hot[:, :, :, :], pos[:, :, :].unsqueeze(2).to_broadcast([P, TG, TOPK, E]), ALU.mult)
                dve.drain()
                v.tensor_reduce(posf[:, :, :], posh[:, :, :, :], AX.X, ALU.add)
                dve.drain()
                v.tensor_copy(posi[:, :, :], posf[:, :, :]).then_inc(pos_ok, 1)

            def iteration(it, a, b, c, d, par):
                stats1(a, 0)
                place(d)
                stats1(a, 1)
                moments(it, a, c)
                scale_scores(b, 1 - par, 0)
                quantise(it, a, c, par)
                scale_scores(b, 1 - par, 1)
                scale_scores(b, 1 - par, 2)
                residual(c, 0)
                residual(c, 1)
                scale_k(a, 0)
                scale_scores(b, 1 - par, 3)
                norm_o(b, 0)
                scale_k(a, 1)
                norm_o(b, 1)
                norm_o(b, 2)
                route(c)
                norm_o(b, 3)
                choose(c)

            pipeline(dve, iteration)

            dve.drain()
            v.tensor_tensor(sel[:, :], eighth[:, :], filled[:, :], ALU.mult)
            v.tensor_scalar(cnt[:, :], expert_no[:, :], -float(PITCH), None, ALU.mult)
            dve.drain()
            v.tensor_reduce(pad_at[:, 1:2], sel[:, :], AX.X, ALU.add)
            v.tensor_tensor(cnt[:, :], cnt[:, :], filled[:, :], ALU.add)
            dve.drain()
            v.tensor_tensor(sel[:, :], eighth[:, :], expert_no[:, :], ALU.mult)
            v.tensor_scalar(cnt[:, :], cnt[:, :], float(P - 1), 1.0 / P, ALU.add, ALU.mult)
            dve.drain()
            v.tensor_reduce(pad_at[:, 2:3], sel[:, :], AX.X, ALU.add)
            v.tensor_scalar(cnt[:, :], cnt[:, :], 0.5 - 0.25 / P, MAGIC, ALU.subtract, ALU.add)
            dve.drain()
            v.tensor_scalar(pad_at[:, 2:3], pad_at[:, 2:3], -float(P), None, ALU.mult)
            v.tensor_scalar(cnt[:, :], cnt[:, :], MAGIC, None, ALU.subtract)
            dve.drain()
            v.tensor_tensor(pad_at[:, 0:1], pad_at[:, 0:1], pad_at[:, 2:3], ALU.add)
            v.tensor_copy(cum[0][:, E // 2:], cnt[:, :])
            dve.drain()
            v.tensor_tensor(pad_at[:, 1:2], pad_at[:, 1:2], pad_at[:, 0:1], ALU.add)
            dve.wait_ge(pad_ok, 1)
            v.tensor_scalar(pad[:, :, D], pad_no[:, :], pad_at[:, 0:1], None, ALU.add)
            for n, step_ in enumerate((1, 2, 4, 8)):
                v.tensor_tensor(cum[(n + 1) % 2][:, E // 2:], cum[n % 2][:, E // 2:], cum[n % 2][:, E // 2 - step_:E // 2 + E - step_], ALU.add)
                dve.drain()
                if n == 0:
                    v.tensor_copy(pad_i[:, :], pad_at[:, 1:2]).then_inc(padi_ok, 1)
            ends = cum[0][:, E // 2:]
            v.tensor_scalar(live[:, :], tile_no[:, :], ends[:, E - 1:E], None, ALU.is_lt)
            dve.drain()
            v.tensor_tensor(kp[:, :], tile_no[:, :], live[:, :], ALU.mult)
            v.tensor_scalar(live[:, :], live[:, :], -float(Y_ROWS), float(Y_ROWS), ALU.mult, ALU.add)
            dve.drain()
            v.tensor_tensor(past[:, :, :], kp[:, :].unsqueeze(2).to_broadcast([P, EXPERT_TILES, E]), ends.unsqueeze(1).to_broadcast([P, EXPERT_TILES, E]), ALU.is_ge)
            dve.drain()
            at = slice(4, 4 + EXPERT_TILES)
            v.tensor_reduce(ek[:, 0, at], past[:, :, :], AX.X, ALU.add)
            dve.drain()
            v.tensor_tensor(past[:, :, :], past[:, :, :], cnt[:, :].unsqueeze(1).to_broadcast([P, EXPERT_TILES, E]), ALU.mult)
            for n, ago in enumerate((1, 3)):
                v.tensor_copy(expert_of[:, :, n, :], ek[:, 0, 4 - ago:4 - ago + 4 * TURNS].rearrange("p (i j) -> p i j", j=4))
            dve.drain()
            v.tensor_reduce(ek[:, 1, at], past[:, :, :], AX.X, ALU.add)
            v.tensor_scalar(ek[:, 0, at], ek[:, 0, at], float(PITCH), None, ALU.mult)
            dve.drain()
            v.tensor_tensor(ek[:, 1, at], kp[:, :], ek[:, 1, at], ALU.subtract)
            dve.drain()
            v.scalar_tensor_tensor(out=first_row[:, :], in0=ek[:, 1, at], scalar=float(P), in1=ek[:, 0, at], op0=ALU.mult, op1=ALU.add).then_inc(table_ok, 1)

            def step(k, j, i, _):
                if not (isinstance(k, int) and not 1 <= k <= EXPERT_TILES):
                    n = (j + 3) % 4
                    since(dve, silu_ok, k, 1)
                    since(dve, hhT_ready, k, 3)
                    v.scalar_tensor_tensor(out=hh[n % 2], in0=sg[n % 2], scalar=xe[n][:, D + 1:D + 2], in1=bank[2 + n % 2][:, F:2 * F], op0=ALU.mult, op1=ALU.mult)
                    if isinstance(k, int):
                        if k >= 5:
                            dve.wait_ge(y_put[n], 16 * ((k - 1) // 4))
                    else:
                        dve.wait_ge(y_put[n], 16 * i if j else 16 * (i - 1))
                    v.tensor_scalar(di[:, n:n + 1], xe[n][:, D:D + 1], live[:, bass.ds(k - 1, 1)], None, ALU.add).then_inc(hh_ok, 1)
                if not (isinstance(k, int) and not 2 <= k <= EXPERT_TILES + 1):
                    n = j % 2
                    since(dve, hhT_ready, k, 2)
                    since(dve, ye_ready, k, 4)
                    v.tensor_copy(hhT[n], bank[4 + n][0:F, 0:P]).then_inc(hhT_copied, 1)

            tiles(dve, step)

            def add_x(g, par):
                wait(dve, pair_ok, g, 1, 1)
                xg = X[:, bass.ds(g * TG, TG), :]
                v.tensor_tensor(xg, xg, fin[par][:, :, 0, :], ALU.add).then_inc(fin_ok, 1)

            groups(dve, add_x)

        @block.tensor
        def _(pe):
            t_ = nc.tensor

            pe.wait_ge(wabs_ok, 1)
            pe.wait_ge(const_ok, 1)
            t_.matmul(bank[0][:, 0:4], ones[:, :], wabs[:, :], start=True, stop=True).then_inc(am_sum, 1)
            pe.wait_ge(am_ok, 1)
            for i in range(4):
                ps = bank[i // 2][:, :].bitcast(bf16).rearrange("p (w c o) -> p w c o", w=2, c=KC)
                for c in range(KC):
                    for o in range(KC):
                        last = t_.transpose(ps[:, i % 2, c, o * P:(o + 1) * P], w_q[:, i, o, c * P:(c + 1) * P], ident_b[:, :])
            last.then_inc(wT_ps, 1)
            pe.wait_ge(wT_ok, 2)

            def mix1(g, par, n):
                if g is None:
                    return
                if n == 0:
                    wait(pe, bd1_ok, g, 1, 1)
                    if isinstance(g, int):
                        pe.wait_ge(x_in[par], 16 * (g // 2 + 1))
                    else:
                        pe.wait_ge(x_in[par], (g - par) * 8 + 16)
                wait(pe, v_copied, g, 2, n + 1, lag=1)
                for k in range(2):
                    t = 2 * n + k
                    last = t_.matmul((ps_q, ps_k)[n][:, k * D:(k + 1) * D], bd1[par][:, t, :, :].rearrange("p b d -> p (b d)"),
                                     X[:, bass.ds(g * TG + t, 1), :].rearrange("p o d -> p (o d)"), start=True, stop=True)
                last.then_inc(y_ready, 1)

            def transpose_q(g, n, q_ok, dst, done):
                if g is None:
                    return
                wait(pe, q_ok, g, 1, 1)
                if n == 0:
                    wait(pe, srow_copied, g, 1, 1, lag=1)
                    wait(pe, rank_used, g, 1, 1, lag=3)
                else:
                    wait(pe, rsub_ok, g, 1, 1, lag=1)
                stand(pe)
                ps = dst[:, :].bitcast(bf16).rearrange("p (c t) -> p c t", c=KC)
                for t in range(TG):
                    for c in range(KC):
                        last = t_.transpose(ps[:, c, t * P:(t + 1) * P], qn[:, n, t, c * P:(c + 1) * P], ident_b[:, :])
                last.then_inc(done, 1)

            def spread_s(g):
                if g is None:
                    return
                wait(pe, diag_ok, g, 1, 1)
                wait(pe, xqT_copied, g, 1, 1)
                t_.matmul(ps_a[:, :], ones[:, :], diag[:, :, :].rearrange("p t q -> p (t q)"), start=True, stop=True).then_inc(srow_ready, 1)

            def project_T(g, w, cc, ps, done):
                for c in range(KC):
                    last = t_.matmul(ps[:, :], wT[:, w, c, cc * P:(cc + 1) * P], xq[:, c, :], start=(c == 0), stop=(c == KC - 1))
                last.then_inc(done, 1)

            def project_qk(g, cc):
                if g is None:
                    return
                wait(pe, xqT_copied, g, 1, 1)
                if cc == 0:
                    wait(pe, centred, g, 1, 1)
                else:
                    wait(pe, q_copied, g, 2, 1)
                project_T(g, 0, cc, ps_q, q_ready)
                if cc == 1:
                    wait(pe, k_scaled, g, 2, 1)
                project_T(g, 1, cc, ps_k, k_ready)

            def project_v(g, n):
                if g is None:
                    return
                if n == 0:
                    wait(pe, q_copied, g, 2, 2)
                else:
                    wait(pe, k_scaled, g, 2, 2)
                for k in range(2):
                    t = 2 * n + k
                    for c in range(KC):
                        last = t_.matmul((ps_q, ps_k)[n][:, k * D:(k + 1) * D], xq[:, c, t * P:(t + 1) * P], wT[:, 2, c, :], start=(c == 0), stop=(c == KC - 1))
                last.then_inc(v_ready, 1)

            def scores(g, par, t):
                if g is None:
                    return
                if t == 0:
                    wait(pe, kx_in, g, 16 * HC, 16 * HC)
                    wait(pe, q_copied, g, 2, 2)
                if t >= 2:
                    wait(pe, sc_scaled, g, TG, t - 1)
                else:
                    wait(pe, sc_scaled, g, TG, TG + t - 1, lag=1)
                for c in range(KC):
                    for b in range(BT):
                        cols = slice(t * P + b * SEQ, t * P + (b + 1) * SEQ)
                        last = t_.matmul(ps_s[t % 2][b * SEQ:(b + 1) * SEQ, c * HC * SEQ:(c + 1) * HC * SEQ], qT[par][:, c, cols], kx[par][:, c, :, cols],
                                         start=True, stop=True)
                last.then_inc(sc_ready, 1)

            def transpose_p(g, t):
                if g is None:
                    return
                wait(pe, exp_ok, g, TG, t + 1)
                if t > 0:
                    wait(pe, pT_copied, g, TG, t)
                else:
                    wait(pe, pT_copied, g, TG, TG, lag=1)
                for c in range(SLOTS):
                    last = t_.transpose(ps_pt[:, c * P:(c + 1) * P], pr[t % 2][:, c, :, :].rearrange("p s j -> p (s j)"), ident[:, :])
                last.then_inc(pT_ready, 1)

            def attend(g, par, t):
                if g is None:
                    return
                wait(pe, pT_copied, g, TG, t + 1)
                if t == 0:
                    wait(pe, vx_in, g, 16 * SLOTS, 16 * SLOTS)
                    wait(pe, o_ok, g, TG, TG, lag=1)
                else:
                    wait(pe, o_ok, g, TG, t)
                o = ps_o[:, 0:H * VW].rearrange("p (s c r) -> p s c r", s=SLOTS, c=SLOTS)
                for c in range(SLOTS):
                    for b in range(BT):
                        last = t_.matmul(o[b * SEQ:(b + 1) * SEQ, :, c, :], pT[t % 2][:, c, b * SEQ:(b + 1) * SEQ],
                                         vx[:, t * BT + b, :, c * VW:(c + 1) * VW], start=True, stop=True)
                last.then_inc(o_ready, 1)

            def project_o(g, n):
                if g is None:
                    return
                if n == 0:
                    wait(pe, oqT_copied, g, 1, 1)
                else:
                    wait(pe, x1_ok, g, 2, 1)
                for k in range(2):
                    t = 2 * n + k
                    for c in range(KC):
                        last = t_.matmul(ps_c[:, k * D:(k + 1) * D], oq[:, c, t * P:(t + 1) * P], wT[:, 3, c, :], start=(c == 0), stop=(c == KC - 1))
                last.then_inc(proj_ready, 1)

            def mix2(g, par, n):
                if g is None:
                    return
                if n == 0:
                    wait(pe, bd2_ok, g, 1, 1)
                    wait(pe, x1_ok, g, 2, 2)
                else:
                    wait(pe, h_copied, g, 2, 1)
                for k in range(2):
                    t = 2 * n + k
                    last = t_.matmul(ps_c[:, k * D:(k + 1) * D], bd2[par][:, t, :, :].rearrange("p b d -> p (b d)"),
                                     X[:, bass.ds(g * TG + t, 1), :].rearrange("p o d -> p (o d)"), start=True, stop=True)
                last.then_inc(h_ready, 1)

            def transpose_h(g, n):
                if g is None:
                    return
                if n == 0:
                    wait(pe, h_copied, g, 2, 2)
                else:
                    wait(pe, hT_copied, g, 2, 1)
                for k in range(2):
                    for c in range(KC):
                        last = t_.transpose(ps_c[:, (c * 2 + k) * P:(c * 2 + k + 1) * P], hrow[:, 2 * n + k, 0, c * P:(c + 1) * P], ident[:, :])
                last.then_inc(hT_ready, 1)

            def router(g):
                if g is None:
                    return
                if isinstance(g, int) and g == 0:
                    pe.wait_ge(rw_in, 16)
                wait(pe, hT_copied, g, 2, 2)
                for c in range(KC):
                    last = t_.matmul(ps_c[0:E, :], rw[:, c, :], hT[:, c, :], start=(c == 0), stop=(c == KC - 1))
                last.then_inc(scT_ready, 1)

            def logits(g):
                if g is None:
                    return
                wait(pe, scT_copied, g, 1, 1)
                stand(pe)
                for t in range(TG):
                    last = t_.transpose(ps_c[:, t * E:(t + 1) * E], scT[:, t * P:(t + 1) * P], ident[0:E, 0:E])
                last.then_inc(rt_ready, 1)

            def rank(g):
                if g is None:
                    return
                wait(pe, both_ok, g, 1, 1)
                if not isinstance(g, int):
                    wait(pe, srow_copied, g, 1, 3)
                else:
                    pe.wait_ge(srow_copied, min(g + 3, GROUPS))
                m = both[:, :, :].rearrange("p t e -> p (t e)")
                for k in range(1, TG):
                    t_.matmul(ps_a[:, k * E:TG * E], ones_b[:, :], m[:, 0:(TG - k) * E], start=(k == 1), stop=False, skip_group_check=True)
                t_.matmul(ps_a[:, 0:TG * E], before[:, :], m, start=False, stop=True, skip_group_check=True)
                for k in range(TG):
                    last = t_.matmul(ps_a[:, TG * E:(TG + 1) * E], ones_b[:, :], m[:, k * E:(k + 1) * E], start=(k == 0), stop=(k == TG - 1), skip_group_check=True)
                last.then_inc(rank_ready, 1)

            def iteration(it, a, b, c, d, par):
                mix1(a, par, 0)
                rank(d)
                mix1(a, par, 1)
                scores(b, 1 - par, 0)
                scores(b, 1 - par, 1)
                transpose_p(b, 0)
                scores(b, 1 - par, 2)
                attend(b, 1 - par, 0)
                transpose_q(a, 0, q1_ok, ps_a, xqT_ready)
                transpose_q(c, 1, q2_ok, ps_c, oqT_ready)
                project_qk(a, 0)
                project_o(c, 0)
                spread_s(a)
                project_o(c, 1)
                scores(b, 1 - par, 3)
                mix2(c, par, 0)
                transpose_p(b, 1)
                project_qk(a, 1)
                mix2(c, par, 1)
                attend(b, 1 - par, 1)
                transpose_p(b, 2)
                transpose_h(c, 0)
                attend(b, 1 - par, 2)
                transpose_h(c, 1)
                transpose_p(b, 3)
                router(c)
                attend(b, 1 - par, 3)
                logits(c)
                project_v(a, 0)
                project_v(a, 1)

            pipeline(pe, iteration)

            pe.wait_ge(gu_in, 64)
            pe.wait_ge(dw_in, 16)
            pe.wait_ge(table_ok, 1)

            def experts_of(i):
                experts = registers(pe, "expert", 8, i)
                pe.load(experts, expert_of[0:1, bass.ds(i, 1), :, :].rearrange("p o s j -> p (o s j)"))
                return [pe.snap(r, donate=True, min_val=0, max_val=E - 1) for r in experts]

            def step(k, j, i, expert):
                if not (isinstance(k, int) and k >= EXPERT_TILES):
                    pe.wait_ge(xe_in[j], 16 * i + 16)
                    since(pe, xeT_copied, k, 2)
                    for c in range(KC):
                        last = t_.transpose(bank[j % 2][:, c * P:(c + 1) * P], xe[j][:, c * P:(c + 1) * P], ident[:, :])
                    last.then_inc(xeT_ready, 1)
                if not (isinstance(k, int) and not 1 <= k <= EXPERT_TILES):
                    n = (j + 1) % 2
                    since(pe, xeT_copied, k, 1)
                    since(pe, hh_ok, k, 3)
                    for c in range(KC):
                        last = t_.matmul(bank[2 + n][:, 0:2 * F], xeT[n][:, c, :], gu[:, c, bass.ds(expert[j], 1), :].rearrange("p o f -> p (o f)"), start=(c == 0), stop=(c == KC - 1))
                    last.then_inc(gu_ready, 1)
                if not (isinstance(k, int) and not 2 <= k <= EXPERT_TILES + 1):
                    n = j % 2
                    since(pe, hh_ok, k, 2)
                    since(pe, hhT_copied, k, 4)
                    t_.transpose(bank[4 + n][0:F, 0:P], hh[n], ident[:, :]).then_inc(hhT_ready, 1)
                if not (isinstance(k, int) and k < 3):
                    n = (j + 1) % 2
                    since(pe, hhT_copied, k, 3)
                    since(pe, ye_copied, k, 5)
                    t_.matmul(bank[6 + n][:, 0:D], hhT[n], dw[:, bass.ds(expert[4 + j], 1), :].rearrange("p o d -> p (o d)"), start=True, stop=True).then_inc(ye_ready, 1)

            tiles(pe, step, experts_of)


_INS = ["x", "itok_B_0_7", "itok_B_1_198", "L0_cond_weights", "L0_attn_wq", "L0_attn_wk", "L0_attn_wv", "L0_attn_wp",
        "L0_cond2_weights", "L0_ffn_router_w", "L0_ffn_gate_w", "L0_ffn_up_w", "L0_ffn_down_w"]


def kernel(**inputs):
    import numpy as _np
    import concourse.bacc as _bacc
    from concourse.bass_utils import run_bass_kernel_spmd as _run

    nc = _bacc.Bacc("TRN2", target_bir_lowering=False, num_devices=1)
    arrays, args = {}, []
    for name in _INS:
        a = _np.ascontiguousarray(inputs[name])
        arrays[f"in_{name}"] = a
        args.append(nc.dram_tensor(f"in_{name}", a.shape, mybir.dt.from_np(a.dtype), kind="ExternalInput").ap())
    args.append(nc.dram_tensor("out_x", (BATCH, SEQ, D), fp32, kind="ExternalOutput").ap())
    build(nc, *args)
    r = _run(nc, [arrays], core_ids=[0])
    return r.results[0]["out_x"]
```

```python
import concourse.bass as bass
from concourse import mybir
from contextlib import ExitStack

P = 128
BATCH, SEQ, D = 128, 32, 256
TOKENS = BATCH * SEQ
TILES = TOKENS // P
TG = 4
GROUPS = TILES // TG
GT = TG * P
BT = P // SEQ
KC = D // P
H, HD = 16, 16
HC = P // HD
VW = HD + 1
SLOTS = 4
E, F, TOPK = 16, 96, 2
ROW = D + 2
PITCH = TOKENS + P
EXPERT_TILES = (TOKENS * TOPK + E * (P - 1)) // P + 1
LAG = 3
DEEP = 8
TF, FIN = 2, 4
PADS = 16
EPS = 1e-5
MAGIC = 1.5 * 2.0 ** 23
QMAX = 127.0
NEG = -1e30
Y_ROWS = TOKENS * TOPK

fp32 = mybir.dt.float32
bf16 = mybir.dt.bfloat16
i32 = mybir.dt.int32
u32 = mybir.dt.uint32
ALU = mybir.AluOpType
ACT = mybir.ActivationFunctionType
AX = mybir.AxisListType


def build(nc, x, sub, cond, w_mix1, wq, wk, wv, wp, w_mix2, w_router, w_gate, w_up, w_down, out):
    with ExitStack() as ctx:
        build_in(ctx, nc, x, sub, cond, w_mix1, wq, wk, wv, wp, w_mix2, w_router, w_gate, w_up, w_down, out)


def build_in(ctx, nc, x, sub, cond, w_mix1, wq, wk, wv, wp, w_mix2, w_router, w_gate, w_up, w_down, out):
    def sb(name, shape, dt=fp32):
        return ctx.enter_context(nc.sbuf_tensor(name, shape, dt))

    def sem(name):
        return ctx.enter_context(nc.semaphore(name))

    mix_d = [nc.dram_tensor(f"mix{i}_d", [BATCH, SEQ * SEQ], fp32, kind="Internal").ap() for i in range(2)]
    v_d = nc.dram_tensor("v_d", [GT, H * VW], fp32, kind="Internal").ap()
    routed = nc.dram_tensor("routed", [E * PITCH, ROW], fp32, kind="Internal").ap()
    y_d = nc.dram_tensor("y_d", [Y_ROWS, D], fp32, kind="Internal").ap()

    X = sb("X", [P, TILES, D])
    arena = sb("arena", [P, 2 * KC * HC * GT])
    KX_WORDS = KC * HC * GT
    kx = [arena[:, i * KX_WORDS:(i + 1) * KX_WORDS].rearrange("p (c h t) -> p c h t", c=KC, h=HC) for i in range(2)]
    vx = sb("vx", [P, TG * BT, SLOTS, SLOTS * VW])
    ids = sb("ids", [P, 2], i32)
    mix_rows = [arena[:, KX_WORDS:KX_WORDS + 1024], arena[:, KX_WORDS + 1024:KX_WORDS + 2048]]
    mix = [sb(f"mix{i}", [P, TILES + TG, SEQ]) for i in range(2)]
    bd1 = [sb(f"bd1_{i}", [P, TG, BT, SEQ]) for i in range(2)]
    bd2 = [sb(f"bd2_{i}", [P, TG, BT, SEQ]) for i in range(2)]
    w_nat = arena[:, KX_WORDS + 2048:KX_WORDS + 4096].rearrange("p (w o d) -> p w o d", w=4, o=KC)
    w_z = arena[:, KX_WORDS + 4096:KX_WORDS + 6144].rearrange("p (w o d) -> p w o d", w=4, o=KC)
    w_q = arena[:, KX_WORDS + 6144:KX_WORDS + 7168].bitcast(bf16).rearrange("p (w o d) -> p w o d", w=4, o=KC)
    wT = sb("wT", [P, 4, KC, D], bf16)
    wabs = sb("wabs", [P, 4])
    am = sb("am", [P, 4])
    am_eps = sb("am_eps", [P, 4])
    am_inv = sb("am_inv", [P, 4])
    c_qk = sb("c_qk", [P, 2])
    rw = sb("rw", [P, KC, E])

    ident = sb("ident", [P, P])
    ident_b = sb("ident_b", [P, P], bf16)
    ones = sb("ones", [P, P])
    ones_b = sb("ones_b", [P, P], bf16)
    before = sb("before", [P, P], bf16)
    causal = sb("causal", [P, SEQ])
    seen = sb("seen", [P, BT, SEQ])
    own = sb("own", [P, BT])
    half = sb("half", [P, 2, TG])
    expert_no = sb("expert_no", [P, E])

    cen = sb("cen", [P, 2, TG, D])
    o_sb = cen[:, 1]
    stats = sb("stats", [P, 2, TG, 6])
    mv = sb("mv", [P, 2, TG, 2])
    veps = sb("veps", [P, 2, TG])
    rstd = sb("rstd", [P, 2, TG])
    amax = sb("amax", [P, 2, TG])
    inv = sb("inv", [P, 2, TG])
    mul = sb("mul", [P, 2, TG])
    nmean = sb("nmean", [P, 2, TG])
    step_of = sb("step_of", [P, 2, TG])
    s1 = step_of[:, 0, :]
    s_qk = [sb(f"s_qk{i}", [P, TG]) for i in range(2)]
    s_v = sb("s_v", [P, TG])
    s_p = sb("s_p", [P, TG])
    qn = sb("qn", [P, 2, TG, D], bf16)
    diag = sb("diag", [P, TG, P])
    xq = sb("xq", [P, KC, GT], bf16)
    oq = sb("oq", [P, KC, GT], bf16)
    s_row = sb("s_row", [P, GT])
    qT = [sb(f"qT{i}", [P, KC, GT]) for i in range(2)]
    kT = sb("kT", [P, KC, GT])
    v_sb = sb("v_sb", [P, TG, H, VW])
    sc = [sb(f"sc{i}", [P, H, SEQ]) for i in range(2)]
    mx = [sb(f"mx{i}", [P, H]) for i in range(2)]
    pr = [sb(f"pr{i}", [P, SLOTS, SLOTS, SEQ]) for i in range(2)]
    pT = [sb(f"pT{i}", [P, SLOTS, P]) for i in range(2)]
    rs = sb("rs", [P, H])
    hrow = sb("hrow", [P, TG, TOPK, ROW])
    hT = sb("hT", [P, KC, GT])
    scT = sb("scT", [E, GT])
    rmax = sb("rmax", [P, TG])
    rsub = sb("rsub", [P, TG, E])
    rexp = sb("rexp", [P, TG, E])
    top = sb("top", [P, TG, 8])
    topi = sb("topi", [P, TG, 8], u32)
    topf = sb("topf", [P, TG, TOPK])
    hot = sb("hot", [P, TG, TOPK, E])
    both = sb("both", [P, TG, E], bf16)
    den = sb("den", [P, TG])
    deni = sb("deni", [P, TG])
    dest = sb("dest", [P, TG, TOPK])
    filled = sb("filled", [P, E])
    pos = sb("pos", [P, TG, E])
    posh = sb("posh", [P, TG, TOPK, E])
    posf = sb("posf", [P, TG, TOPK])
    posi = sb("posi", [P, TG, TOPK], i32)

    GU_WORDS, DW_WORDS, PAD_WORDS = KC * E * 2 * F, E * D, PADS * ROW
    gu = arena[:, 0:GU_WORDS].rearrange("p (c e f) -> p c e f", c=KC, e=E)
    dw = arena[0:F, GU_WORDS:GU_WORDS + DW_WORDS].rearrange("p (e d) -> p e d", e=E)
    PAD_AT = GU_WORDS + DW_WORDS
    pad = arena[:, PAD_AT:PAD_AT + PAD_WORDS].rearrange("p (k r) -> p k r", r=ROW)
    FIN_WORDS = TF * TOPK * D
    fin = [arena[:, PAD_AT + i * FIN_WORDS:PAD_AT + (i + 1) * FIN_WORDS].rearrange("p (t k d) -> p t k d", t=TF, k=TOPK) for i in range(FIN)]
    xe = [hrow[:, i // TOPK, i % TOPK, :] for i in range(DEEP)]
    xeT = [qT[0][:, i, 0:D].rearrange("p (c t) -> p c t", c=KC) for i in range(2)]
    sg = [kT[:, 0, i * F:(i + 1) * F] for i in range(2)]
    hh = [kT[:, 1, i * F:(i + 1) * F] for i in range(2)]
    hhT = [sc[i][:, :, :].rearrange("p h j -> p (h j)")[0:F, 0:P] for i in range(2)]
    ye = [cen[:, i // TG, i % TG, :] for i in range(DEEP)]
    di = sb("di", [P, DEEP], i32)
    eighth = sb("eighth", [P, E])
    pad_at = sb("pad_at", [P, 3])
    pad_no = sb("pad_no", [P, PADS])
    pad_i = sb("pad_i", [P, 1], i32)
    sel = sb("sel", [P, E])
    cnt = sb("cnt", [P, E])
    cum = [sb(f"cum{i}", [P, E // 2 + E]) for i in range(2)]
    tile_no = sb("tile_no", [P, EXPERT_TILES])
    live = sb("live", [P, EXPERT_TILES])
    kp = sb("kp", [P, EXPERT_TILES])
    past = arena[:, PAD_AT + PAD_WORDS:PAD_AT + PAD_WORDS + EXPERT_TILES * E].rearrange("p (k e) -> p k e", e=E)
    skip = vx[:, :, :, :].rearrange("p n s r -> p (n s r)")[:, 0:EXPERT_TILES * E].rearrange("p (k e) -> p k e", e=E)
    ek = sb("ek", [P, EXPERT_TILES])
    first_row = sb("first_row", [P, EXPERT_TILES], i32)
    expert_of = sb("expert_of", [P, EXPERT_TILES + DEEP], i32)

    bank = [ctx.enter_context(nc.psum_tensor(f"bank{i}", [P, 512], fp32)) for i in range(8)]
    ps_a, ps_q, ps_k, ps_pt, ps_o, ps_c = bank[0], bank[1], bank[2], bank[5], bank[6], bank[7]
    ps_s = [bank[3], bank[4]]
    ps_h = [ps_c, ps_a]

    ids_in, w_in, rw_in = sem("ids_in"), sem("w_in"), sem("rw_in")
    mix_got, mix_put, mix_in = [[sem(f"{n}{i}") for i in range(m)] for n, m in (("mix_got", 2), ("mix_put", 3), ("mix_in", 3))]
    x_in = [sem("x_in0"), sem("x_in1")]
    const_ok, mixz_ok, zero0_ok, zero1_ok = sem("const_ok"), sem("mixz_ok"), sem("zero0_ok"), sem("zero1_ok")
    wabs_ok, am_sum, am_ok, wT_ps, wT_ok = [sem(n) for n in ("wabs_ok", "am_sum", "am_ok", "wT_ps", "wT_ok")]
    bd1_ok, bd2_ok = sem("bd1_ok"), sem("bd2_ok")
    y_ready, var_ok, rstd_ok, centred, s1_ok, z1_ok, z2_ok, q1_ok, q2_ok = [sem(n) for n in ("y_ready", "var_ok", "rstd_ok", "centred", "s1_ok", "z1_ok", "z2_ok", "q1_ok", "q2_ok")]
    diag_ok, xqT_ready, xqT_copied, srow_ready, srow_copied = [sem(n) for n in ("diag_ok", "xqT_ready", "xqT_copied", "srow_ready", "srow_copied")]
    q_ready, q_copied, k_ready, k_scaled, v_ready, v_copied = [sem(n) for n in ("q_ready", "q_copied", "k_ready", "k_scaled", "v_ready", "v_copied")]
    kx_in, v_put, vx_in = sem("kx_in"), sem("v_put"), sem("vx_in")
    sc_ready, sc_scaled, mx_ok, sub_ok, exp_ok = [sem(n) for n in ("sc_ready", "sc_scaled", "mx_ok", "sub_ok", "exp_ok")]
    pT_ready, pT_copied, o_ready, o_ok = [sem(n) for n in ("pT_ready", "pT_copied", "o_ready", "o_ok")]
    oqT_ready, oqT_copied, proj_ready, x1_ok, h_ready, h_copied = [sem(n) for n in ("oqT_ready", "oqT_copied", "proj_ready", "x1_ok", "h_ready", "h_copied")]
    hT_ready, hT_copied, scT_ready, scT_copied, rt_ready, rsub_ok, rexp_ok, both_ok, rank_ready, rank_used, pos_ok, scattered = [
        sem(n) for n in ("hT_ready", "hT_copied", "scT_ready", "scT_copied", "rt_ready", "rsub_ok", "rexp_ok", "both_ok", "rank_ready", "rank_used", "pos_ok", "scattered")]

    gu_in, dw_in, pad_ok, padi_ok, padded, first_row_ok, expert_ok = [
        sem(n) for n in ("gu_in", "dw_in", "pad_ok", "padi_ok", "padded", "first_row_ok", "expert_ok")]
    xe_in = [sem(f"xe_in{i}") for i in range(DEEP)]
    y_put = [sem(f"y_put{i}") for i in range(DEEP)]
    xeT_ready, xeT_copied, gu_ready, silu_ok, hh_ok, hhT_ready, hhT_copied, ye_ready, ye_copied = [
        sem(n) for n in ("xeT_ready", "xeT_copied", "gu_ready", "silu_ok", "hh_ok", "hhT_ready", "hhT_copied", "ye_ready", "ye_copied")]
    fin_in = [sem(f"fin_in{i}") for i in range(FIN)]
    passed = sem("passed")
    pair_ok, fin_ok, out_put = sem("pair_ok"), sem("fin_ok"), sem("out_put")

    def wait(eng, s, g, per_group, nth, lag=0):
        if isinstance(g, int) and g < lag:
            return
        eng.wait_ge(s, (g - lag) * per_group + nth)

    def pipeline(eng, iteration, without_a, without_b):
        iteration(0, 0, None, None, None, 0)
        iteration(1, 1, 0, None, None, 1)
        iteration(2, 2, 1, 0, None, 0)
        iteration(3, 3, 2, 1, 0, 1)
        with eng.Fori(2, GROUPS // 2) as i:
            iteration(2 * i, 2 * i, 2 * i - 1, 2 * i - 2, 2 * i - 3, 0)
            iteration(2 * i + 1, 2 * i + 1, 2 * i, 2 * i - 1, 2 * i - 2, 1)
        without_a(GROUPS, None, GROUPS - 1, GROUPS - 2, GROUPS - 3, 0)
        without_b(GROUPS + 1, None, None, GROUPS - 1, GROUPS - 2, 1)
        without_b(GROUPS + 2, None, None, None, GROUPS - 1, 0)

    def both_of(a, c):
        if a is None and c is None:
            return None
        return slice(0 if a is not None else 1, 2 if c is not None else 1)

    def stand(eng):
        eng.sem_inc(passed, 1)

    def since(eng, s, k, ago, first=1):
        if isinstance(k, int) and k < ago:
            return
        eng.wait_ge(s, k - ago + first)

    def tiles(eng, step, begin=None):
        for i in range(2):
            got = begin(i) if begin else None
            for j in range(DEEP):
                step(DEEP * i + j, j, i, got)
        with eng.Fori(2, EXPERT_TILES // DEEP) as i:
            got = begin(i) if begin else None
            for j in range(DEEP):
                step(DEEP * i + j, j, i, got)
        got = begin(EXPERT_TILES // DEEP) if begin else None
        for k in range(EXPERT_TILES, EXPERT_TILES + LAG):
            step(k, k % DEEP, k // DEEP, got)

    def put_before(eng, j, i, ago):
        turn = i - 1 if j < ago else i
        if not (isinstance(turn, int) and turn < 1):
            eng.wait_ge(y_put[(j - ago) % DEEP], 16 * turn)

    def registers(eng, name, n, i):
        turn = i if isinstance(i, int) else "n"
        return [eng.alloc_register(f"{name}{m}_{turn}") for m in range(n)]

    def parts(eng, step):
        for j in range(FIN):
            step(j, j, 0)
        with eng.Fori(1, TILES // (TF * FIN)) as i:
            for j in range(FIN):
                step(FIN * i + j, j, i)

    out_v = out.rearrange("(t b) s d -> (b s) t d", b=BT)
    y_v = y_d.rearrange("(t p k) d -> p t k d", p=P, k=TOPK)

    x_v = x.rearrange("(t b) s d -> (b s) t d", b=BT)
    v_rows = v_d.rearrange("(t p) r -> p t r", p=P)
    v_slots = v_d.rearrange("(n j) (s r) -> s j n r", j=SEQ, s=SLOTS)

    with nc.Block() as block:

        @block.sync
        def _(sp):
            sp.dma_start(ids[:, 0:1], sub.unsqueeze(1)).then_inc(ids_in, 16)
            sp.dma_start(ids[:, 1:2], cond.unsqueeze(1)).then_inc(ids_in, 16)
            for i, w in enumerate((wq, wk, wv, wp)):
                sp.dma_start(w_nat[:, i], w.rearrange("(o p) d -> p o d", p=P)).then_inc(w_in, 16)

            def load_x(g):
                sp.dma_start(X[:, g * TG:(g + 1) * TG, :], x_v[:, g * TG:(g + 1) * TG, :]).then_inc(x_in[g % 2], 16)

            def regroup(i, t0, t1, part):
                put = mix_d[i][t0 * BT:t1 * BT, :]
                sp.dma_start(put, mix_rows[i][t0 * BT:t1 * BT, :]).then_inc(mix_put[part], 16)
                if part < 2:
                    load_x(part)
                sp.wait_ge(mix_put[part], 16)
                sp.dma_start(mix[i][:, t0:t1, :], put.rearrange("b (c d) -> (b c) d", d=SEQ).rearrange("(t p) d -> p t d", p=P)).then_inc(mix_in[part], 16)

            sp.wait_ge(mix_got[0], 16)
            sp.wait_ge(mixz_ok, 1)
            regroup(0, 0, TG, 0)
            regroup(0, TG, TILES, 1)
            sp.wait_ge(mix_got[1], 16)
            regroup(1, 0, TILES, 2)
            sp.dma_start(rw[:, :, :], w_router.rearrange("(c p) e -> p c e", p=P)).then_inc(rw_in, 16)

            def spread_k(g, par):
                if g is None:
                    return
                wait(sp, k_scaled, g, 2, 2)
                wait(sp, sc_ready, g, TG, TG, lag=2)
                if isinstance(g, int) and g < 2:
                    sp.wait_ge((zero0_ok, zero1_ok)[g], 1)
                for h in range(HC):
                    rows = slice(h * HD, (h + 1) * HD)
                    sp.dma_start(kx[par][rows, :, h, :], kT[rows, :, :]).then_inc(kx_in, 16)

            def spread_v(g):
                if g is None:
                    return
                wait(sp, v_copied, g, 2, 2)
                wait(sp, vx_in, g, 16 * SLOTS, 16 * SLOTS, lag=1)
                sp.dma_start(v_rows, v_sb[:, :, :, :].rearrange("p t h r -> p t (h r)")).then_inc(v_put, 16)
                wait(sp, v_put, g, 16, 16)
                wait(sp, o_ready, g, TG, TG, lag=1)
                for s in range(SLOTS):
                    sp.dma_start(vx[s * SEQ:(s + 1) * SEQ, :, s, :], v_slots[s]).then_inc(vx_in, 16)

            def iteration(it, a, b, c, d, par):
                spread_k(a, par)
                spread_v(a)

            for g in range(2, GROUPS):
                sp.wait_ge(x_in[g % 2], (g // 2) * 16)
                load_x(g)
            pipeline(sp, iteration, iteration, iteration)
            sp.wait_ge(sc_ready, TILES - TG)
            E_PIECE = E // 2
            pieces = [(half_, c, e) for half_ in range(2) for c in range(KC) for e in range(0, E, E_PIECE)]
            for n, (half_, c, e) in enumerate(pieces):
                if n:
                    sp.wait_ge(gu_in, 16 * n)
                sp.dma_start(gu[:, c, e:e + E_PIECE, half_ * F:(half_ + 1) * F],
                             (w_gate, w_up)[half_][e:e + E_PIECE, c * P:(c + 1) * P, :].rearrange("e p f -> p e f")).then_inc(gu_in, 16)
            sp.wait_ge(sc_ready, TILES)
            for n in range(2):
                if n:
                    sp.wait_ge(dw_in, 16 * n)
                sp.dma_start(dw[:, n * E_PIECE:(n + 1) * E_PIECE, :], w_down[n * E_PIECE:(n + 1) * E_PIECE].rearrange("e f d -> f e d")).then_inc(dw_in, 16)
            sp.wait_ge(first_row_ok, 1)

            def first_rows(i):
                if isinstance(i, int) and i >= EXPERT_TILES // DEEP:
                    return None
                rows = registers(sp, "row", DEEP, i)
                sp.load(rows, first_row[0:1, bass.ds(DEEP * i, DEEP)])
                if isinstance(i, int) and i == 0:
                    sp.wait_ge(scattered, 16 * TOPK * TILES)
                    sp.wait_ge(padded, 16)
                return [sp.snap(r, donate=True, min_val=0, max_val=E * PITCH - P) for r in rows]

            def load_rows(k, j, i, row):
                if isinstance(k, int) and k >= EXPERT_TILES:
                    return
                since(sp, hh_ok, k, DEEP)
                sp.dma_start(xe[j], routed[bass.ds(row[j], P), :]).then_inc(xe_in[j], 16)

            tiles(sp, load_rows, first_rows)
            for j in range(DEEP):
                sp.wait_ge(y_put[j], 16 * (EXPERT_TILES // DEEP))

            def load_pair(q, j, i):
                wait(sp, fin_ok, q, 1, 1, lag=FIN)
                sp.dma_start(fin[j], y_v[:, bass.ds(q * TF, TF), :, :]).then_inc(fin_in[j], 16)

            parts(sp, load_pair)
            sp.wait_ge(out_put, 16 * (TILES // TF))

        @block.gpsimd
        def _(pool):
            g_ = nc.gpsimd
            g_.iota(pad_no[:, :], [[1, PADS]], base=Y_ROWS, channel_multiplier=0, allow_small_or_imprecise_dtypes=True)
            g_.iota(pad_at[:, 0:1], [[0, 1]], base=0, channel_multiplier=PADS, allow_small_or_imprecise_dtypes=True)
            g_.iota(tile_no[:, :], [[1, EXPERT_TILES]], base=0, channel_multiplier=0, allow_small_or_imprecise_dtypes=True)
            g_.memset(cum[0][:, :], 0.0)
            g_.memset(cum[1][:, :], 0.0)
            for t_, v_ in ((eighth, 1.0), (expert_of, 0), (ident, 0.0), (ones, 1.0), (ones_b, 1.0), (before, 1.0), (seen, 1.0), (own, 1.0), (half, -0.5)):
                g_.memset(t_[tuple([slice(None)] * len(t_.shape))], v_)
            g_.iota(expert_no[:, :], [[1, E]], base=0, channel_multiplier=0, allow_small_or_imprecise_dtypes=True)
            g_.iota(filled[:, :], [[PITCH, E]], base=0, channel_multiplier=0, allow_small_or_imprecise_dtypes=True)
            g_.iota(dest[:, :, :], [[TOPK * P, TG], [1, TOPK]], base=-TOPK * GT, channel_multiplier=TOPK, allow_small_or_imprecise_dtypes=True)
            pool.drain()
            g_.affine_select(out=ident[:, :], in_=ident[:, :], compare_op=ALU.not_equal, fill=1.0, base=0, pattern=[[-1, P]], channel_multiplier=1)
            g_.affine_select(out=before[:, :], in_=before[:, :], compare_op=ALU.is_gt, fill=0.0, base=0, pattern=[[1, P]], channel_multiplier=-1)
            g_.affine_select(out=seen[:, :, :], in_=seen[:, :, :], compare_op=ALU.is_ge, fill=0.0, base=0, pattern=[[-SEQ, BT], [-1, SEQ]], channel_multiplier=1)
            g_.affine_select(out=own[:, :], in_=own[:, :], compare_op=ALU.is_ge, fill=0.0, base=0, pattern=[[-SEQ, BT]], channel_multiplier=1)
            g_.affine_select(out=eighth[:, :], in_=eighth[:, :], compare_op=ALU.is_ge, fill=0.0, base=0, pattern=[[-(P // E), E]], channel_multiplier=1)
            pool.drain()
            g_.affine_select(out=eighth[:, :], in_=eighth[:, :], compare_op=ALU.is_ge, fill=0.0, base=P // E - 1, pattern=[[P // E, E]], channel_multiplier=-1)
            g_.affine_select(out=own[:, :], in_=own[:, :], compare_op=ALU.is_ge, fill=0.0, base=SEQ - 1, pattern=[[SEQ, BT]], channel_multiplier=-1)
            pool.drain()
            g_.tensor_copy(ident_b[:, :], ident[:, :]).then_inc(const_ok, 1)
            pool.wait_ge(ids_in, 32)
            for i, table in enumerate((w_mix1, w_mix2)):
                g_.indirect_dma_start(mix_rows[i], None, table.rearrange("s c d -> s (c d)"),
                                      bass.IndirectOffsetOnAxis(ap=ids[:, i:i + 1], axis=0)).then_inc(mix_got[i], 16)
            g_.memset(mix[0][:, :, :], 0.0).then_inc(mixz_ok, 1)
            g_.memset(v_sb[:, :, :, :], 1.0)
            g_.memset(vx[:, :, :, :], 0.0)
            pool.wait_ge(mix_in[0], 16)

            def spread(dst, i, g):
                src = mix[i][:, bass.ds(g * TG, TG), :].unsqueeze(2).to_broadcast([P, TG, BT, SEQ])
                return g_.tensor_tensor(dst[:, :, :, :], src, own[:, :].unsqueeze(1).unsqueeze(3).to_broadcast([P, TG, BT, SEQ]), ALU.mult)

            def spread1(g, par):
                if g is not None:
                    wait(pool, y_ready, g, 2, 2, lag=2)
                    spread(bd1[par], 0, g).then_inc(bd1_ok, 1)

            def spread2(g, par):
                if g is not None:
                    if isinstance(g, int) and g == 0:
                        pool.wait_ge(mix_in[2], 16)
                    wait(pool, h_ready, g, 2, 2, lag=2)
                    spread(bd2[par], 1, g).then_inc(bd2_ok, 1)

            spread1(0, 0)
            g_.memset(kx[0][:, :, :, :], 0.0).then_inc(zero0_ok, 1)

            def rstd_(it, which):
                if which is not None:
                    wait(pool, var_ok, it, 1, 1)
                    g_.tensor_tensor(rstd[:, which, :], veps[:, which, :], half[:, which, :], ALU.pow).then_inc(rstd_ok, 1)

            def diag_(g):
                if g is not None:
                    wait(pool, s1_ok, g, 1, 1)
                    wait(pool, srow_ready, g, 1, 1, lag=1)
                    g_.tensor_tensor(diag[:, :, :], ident[:, :].unsqueeze(1).to_broadcast([P, TG, P]),
                                     s1[:, :].unsqueeze(2).to_broadcast([P, TG, P]), ALU.mult).then_inc(diag_ok, 1)

            def sub_max(g, t):
                if g is not None:
                    wait(pool, mx_ok, g, TG, t + 1)
                    g_.tensor_tensor(sc[t % 2][:, :, :], sc[t % 2][:, :, :], mx[t % 2][:, :].unsqueeze(2).to_broadcast([P, H, SEQ]),
                                     ALU.subtract).then_inc(sub_ok, 1)

            def scatter(g, t):
                if g is not None:
                    if t == 0:
                        wait(pool, pos_ok, g, 1, 1)
                        wait(pool, h_copied, g, 2, 2)
                        stand(pool)
                    for k in range(TOPK):
                        g_.indirect_dma_start(routed, bass.IndirectOffsetOnAxis(ap=posi[:, t, k:k + 1], axis=0),
                                              hrow[:, t, k, :], None).then_inc(scattered, 16)

            def last_zeros(it):
                if isinstance(it, int) and it == 0:
                    pool.wait_ge(wT_ps, 1)
                    for part in range(3):
                        pool.wait_ge(mix_put[part], 16)
                    g_.memset(kx[1][:, :, :, :], 0.0).then_inc(zero1_ok, 1)

            def zero_pad(it):
                if isinstance(it, int) and it == GROUPS + 2:
                    pool.wait_ge(sc_ready, TILES)
                    g_.memset(pad[:, :, :], 0.0).then_inc(pad_ok, 1)

            def put_pad(it):
                if isinstance(it, int) and it == GROUPS + 2:
                    pool.wait_ge(padi_ok, 1)
                    g_.indirect_dma_start(routed, bass.IndirectOffsetOnAxis(ap=pad_i[:, 0:1], axis=0), pad.rearrange("p k r -> p (k r)"), None).then_inc(padded, 16)

            def next_spread1(a, par):
                if a is not None:
                    if isinstance(a, int) and a == 0:
                        pool.wait_ge(mix_in[1], 16)
                    spread1(a + 1, 1 - par)

            def iteration(it, a, b, c, d, par):
                spread2(c, par)
                scatter(d, 0)
                rstd_(it, both_of(a, c))
                sub_max(b, 0)
                zero_pad(it)
                scatter(d, 1)
                diag_(a)
                next_spread1(a, par)
                put_pad(it)
                scatter(d, 2)
                sub_max(b, 1)
                scatter(d, 3)
                sub_max(b, 2)
                last_zeros(it)
                sub_max(b, 3)

            def without_a(it, a, b, c, d, par):
                scatter(d, 0)
                rstd_(it, both_of(a, c))
                sub_max(b, 0)
                scatter(d, 1)
                spread2(c, par)
                scatter(d, 2)
                scatter(d, 3)
                sub_max(b, 1)
                sub_max(b, 2)
                sub_max(b, 3)

            def without_b(it, a, b, c, d, par):
                zero_pad(it)
                scatter(d, 0)
                rstd_(it, both_of(a, c))
                put_pad(it)
                scatter(d, 1)
                scatter(d, 2)
                spread2(c, par)
                scatter(d, 3)

            pipeline(pool, iteration, without_a, without_b)

            def put_rows(k, j, i, _):
                if isinstance(k, int) and k < 3:
                    return
                since(pool, ye_copied, k, 3)
                stand(pool)
                n = (j - 3) % DEEP
                g_.indirect_dma_start(y_d, bass.IndirectOffsetOnAxis(ap=di[:, n:n + 1], axis=0), ye[n], None,
                                      bounds_check=Y_ROWS - 1, oob_is_err=False).then_inc(y_put[n], 16)

            tiles(pool, put_rows)

            def add_pair(q, j, i):
                pool.wait_ge(fin_in[j], 16 * i + 16)
                g_.tensor_tensor(fin[j][:, :, 0, :], fin[j][:, :, 0, :], fin[j][:, :, 1, :], ALU.add).then_inc(pair_ok, 1)

            parts(pool, add_pair)

        @block.scalar
        def _(act):
            a_ = nc.scalar

            act.wait_ge(wT_ps, 1)
            for i in range(2):
                a_.activation(wT[:, 2 * i:2 * i + 2, :, :], ps_s[i][:, :].bitcast(bf16).rearrange("p (w c o) -> p w c o", w=2, c=KC), ACT.Copy).then_inc(wT_ok, 1)

            def centre(it, a):
                if a is None:
                    return
                wait(act, var_ok, it, 1, 1)
                wait(act, z1_ok, a, 1, 1, lag=1)
                for t in range(TG):
                    last = a_.activation(cen[:, 0, t, :], (ps_q, ps_k)[t // 2][:, (t % 2) * D:(t % 2 + 1) * D], ACT.Identity, bias=nmean[:, 0, t:t + 1])
                last.then_inc(centred, 1)

            def whole(g, n, z_ok, read, done):
                if g is None:
                    return
                wait(act, z_ok, g, 1, 1)
                wait(act, read, g, 1, 1, lag=1)
                a_.activation(qn[:, n, :, :], cen[:, n, :, :], ACT.Copy, bias=-MAGIC).then_inc(done, 1)

            def copy_T(g, ready, dst, src, free, per, done):
                if g is None:
                    return
                wait(act, ready, g, 1, 1)
                wait(act, free, g, per, per, lag=1)
                a_.activation(dst[:, :, :], src[:, :].bitcast(bf16).rearrange("p (c t) -> p c t", c=KC), ACT.Copy).then_inc(done, 1)

            def copy_srow(g):
                if g is None:
                    return
                wait(act, srow_ready, g, 1, 1)
                wait(act, k_scaled, g, 2, 2, lag=1)
                a_.activation(s_row[:, :], ps_a[:, :], ACT.Copy).then_inc(srow_copied, 1)

            def copy_q(g, par, cc):
                if g is None:
                    return
                wait(act, q_ready, g, 2, cc + 1)
                wait(act, sc_ready, g, TG, TG, lag=2)
                a_.activation(qT[par][:, cc, :], ps_q[:, :], ACT.Copy).then_inc(q_copied, 1)

            def copy_v(g, n):
                if g is None:
                    return
                wait(act, v_ready, g, 2, n + 1)
                wait(act, s1_ok, g, 1, 1)
                wait(act, v_put, g, 16, 16, lag=1)
                src = (ps_q, ps_k)[n]
                for k in range(2):
                    t = 2 * n + k
                    last = a_.activation(v_sb[:, t, :, 0:HD], src[:, k * D:(k + 1) * D].rearrange("p (h r) -> p h r", h=H), ACT.Copy, scale=s_v[:, t:t + 1])
                last.then_inc(v_copied, 1)

            def exp_(g, t):
                if g is None:
                    return
                wait(act, sub_ok, g, TG, t + 1)
                if t >= 2:
                    wait(act, pT_ready, g, TG, t - 1)
                else:
                    wait(act, pT_ready, g, TG, TG + t - 1, lag=1)
                a_.activation(pr[t % 2][:, :, :, :].rearrange("p c s j -> p s c j"),
                              sc[t % 2][:, :, :].rearrange("p (s c) j -> p s c j", c=SLOTS), ACT.Exp).then_inc(exp_ok, 1)

            def copy_pT(g, t):
                if g is None:
                    return
                wait(act, pT_ready, g, TG, t + 1)
                if t >= 2:
                    wait(act, o_ready, g, TG, t - 1)
                else:
                    wait(act, o_ready, g, TG, TG + t - 1, lag=1)
                a_.activation(pT[t % 2][:, :, :], ps_pt[:, :].rearrange("p (c i) -> p c i", c=SLOTS), ACT.Copy).then_inc(pT_copied, 1)

            def copy_h(g, n):
                if g is None:
                    return
                wait(act, h_ready, g, 2, n + 1)
                wait(act, scattered, g, 16 * TG * TOPK, 16 * TG * TOPK, lag=1)
                for k in range(TOPK):
                    last = a_.activation(hrow[:, 2 * n:2 * n + 2, k, 0:D], ps_h[n][:, :].rearrange("p (t d) -> p t d", t=2), ACT.Copy)
                last.then_inc(h_copied, 1)

            def copy_hT(g, n):
                if g is None:
                    return
                wait(act, hT_ready, g, 2, n + 1)
                wait(act, scT_ready, g, 1, 1, lag=1)
                a_.activation(hT[:, :, 2 * n * P:(2 * n + 2) * P], ps_h[n][:, :].rearrange("p (c t) -> p c t", c=KC), ACT.Copy).then_inc(hT_copied, 1)

            def copy_scT(g):
                if g is None:
                    return
                wait(act, scT_ready, g, 1, 1)
                wait(act, rt_ready, g, 1, 1, lag=1)
                a_.activation(scT[:, :], ps_c[0:E, :], ACT.Copy).then_inc(scT_copied, 1)

            def exp_router(g):
                if g is None:
                    return
                wait(act, rsub_ok, g, 1, 1)
                a_.activation(rexp[:, :, :], rsub[:, :, :], ACT.Exp).then_inc(rexp_ok, 1)

            def iteration(it, a, b, c, d, par):
                centre(it, a)
                exp_(b, 0)
                copy_pT(b, 0)
                whole(a, 0, z1_ok, xqT_ready, q1_ok)
                whole(c, 1, z2_ok, oqT_ready, q2_ok)
                copy_T(a, xqT_ready, xq, ps_a, v_ready, 2, xqT_copied)
                copy_T(c, oqT_ready, oq, ps_c, proj_ready, 2, oqT_copied)
                exp_(b, 1)
                copy_srow(a)
                copy_pT(b, 1)
                exp_(b, 2)
                copy_q(a, par, 0)
                copy_h(c, 0)
                copy_h(c, 1)
                copy_pT(b, 2)
                copy_hT(c, 0)
                exp_(b, 3)
                copy_hT(c, 1)
                copy_scT(c)
                copy_q(a, par, 1)
                copy_pT(b, 3)
                exp_router(c)
                copy_v(a, 0)
                copy_v(a, 1)

            def without_a(it, a, b, c, d, par):
                exp_(b, 0)
                whole(c, 1, z2_ok, oqT_ready, q2_ok)
                copy_T(c, oqT_ready, oq, ps_c, proj_ready, 2, oqT_copied)
                copy_pT(b, 0)
                exp_(b, 1)
                exp_(b, 2)
                copy_pT(b, 1)
                copy_h(c, 0)
                copy_h(c, 1)
                copy_pT(b, 2)
                copy_hT(c, 0)
                copy_hT(c, 1)
                exp_(b, 3)
                copy_scT(c)
                copy_pT(b, 3)
                exp_router(c)

            def without_b(it, a, b, c, d, par):
                whole(c, 1, z2_ok, oqT_ready, q2_ok)
                copy_T(c, oqT_ready, oq, ps_c, proj_ready, 2, oqT_copied)
                copy_h(c, 0)
                copy_h(c, 1)
                copy_hT(c, 0)
                copy_hT(c, 1)
                copy_scT(c)
                exp_router(c)

            pipeline(act, iteration, without_a, without_b)

            act.wait_ge(both_ok, GROUPS)
            a_.activation(rsub[:, 0, 0:1], rsub[:, 0, 0:1], ACT.Silu)
            def step(k, j, i, _):
                if not (isinstance(k, int) and k >= EXPERT_TILES):
                    since(act, xeT_ready, k, 0)
                    since(act, gu_ready, k, 2)
                    a_.activation(xeT[j % 2], bank[j % 2][:, 0:D].rearrange("p (c t) -> p c t", c=KC), ACT.Copy).then_inc(xeT_copied, 1)
                if not (isinstance(k, int) and not 1 <= k <= EXPERT_TILES):
                    n = (j + 1) % 2
                    since(act, gu_ready, k, 1)
                    since(act, hh_ok, k, 3)
                    a_.activation(sg[n], bank[2 + n][:, 0:F], ACT.Silu).then_inc(silu_ok, 1)
                if not (isinstance(k, int) and k < 3):
                    n = (j - 3) % DEEP
                    since(act, ye_ready, k, 3)
                    put_before(act, j, i, 3)
                    a_.activation(ye[n], bank[6 + n % 2][:, 0:D], ACT.Copy).then_inc(ye_copied, 1)

            tiles(act, step)

            def put_out(q, j, i):
                wait(act, fin_ok, q, 1, 1)
                act.dma_start(out_v[:, bass.ds(q * TF, TF), :], X[:, bass.ds(q * TF, TF), :]).then_inc(out_put, 16)

            parts(act, put_out)

        @block.vector
        def _(dve):
            v = nc.vector

            dve.wait_ge(w_in, 64)
            v.tensor_reduce(wabs[:, :], w_nat[:, :, :, :], AX.XY, ALU.add, apply_absolute_value=True).then_inc(wabs_ok, 1)
            dve.wait_ge(am_sum, 1)
            v.tensor_scalar(am[:, :], bank[0][:, 0:4], 1.0 / (D * D), None, ALU.mult)
            v.tensor_scalar(am_eps[:, :], bank[0][:, 0:4], 1.0 / (D * D), EPS, ALU.mult, ALU.add)
            dve.drain()
            v.reciprocal(am_inv[:, :], am_eps[:, :])
            v.tensor_scalar(c_qk[:, 0:1], am[:, 0:1], am[:, 1:2], HD ** -0.5, ALU.mult, ALU.mult)
            dve.drain()
            for i in range(4):
                v.tensor_scalar(w_z[:, i], w_nat[:, i], am_inv[:, i:i + 1], MAGIC, ALU.mult, ALU.add)
            dve.drain()
            v.tensor_scalar(w_z[:, :, :, :], w_z[:, :, :, :], MAGIC, 1.0, ALU.subtract, ALU.min)
            dve.drain()
            v.tensor_scalar(w_q[:, :, :, :], w_z[:, :, :, :], -1.0, None, ALU.max).then_inc(am_ok, 1)
            dve.wait_ge(const_ok, 1)
            v.tensor_tensor(seen[:, :, :], seen[:, :, :], own[:, :].unsqueeze(2).to_broadcast([P, BT, SEQ]), ALU.mult)
            dve.drain()
            v.tensor_reduce(causal[:, :], seen[:, :, :].rearrange("p b j -> p j b"), AX.X, ALU.add)
            dve.drain()
            v.tensor_scalar(causal[:, :], causal[:, :], 1.0, -NEG, ALU.subtract, ALU.mult)

            def stats1(g, n):
                if g is None:
                    return
                wait(dve, y_ready, g, 2, n + 1)
                for t in (2 * n, 2 * n + 1):
                    v.bn_stats(stats[:, 0, t, :], (ps_q, ps_k)[n][:, (t % 2) * D:(t % 2 + 1) * D])

            def moments(it, a, c):
                which = both_of(a, c)
                if which is None:
                    return
                dve.drain()
                for n in range(which.start, which.stop):
                    for t in range(TG):
                        v.bn_aggr(mv[:, n, t, :], stats[:, n, t, :])
                dve.drain()
                v.tensor_scalar(nmean[:, which, :], mv[:, which, :, 0], -1.0, None, ALU.mult)
                v.tensor_scalar(veps[:, which, :], mv[:, which, :, 1], EPS, None, ALU.add).then_inc(var_ok, 1)
                if c is not None:
                    for t in range(TG):
                        v.tensor_scalar(cen[:, 1, t, :], cen[:, 1, t, :], mv[:, 1, t, 0:1], None, ALU.subtract)

            def quantise(it, a, c, par):
                which = both_of(a, c)
                if which is None:
                    return
                if a is not None:
                    wait(dve, centred, a, 1, 1)
                    wait(dve, diag_ok, a, 1, 1, lag=1)
                    wait(dve, v_copied, a, 2, 2, lag=1)
                    stand(dve)
                dve.drain()
                v.tensor_reduce(amax[:, which, :], cen[:, which, :, :], AX.X, ALU.max, apply_absolute_value=True)
                wait(dve, rstd_ok, it, 1, 1)
                stand(dve)
                dve.drain()
                v.tensor_tensor(amax[:, which, :], amax[:, which, :], rstd[:, which, :], ALU.mult)
                dve.drain()
                v.tensor_scalar(step_of[:, which, :], amax[:, which, :], 1e-5, 1.0 / QMAX, ALU.max, ALU.mult)
                dve.drain()
                v.reciprocal(inv[:, which, :], step_of[:, which, :])
                if c is not None:
                    v.tensor_scalar(s_p[:, :], step_of[:, 1, :], am[:, 3:4], None, ALU.mult)
                if a is not None:
                    v.tensor_scalar(s_qk[par][:, :], s1, c_qk[:, 0:1], None, ALU.mult)
                    v.tensor_scalar(s_v[:, :], s1, am[:, 2:3], None, ALU.mult).then_inc(s1_ok, 1)
                dve.drain()
                v.tensor_tensor(mul[:, which, :], inv[:, which, :], rstd[:, which, :], ALU.mult)
                dve.drain()
                for n in range(which.start, which.stop):
                    for t in range(TG):
                        last = v.tensor_scalar(cen[:, n, t, :], cen[:, n, t, :], mul[:, n, t:t + 1], MAGIC, ALU.mult, ALU.add)
                    last.then_inc((z1_ok, z2_ok)[n], 1)

            def scale_k(g, cc):
                if g is None:
                    return
                wait(dve, k_ready, g, 2, cc + 1)
                wait(dve, srow_copied, g, 1, 1)
                wait(dve, kx_in, g, 16 * HC, 16 * HC, lag=1)
                v.tensor_tensor(kT[:, cc, :], ps_k[:, :], s_row[:, :], ALU.mult).then_inc(k_scaled, 1)

            def scale_scores(g, par, t):
                if g is None:
                    return
                wait(dve, sc_ready, g, TG, t + 1)
                if t >= 2:
                    wait(dve, exp_ok, g, TG, t - 1)
                else:
                    wait(dve, exp_ok, g, TG, TG + t - 1, lag=1)
                v.scalar_tensor_tensor(out=sc[t % 2][:, :, :], in0=ps_s[t % 2][:, :].rearrange("p (h j) -> p h j", j=SEQ), scalar=s_qk[par][:, t:t + 1],
                                       in1=causal[:, :].unsqueeze(1).to_broadcast([P, H, SEQ]), op0=ALU.mult, op1=ALU.add).then_inc(sc_scaled, 1)
                dve.drain()
                v.tensor_reduce(mx[t % 2][:, :], sc[t % 2][:, :, :], AX.X, ALU.max).then_inc(mx_ok, 1)

            def norm_o(g, t):
                if g is None:
                    return
                wait(dve, o_ready, g, TG, t + 1)
                if t == 0:
                    wait(dve, q2_ok, g, 1, 1, lag=1)
                    if not (isinstance(g, int) and g < 1):
                        stand(dve)
                o = ps_o[:, 0:H * VW].rearrange("p (h r) -> p h r", r=VW)
                v.reciprocal(rs[:, :], o[:, :, HD])
                dve.drain()
                v.tensor_tensor(o_sb[:, t, :].rearrange("p (h r) -> p h r", r=HD), o[:, :, 0:HD], rs[:, :].unsqueeze(2).to_broadcast([P, H, HD]),
                                ALU.mult).then_inc(o_ok, 1)
                dve.drain()
                v.bn_stats(stats[:, 1, t, :], o_sb[:, t, :])

            def residual(g, n):
                if g is None:
                    return
                wait(dve, proj_ready, g, 2, n + 1)
                for k in range(2):
                    t = 2 * n + k
                    xt = X[:, bass.ds(g * TG + t, 1), :].rearrange("p o d -> p (o d)")
                    last = v.scalar_tensor_tensor(out=xt, in0=ps_h[n][:, k * D:(k + 1) * D], scalar=s_p[:, t:t + 1], in1=xt, op0=ALU.mult, op1=ALU.add)
                last.then_inc(x1_ok, 1)

            def route(g):
                if g is None:
                    return
                wait(dve, rt_ready, g, 1, 1)
                logits = ps_c[:, 0:TG * E].rearrange("p (t e) -> p t e", e=E)
                v.tensor_reduce(rmax[:, :], logits, AX.X, ALU.max)
                dve.drain()
                v.tensor_tensor(rsub[:, :, :], logits, rmax[:, :].unsqueeze(2).to_broadcast([P, TG, E]), ALU.subtract).then_inc(rsub_ok, 1)

            def choose(g):
                if g is None:
                    return
                wait(dve, rexp_ok, g, 1, 1)
                v.tensor_scalar(dest[:, :, :], dest[:, :, :], float(TOPK * GT), None, ALU.add)
                for t in range(TG):
                    v.max(top[:, t, :], rexp[:, t, :])
                dve.drain()
                for t in range(TG):
                    v.max_index(topi[:, t, :], top[:, t, :], rexp[:, t, :])
                v.tensor_tensor(den[:, :], top[:, :, 0], top[:, :, 1], ALU.add)
                dve.drain()
                v.tensor_copy(topf[:, :, :], topi[:, :, 0:TOPK])
                v.reciprocal(deni[:, :], den[:, :])
                dve.drain()
                v.tensor_tensor(hot[:, :, :, :], expert_no[:, :].unsqueeze(1).unsqueeze(1).to_broadcast([P, TG, TOPK, E]),
                                topf[:, :, :].unsqueeze(3).to_broadcast([P, TG, TOPK, E]), ALU.is_equal)
                wait(dve, scattered, g, 16 * TG * TOPK, 16 * TG * TOPK, lag=1)
                v.tensor_tensor(hrow[:, :, :, D + 1], top[:, :, 0:TOPK], deni[:, :].unsqueeze(2).to_broadcast([P, TG, TOPK]), ALU.mult)
                v.tensor_copy(hrow[:, :, :, D], dest[:, :, :])
                dve.drain()
                v.tensor_tensor(both[:, :, :], hot[:, :, 0, :], hot[:, :, 1, :], ALU.add).then_inc(both_ok, 1)

            def place(g):
                if g is None:
                    return
                wait(dve, rank_ready, g, 1, 1)
                v.tensor_tensor(pos[:, :, :], ps_a[:, 0:TG * E].rearrange("p (t e) -> p t e", e=E),
                                filled[:, :].unsqueeze(1).to_broadcast([P, TG, E]), ALU.add)
                dve.drain()
                v.tensor_tensor(filled[:, :], filled[:, :], ps_a[:, TG * E:(TG + 1) * E], ALU.add).then_inc(rank_used, 1)
                v.tensor_tensor(posh[:, :, :, :], hot[:, :, :, :], pos[:, :, :].unsqueeze(2).to_broadcast([P, TG, TOPK, E]), ALU.mult)
                dve.drain()
                v.tensor_reduce(posf[:, :, :], posh[:, :, :, :], AX.X, ALU.add)
                dve.drain()
                v.tensor_copy(posi[:, :, :], posf[:, :, :]).then_inc(pos_ok, 1)

            def iteration(it, a, b, c, d, par):
                place(d)
                stats1(a, 0)
                stats1(a, 1)
                moments(it, a, c)
                scale_scores(b, 1 - par, 0)
                quantise(it, a, c, par)
                scale_scores(b, 1 - par, 1)
                scale_scores(b, 1 - par, 2)
                residual(c, 0)
                residual(c, 1)
                norm_o(b, 0)
                scale_scores(b, 1 - par, 3)
                scale_k(a, 0)
                norm_o(b, 1)
                scale_k(a, 1)
                norm_o(b, 2)
                route(c)
                choose(c)
                norm_o(b, 3)

            def without_a(it, a, b, c, d, par):
                place(d)
                moments(it, a, c)
                scale_scores(b, 1 - par, 0)
                quantise(it, a, c, par)
                scale_scores(b, 1 - par, 1)
                scale_scores(b, 1 - par, 2)
                residual(c, 0)
                residual(c, 1)
                norm_o(b, 0)
                scale_scores(b, 1 - par, 3)
                norm_o(b, 1)
                norm_o(b, 2)
                route(c)
                choose(c)
                norm_o(b, 3)

            def without_b(it, a, b, c, d, par):
                place(d)
                moments(it, a, c)
                quantise(it, a, c, par)
                residual(c, 0)
                residual(c, 1)
                route(c)
                choose(c)

            pipeline(dve, iteration, without_a, without_b)

            dve.drain()
            v.tensor_tensor(sel[:, :], eighth[:, :], filled[:, :], ALU.mult)
            v.tensor_scalar(cnt[:, :], expert_no[:, :], -float(PITCH), None, ALU.mult)
            dve.drain()
            v.tensor_reduce(pad_at[:, 1:2], sel[:, :], AX.X, ALU.add)
            v.tensor_tensor(cnt[:, :], cnt[:, :], filled[:, :], ALU.add)
            dve.drain()
            v.tensor_tensor(sel[:, :], eighth[:, :], expert_no[:, :], ALU.mult)
            v.tensor_scalar(cnt[:, :], cnt[:, :], float(P - 1), 1.0 / P, ALU.add, ALU.mult)
            dve.drain()
            v.tensor_reduce(pad_at[:, 2:3], sel[:, :], AX.X, ALU.add)
            v.tensor_scalar(cnt[:, :], cnt[:, :], 0.5 - 0.25 / P, MAGIC, ALU.subtract, ALU.add)
            dve.drain()
            v.tensor_scalar(pad_at[:, 2:3], pad_at[:, 2:3], -float(P), None, ALU.mult)
            v.tensor_scalar(cnt[:, :], cnt[:, :], MAGIC, None, ALU.subtract)
            dve.drain()
            v.tensor_tensor(pad_at[:, 0:1], pad_at[:, 0:1], pad_at[:, 2:3], ALU.add)
            v.tensor_copy(cum[0][:, E // 2:], cnt[:, :])
            dve.drain()
            v.tensor_tensor(pad_at[:, 1:2], pad_at[:, 1:2], pad_at[:, 0:1], ALU.add)
            dve.wait_ge(pad_ok, 1)
            v.tensor_scalar(pad[:, :, D], pad_no[:, :], pad_at[:, 0:1], None, ALU.add)
            for n, step_ in enumerate((1, 2, 4, 8)):
                v.tensor_tensor(cum[(n + 1) % 2][:, E // 2:], cum[n % 2][:, E // 2:], cum[n % 2][:, E // 2 - step_:E // 2 + E - step_], ALU.add)
                dve.drain()
                if n == 0:
                    v.tensor_copy(pad_i[:, :], pad_at[:, 1:2]).then_inc(padi_ok, 1)
            ends = cum[0][:, E // 2:]
            v.tensor_scalar(live[:, :], tile_no[:, :], ends[:, E - 1:E], None, ALU.is_lt)
            dve.drain()
            v.tensor_tensor(kp[:, :], tile_no[:, :], live[:, :], ALU.mult)
            v.tensor_scalar(live[:, :], live[:, :], -float(Y_ROWS), float(Y_ROWS), ALU.mult, ALU.add)
            v.tensor_scalar(cnt[:, :], cnt[:, :], -float(P), float(PITCH), ALU.mult, ALU.add)
            dve.drain()
            v.tensor_tensor(past[:, :, :], kp[:, :].unsqueeze(2).to_broadcast([P, EXPERT_TILES, E]), ends.unsqueeze(1).to_broadcast([P, EXPERT_TILES, E]), ALU.is_ge)
            dve.drain()
            v.tensor_tensor(skip[:, :, :], past[:, :, :], cnt[:, :].unsqueeze(1).to_broadcast([P, EXPERT_TILES, E]), ALU.mult)
            v.tensor_scalar(kp[:, :], kp[:, :], float(P), None, ALU.mult)
            dve.drain()
            v.tensor_reduce(ek[:, :], skip[:, :, :], AX.X, ALU.add)
            dve.drain()
            v.tensor_tensor(first_row[:, :], ek[:, :], kp[:, :], ALU.add).then_inc(first_row_ok, 1)
            dve.drain()
            v.tensor_reduce(ek[:, :], past[:, :, :], AX.X, ALU.add)
            dve.drain()
            v.tensor_copy(expert_of[:, LAG:LAG + EXPERT_TILES], ek[:, :]).then_inc(expert_ok, 1)

            def step(k, j, i, _):
                if not (isinstance(k, int) and not 1 <= k <= EXPERT_TILES):
                    n = (j - 1) % DEEP
                    since(dve, silu_ok, k, 1)
                    since(dve, hhT_ready, k, 3)
                    v.scalar_tensor_tensor(out=hh[n % 2], in0=sg[n % 2], scalar=xe[n][:, D + 1:D + 2], in1=bank[2 + n % 2][:, F:2 * F], op0=ALU.mult, op1=ALU.mult)
                    put_before(dve, j, i, 1)
                    v.tensor_scalar(di[:, n:n + 1], xe[n][:, D:D + 1], live[:, bass.ds(k - 1, 1)], None, ALU.add).then_inc(hh_ok, 1)
                if not (isinstance(k, int) and not 2 <= k <= EXPERT_TILES + 1):
                    n = j % 2
                    since(dve, hhT_ready, k, 2)
                    since(dve, ye_ready, k, 4)
                    v.tensor_copy(hhT[n], bank[4 + n][0:F, 0:P]).then_inc(hhT_copied, 1)

            tiles(dve, step)

            def add_x(q, j, i):
                wait(dve, pair_ok, q, 1, 1)
                xq_ = X[:, bass.ds(q * TF, TF), :]
                v.tensor_tensor(xq_, xq_, fin[j][:, :, 0, :], ALU.add).then_inc(fin_ok, 1)

            parts(dve, add_x)

        @block.tensor
        def _(pe):
            t_ = nc.tensor

            pe.wait_ge(wabs_ok, 1)
            pe.wait_ge(const_ok, 1)
            t_.matmul(bank[0][:, 0:4], ones[:, :], wabs[:, :], start=True, stop=True).then_inc(am_sum, 1)
            pe.wait_ge(am_ok, 1)
            for i in range(4):
                ps = ps_s[i // 2][:, :].bitcast(bf16).rearrange("p (w c o) -> p w c o", w=2, c=KC)
                for c in range(KC):
                    for o in range(KC):
                        last = t_.transpose(ps[:, i % 2, c, o * P:(o + 1) * P], w_q[:, i, o, c * P:(c + 1) * P], ident_b[:, :])
            last.then_inc(wT_ps, 1)

            def mix1(g, par, n):
                if g is None:
                    return
                if n == 0:
                    wait(pe, bd1_ok, g, 1, 1)
                    if isinstance(g, int):
                        pe.wait_ge(x_in[par], 16 * (g // 2 + 1))
                    else:
                        pe.wait_ge(x_in[par], (g - par) * 8 + 16)
                wait(pe, v_copied, g, 2, n + 1, lag=1)
                for k in range(2):
                    t = 2 * n + k
                    last = t_.matmul((ps_q, ps_k)[n][:, k * D:(k + 1) * D], bd1[par][:, t, :, :].rearrange("p b d -> p (b d)"),
                                     X[:, bass.ds(g * TG + t, 1), :].rearrange("p o d -> p (o d)"), start=True, stop=True)
                last.then_inc(y_ready, 1)

            def transpose_q(g, n, q_ok, dst, done):
                if g is None:
                    return
                wait(pe, q_ok, g, 1, 1)
                if n == 0:
                    wait(pe, srow_copied, g, 1, 1, lag=1)
                    wait(pe, rank_used, g, 1, 1, lag=3)
                else:
                    wait(pe, rsub_ok, g, 1, 1, lag=1)
                stand(pe)
                ps = dst[:, :].bitcast(bf16).rearrange("p (c t) -> p c t", c=KC)
                for t in range(TG):
                    for c in range(KC):
                        last = t_.transpose(ps[:, c, t * P:(t + 1) * P], qn[:, n, t, c * P:(c + 1) * P], ident_b[:, :])
                last.then_inc(done, 1)

            def spread_s(g):
                if g is None:
                    return
                wait(pe, diag_ok, g, 1, 1)
                wait(pe, xqT_copied, g, 1, 1)
                t_.matmul(ps_a[:, :], ones[:, :], diag[:, :, :].rearrange("p t q -> p (t q)"), start=True, stop=True).then_inc(srow_ready, 1)

            def project_T(g, w, cc, ps, done):
                for c in range(KC):
                    last = t_.matmul(ps[:, :], wT[:, w, c, cc * P:(cc + 1) * P], xq[:, c, :], start=(c == 0), stop=(c == KC - 1))
                last.then_inc(done, 1)

            def project_qk(g, cc):
                if g is None:
                    return
                if isinstance(g, int) and g == 0:
                    pe.wait_ge(wT_ok, 2)
                wait(pe, xqT_copied, g, 1, 1)
                if cc == 0:
                    wait(pe, centred, g, 1, 1)
                else:
                    wait(pe, q_copied, g, 2, 1)
                project_T(g, 0, cc, ps_q, q_ready)
                if cc == 1:
                    wait(pe, k_scaled, g, 2, 1)
                project_T(g, 1, cc, ps_k, k_ready)

            def project_v(g, n):
                if g is None:
                    return
                if n == 0:
                    wait(pe, q_copied, g, 2, 2)
                else:
                    wait(pe, k_scaled, g, 2, 2)
                for k in range(2):
                    t = 2 * n + k
                    for c in range(KC):
                        last = t_.matmul((ps_q, ps_k)[n][:, k * D:(k + 1) * D], xq[:, c, t * P:(t + 1) * P], wT[:, 2, c, :], start=(c == 0), stop=(c == KC - 1))
                last.then_inc(v_ready, 1)

            def scores(g, par, t):
                if g is None:
                    return
                if t == 0:
                    wait(pe, kx_in, g, 16 * HC, 16 * HC)
                    wait(pe, q_copied, g, 2, 2)
                if t >= 2:
                    wait(pe, sc_scaled, g, TG, t - 1)
                else:
                    wait(pe, sc_scaled, g, TG, TG + t - 1, lag=1)
                for c in range(KC):
                    for b in range(BT):
                        cols = slice(t * P + b * SEQ, t * P + (b + 1) * SEQ)
                        last = t_.matmul(ps_s[t % 2][b * SEQ:(b + 1) * SEQ, c * HC * SEQ:(c + 1) * HC * SEQ], qT[par][:, c, cols], kx[par][:, c, :, cols],
                                         start=True, stop=True)
                last.then_inc(sc_ready, 1)

            def transpose_p(g, t):
                if g is None:
                    return
                wait(pe, exp_ok, g, TG, t + 1)
                if t > 0:
                    wait(pe, pT_copied, g, TG, t)
                else:
                    wait(pe, pT_copied, g, TG, TG, lag=1)
                for c in range(SLOTS):
                    last = t_.transpose(ps_pt[:, c * P:(c + 1) * P], pr[t % 2][:, c, :, :].rearrange("p s j -> p (s j)"), ident[:, :])
                last.then_inc(pT_ready, 1)

            def attend(g, par, t):
                if g is None:
                    return
                wait(pe, pT_copied, g, TG, t + 1)
                if t == 0:
                    wait(pe, vx_in, g, 16 * SLOTS, 16 * SLOTS)
                    wait(pe, o_ok, g, TG, TG, lag=1)
                else:
                    wait(pe, o_ok, g, TG, t)
                o = ps_o[:, 0:H * VW].rearrange("p (s c r) -> p s c r", s=SLOTS, c=SLOTS)
                for c in range(SLOTS):
                    for b in range(BT):
                        last = t_.matmul(o[b * SEQ:(b + 1) * SEQ, :, c, :], pT[t % 2][:, c, b * SEQ:(b + 1) * SEQ],
                                         vx[:, t * BT + b, :, c * VW:(c + 1) * VW], start=True, stop=True)
                last.then_inc(o_ready, 1)

            def project_o(g, n):
                if g is None:
                    return
                if n == 0:
                    wait(pe, oqT_copied, g, 1, 1)
                elif isinstance(g, int):
                    pe.wait_ge(srow_copied, min(g + 3, GROUPS))
                else:
                    wait(pe, srow_copied, g, 1, 3)
                for k in range(2):
                    t = 2 * n + k
                    for c in range(KC):
                        last = t_.matmul(ps_h[n][:, k * D:(k + 1) * D], oq[:, c, t * P:(t + 1) * P], wT[:, 3, c, :], start=(c == 0), stop=(c == KC - 1))
                last.then_inc(proj_ready, 1)

            def mix2(g, par, n):
                if g is None:
                    return
                if n == 0:
                    wait(pe, bd2_ok, g, 1, 1)
                wait(pe, x1_ok, g, 2, n + 1)
                for k in range(2):
                    t = 2 * n + k
                    last = t_.matmul(ps_h[n][:, k * D:(k + 1) * D], bd2[par][:, t, :, :].rearrange("p b d -> p (b d)"),
                                     X[:, bass.ds(g * TG + t, 1), :].rearrange("p o d -> p (o d)"), start=True, stop=True)
                last.then_inc(h_ready, 1)

            def transpose_h(g, n):
                if g is None:
                    return
                wait(pe, h_copied, g, 2, n + 1)
                for k in range(2):
                    for c in range(KC):
                        last = t_.transpose(ps_h[n][:, (c * 2 + k) * P:(c * 2 + k + 1) * P], hrow[:, 2 * n + k, 0, c * P:(c + 1) * P], ident[:, :])
                last.then_inc(hT_ready, 1)

            def router(g):
                if g is None:
                    return
                if isinstance(g, int) and g == 0:
                    pe.wait_ge(rw_in, 16)
                wait(pe, hT_copied, g, 2, 2)
                for c in range(KC):
                    last = t_.matmul(ps_c[0:E, :], rw[:, c, :], hT[:, c, :], start=(c == 0), stop=(c == KC - 1))
                last.then_inc(scT_ready, 1)

            def logits(g):
                if g is None:
                    return
                wait(pe, scT_copied, g, 1, 1)
                stand(pe)
                for t in range(TG):
                    last = t_.transpose(ps_c[:, t * E:(t + 1) * E], scT[:, t * P:(t + 1) * P], ident[0:E, 0:E])
                last.then_inc(rt_ready, 1)

            def rank(g):
                if g is None:
                    return
                wait(pe, both_ok, g, 1, 1)
                if not isinstance(g, int):
                    wait(pe, srow_copied, g, 1, 3)
                else:
                    pe.wait_ge(srow_copied, min(g + 3, GROUPS))
                m = both[:, :, :].rearrange("p t e -> p (t e)")
                for k in range(1, TG):
                    t_.matmul(ps_a[:, k * E:TG * E], ones_b[:, :], m[:, 0:(TG - k) * E], start=(k == 1), stop=False, skip_group_check=True)
                t_.matmul(ps_a[:, 0:TG * E], before[:, :], m, start=False, stop=True, skip_group_check=True)
                for k in range(TG):
                    last = t_.matmul(ps_a[:, TG * E:(TG + 1) * E], ones_b[:, :], m[:, k * E:(k + 1) * E], start=(k == 0), stop=(k == TG - 1), skip_group_check=True)
                last.then_inc(rank_ready, 1)

            def iteration(it, a, b, c, d, par):
                mix1(a, par, 0)
                mix1(a, par, 1)
                rank(d)
                scores(b, 1 - par, 0)
                scores(b, 1 - par, 1)
                transpose_p(b, 0)
                scores(b, 1 - par, 2)
                attend(b, 1 - par, 0)
                transpose_q(a, 0, q1_ok, ps_a, xqT_ready)
                transpose_q(c, 1, q2_ok, ps_c, oqT_ready)
                scores(b, 1 - par, 3)
                spread_s(a)
                project_o(c, 0)
                transpose_p(b, 1)
                project_o(c, 1)
                project_qk(a, 0)
                mix2(c, par, 0)
                mix2(c, par, 1)
                attend(b, 1 - par, 1)
                transpose_p(b, 2)
                transpose_h(c, 0)
                transpose_h(c, 1)
                project_qk(a, 1)
                attend(b, 1 - par, 2)
                router(c)
                transpose_p(b, 3)
                logits(c)
                project_v(a, 0)
                project_v(a, 1)
                attend(b, 1 - par, 3)

            def without_a(it, a, b, c, d, par):
                rank(d)
                scores(b, 1 - par, 0)
                scores(b, 1 - par, 1)
                scores(b, 1 - par, 2)
                transpose_p(b, 0)
                transpose_q(c, 1, q2_ok, ps_c, oqT_ready)
                project_o(c, 0)
                scores(b, 1 - par, 3)
                project_o(c, 1)
                attend(b, 1 - par, 0)
                transpose_p(b, 1)
                mix2(c, par, 0)
                mix2(c, par, 1)
                attend(b, 1 - par, 1)
                transpose_p(b, 2)
                transpose_h(c, 0)
                transpose_h(c, 1)
                attend(b, 1 - par, 2)
                router(c)
                transpose_p(b, 3)
                logits(c)
                attend(b, 1 - par, 3)

            def without_b(it, a, b, c, d, par):
                rank(d)
                transpose_q(c, 1, q2_ok, ps_c, oqT_ready)
                project_o(c, 0)
                project_o(c, 1)
                mix2(c, par, 0)
                mix2(c, par, 1)
                transpose_h(c, 0)
                transpose_h(c, 1)
                router(c)
                logits(c)

            pipeline(pe, iteration, without_a, without_b)

            pe.wait_ge(gu_in, 16 * 8)
            pe.wait_ge(dw_in, 16 * 2)
            pe.wait_ge(expert_ok, 1)

            def experts_of(i):
                experts = registers(pe, "expert", DEEP + 2, i)
                if isinstance(i, int) and i >= EXPERT_TILES // DEEP:
                    experts = experts[:LAG + 2]
                pe.load(experts, expert_of[0:1, bass.ds(DEEP * i, len(experts))])
                return [pe.snap(r, donate=True, min_val=0, max_val=E - 1) for r in experts]

            def step(k, j, i, expert):
                if not (isinstance(k, int) and k >= EXPERT_TILES):
                    pe.wait_ge(xe_in[j], 16 * i + 16)
                    since(pe, xeT_copied, k, 2)
                    for c in range(KC):
                        last = t_.transpose(bank[j % 2][:, c * P:(c + 1) * P], xe[j][:, c * P:(c + 1) * P], ident[:, :])
                    last.then_inc(xeT_ready, 1)
                if not (isinstance(k, int) and not 1 <= k <= EXPERT_TILES):
                    n = (j + 1) % 2
                    since(pe, xeT_copied, k, 1)
                    since(pe, hh_ok, k, 3)
                    for c in range(KC):
                        last = t_.matmul(bank[2 + n][:, 0:2 * F], xeT[n][:, c, :], gu[:, c, bass.ds(expert[j + LAG - 1], 1), :].rearrange("p o f -> p (o f)"), start=(c == 0), stop=(c == KC - 1))
                    last.then_inc(gu_ready, 1)
                if not (isinstance(k, int) and not 2 <= k <= EXPERT_TILES + 1):
                    n = j % 2
                    since(pe, hh_ok, k, 2)
                    since(pe, hhT_copied, k, 4)
                    t_.transpose(bank[4 + n][0:F, 0:P], hh[n], ident[:, :]).then_inc(hhT_ready, 1)
                if not (isinstance(k, int) and k < 3):
                    n = (j + 1) % 2
                    since(pe, hhT_copied, k, 3)
                    since(pe, ye_copied, k, 5)
                    t_.matmul(bank[6 + n][:, 0:D], hhT[n], dw[:, bass.ds(expert[j], 1), :].rearrange("p o d -> p (o d)"), start=True, stop=True).then_inc(ye_ready, 1)

            tiles(pe, step, experts_of)


_INS = ["x", "itok_B_0_7", "itok_B_1_198", "L0_cond_weights", "L0_attn_wq", "L0_attn_wk", "L0_attn_wv", "L0_attn_wp",
        "L0_cond2_weights", "L0_ffn_router_w", "L0_ffn_gate_w", "L0_ffn_up_w", "L0_ffn_down_w"]


def kernel(**inputs):
    import numpy as _np
    import concourse.bacc as _bacc
    from concourse.bass_utils import run_bass_kernel_spmd as _run

    nc = _bacc.Bacc("TRN2", target_bir_lowering=False, num_devices=1)
    arrays, args = {}, []
    for name in _INS:
        a = _np.ascontiguousarray(inputs[name])
        arrays[f"in_{name}"] = a
        args.append(nc.dram_tensor(f"in_{name}", a.shape, mybir.dt.from_np(a.dtype), kind="ExternalInput").ap())
    args.append(nc.dram_tensor("out_x", (BATCH, SEQ, D), fp32, kind="ExternalOutput").ap())
    build(nc, *args)
    r = _run(nc, [arrays], core_ids=[0])
    return r.results[0]["out_x"]
```
